# Optimizing a Trainium2 kernel written in Bass

```python
import numpy as np
import jax
import jax.numpy as jnp

def _softmax(x, axis=-1):
    return jax.nn.softmax(x, axis=axis)

def _gelu(x):
    return jax.nn.gelu(x, approximate=True)

def _silu(x):
    return jax.nn.silu(x)

def _sigmoid(x):
    return jax.nn.sigmoid(x)

def _layernorm(x, axis=-1, eps=1e-05):
    m = jnp.mean(x, axis=axis, keepdims=True)
    v = jnp.var(x, axis=axis, keepdims=True)
    return (x - m) / jnp.sqrt(v + eps)

def _scatter_add(tgt, idx, src, axis=0):
    return tgt.at[idx].add(src)

def _segment_sum(src, seg, n):
    return jax.ops.segment_sum(src, seg, n)
kernel_name = 'mk_seq_preln_d2_jaxref_r4_74a5ea'

def setup_inputs(seed: int=0):
    np.random.seed(seed)
    _w = jnp.asarray

    def _L0_attn_setup():
        import jax, jax.numpy as jnp
        import numpy as np
        B, T, C, H = (8, 512, 256, 16)
        S = C // H
        LN_EPS = 1e-05
        key = jax.random.key(seed)
        ks = jax.random.split(key, 12)
        w = lambda k: jax.random.normal(k, (C, C), dtype=jnp.float32) * 0.02
        return {'x': jax.random.normal(ks[0], (B, T, C), dtype=jnp.float32), 'time_mix_k': jax.random.uniform(ks[1], (1, 1, C), dtype=jnp.float32), 'time_mix_v': jax.random.uniform(ks[2], (1, 1, C), dtype=jnp.float32), 'time_mix_r': jax.random.uniform(ks[3], (1, 1, C), dtype=jnp.float32), 'time_decay': -jax.random.uniform(ks[4], (H, S), minval=0.1, maxval=5.0, dtype=jnp.float32), 'time_first': jax.random.uniform(ks[5], (H, S), dtype=jnp.float32), 'Wk': w(ks[6]), 'Wv': w(ks[7]), 'Wr': w(ks[8]), 'Wo': w(ks[9]), 'ln_g': jnp.ones((C,), jnp.float32), 'ln_b': jnp.zeros((C,), jnp.float32)}
    _L0_attn_in = _L0_attn_setup()

    def _L0_ffn_setup():
        import jax, jax.numpy as jnp
        import numpy as np
        B, S, D = (2, 256, 256)
        H = 128
        E = 16
        K = 2
        HS = 2 * H
        ROUTE_SCALE = 1.0

        def _gated_mlp_act(y):
            u, g = jnp.split(y, 2, axis=-1)
            return u * jax.nn.silu(g)
        key = jax.random.key(seed)
        ks = jax.random.split(key, 6)
        s = 0.02
        return {'x': jax.random.normal(ks[0], (B, S, D), dtype=jnp.float32), 'Wg': jax.random.normal(ks[1], (E, D), dtype=jnp.float32) * s, 'W1': jax.random.normal(ks[2], (E, D, 2 * H), dtype=jnp.float32) * s, 'W2': jax.random.normal(ks[3], (E, H, D), dtype=jnp.float32) * s, 'Ws1': jax.random.normal(ks[4], (D, 2 * HS), dtype=jnp.float32) * s, 'Ws2': jax.random.normal(ks[5], (HS, D), dtype=jnp.float32) * s}
    _L0_ffn_in = _L0_ffn_setup()

    def _L1_attn_setup():
        import jax, jax.numpy as jnp
        import numpy as np
        B, T, C, H = (2, 512, 256, 16)
        DK = DV = C // H
        CONV_K = 4
        EPS = 1e-05

        def _causal_depthwise_conv(x, w):
            K = w.shape[1]
            xp = jnp.pad(x, ((0, 0), (K - 1, 0), (0, 0)))
            y = jax.lax.conv_general_dilated(xp.transpose(0, 2, 1), w[:, None, :], window_strides=(1,), padding='VALID', feature_group_count=w.shape[0])
            return y.transpose(0, 2, 1)

        def _l2norm(x):
            return x * jax.lax.rsqrt(jnp.sum(x * x, axis=-1, keepdims=True) + 1e-06)

        def _rope(x, rot_dim, base=10000.0):
            t = x.shape[2]
            half = rot_dim // 2
            inv_freq = base ** (-jnp.arange(half, dtype=jnp.float32) / half)
            ang = jnp.arange(t, dtype=jnp.float32)[:, None] * inv_freq[None, :]
            cos, sin = (jnp.cos(ang), jnp.sin(ang))
            x1 = x[..., :half]
            x2 = x[..., half:rot_dim]
            xpass = x[..., rot_dim:]
            return jnp.concatenate([x1 * cos - x2 * sin, x2 * cos + x1 * sin, xpass], axis=-1)
        key = jax.random.key(seed)
        ks = jax.random.split(key, 16)
        s = 0.02
        inp = {'x': jax.random.normal(ks[0], (B, T, C), jnp.float32), 'Wq': jax.random.normal(ks[1], (C, H * DK), jnp.float32) * s, 'Wk': jax.random.normal(ks[2], (C, H * DK), jnp.float32) * s, 'Wv': jax.random.normal(ks[3], (C, H * DV), jnp.float32) * s, 'Wo': jax.random.normal(ks[4], (H * DV, C), jnp.float32) * s, 'Wg': jax.random.normal(ks[5], (C, H * DV), jnp.float32) * s, 'Wgk': jax.random.normal(ks[6], (C, H), jnp.float32) * s, 'Wb': jax.random.normal(ks[7], (C, H), jnp.float32) * s, 'bb': jnp.zeros((H,), jnp.float32), 'A_log': jnp.log(jax.random.uniform(ks[8], (H,), jnp.float32, 0.5, 8.0)), 'conv_q_w': jax.random.normal(ks[10], (H * DK, CONV_K), jnp.float32) * 0.2, 'conv_k_w': jax.random.normal(ks[11], (H * DK, CONV_K), jnp.float32) * 0.2, 'conv_v_w': jax.random.normal(ks[12], (H * DV, CONV_K), jnp.float32) * 0.2, 'gnorm_w': jnp.ones((DV,), jnp.float32)}
        dt = jnp.exp(jax.random.uniform(ks[9], (H,), jnp.float32) * (np.log(0.1) - np.log(0.001)) + np.log(0.001))
        dt = jnp.clip(dt, 0.0001, None)
        inp['dt_bias'] = dt + jnp.log(-jnp.expm1(-dt))
        return inp
    _L1_attn_in = _L1_attn_setup()

    def _L1_ffn_setup():
        import jax, jax.numpy as jnp
        import numpy as np
        D_MODEL = 256
        N_HEADS = 16
        D_HEAD = D_MODEL // N_HEADS
        N_EXPERTS = 8
        TOP_K = 2
        D_FF = 512
        EPS = 1e-06

        def rmsnorm(x, w):
            return x * jax.lax.rsqrt(jnp.mean(x * x, axis=-1, keepdims=True) + EPS) * w

        def swiglu(x, w_gate, w_up, w_down):
            return jax.nn.silu(x @ w_gate) * (x @ w_up) @ w_down
        key = jax.random.key(seed)
        ks = jax.random.split(key, 16)
        s = 0.02
        B, S = (2, 512)
        return {'X': jax.random.normal(ks[0], (B, S, D_MODEL), dtype=jnp.float32), 'norm1_w': jnp.ones((D_MODEL,), jnp.float32), 'norm2_w': jnp.ones((D_MODEL,), jnp.float32), 'wq': jax.random.normal(ks[1], (D_MODEL, D_MODEL), jnp.float32) * s, 'wk': jax.random.normal(ks[2], (D_MODEL, D_MODEL), jnp.float32) * s, 'wv': jax.random.normal(ks[3], (D_MODEL, D_MODEL), jnp.float32) * s, 'wo': jax.random.normal(ks[4], (D_MODEL, D_MODEL), jnp.float32) * s, 'router_w': jax.random.normal(ks[5], (D_MODEL, N_EXPERTS), jnp.float32) * s, 'sh_gate': jax.random.normal(ks[6], (D_MODEL, D_FF), jnp.float32) * s, 'sh_up': jax.random.normal(ks[7], (D_MODEL, D_FF), jnp.float32) * s, 'sh_down': jax.random.normal(ks[8], (D_FF, D_MODEL), jnp.float32) * s, 'e_gate': jax.random.normal(ks[9], (N_EXPERTS, D_MODEL, D_FF), jnp.float32) * s, 'e_up': jax.random.normal(ks[10], (N_EXPERTS, D_MODEL, D_FF), jnp.float32) * s, 'e_down': jax.random.normal(ks[11], (N_EXPERTS, D_FF, D_MODEL), jnp.float32) * s}
    _L1_ffn_in = _L1_ffn_setup()
    _d = {'L0_attn_x': _L0_attn_in['x'], 'L0_attn_time_mix_k': _L0_attn_in['time_mix_k'], 'L0_attn_time_mix_v': _L0_attn_in['time_mix_v'], 'L0_attn_time_mix_r': _L0_attn_in['time_mix_r'], 'L0_attn_time_decay': _L0_attn_in['time_decay'], 'L0_attn_time_first': _L0_attn_in['time_first'], 'L0_attn_Wk': _L0_attn_in['Wk'], 'L0_attn_Wv': _L0_attn_in['Wv'], 'L0_attn_Wr': _L0_attn_in['Wr'], 'L0_attn_Wo': _L0_attn_in['Wo'], 'L0_attn_ln_g': _L0_attn_in['ln_g'], 'L0_attn_ln_b': _L0_attn_in['ln_b'], 'L0_ffn_Wg': _L0_ffn_in['Wg'], 'L0_ffn_W1': _L0_ffn_in['W1'], 'L0_ffn_W2': _L0_ffn_in['W2'], 'L0_ffn_Ws1': _L0_ffn_in['Ws1'], 'L0_ffn_Ws2': _L0_ffn_in['Ws2'], 'L1_attn_Wq': _L1_attn_in['Wq'], 'L1_attn_Wk': _L1_attn_in['Wk'], 'L1_attn_Wv': _L1_attn_in['Wv'], 'L1_attn_Wo': _L1_attn_in['Wo'], 'L1_attn_Wg': _L1_attn_in['Wg'], 'L1_attn_Wgk': _L1_attn_in['Wgk'], 'L1_attn_Wb': _L1_attn_in['Wb'], 'L1_attn_bb': _L1_attn_in['bb'], 'L1_attn_A_log': _L1_attn_in['A_log'], 'L1_attn_conv_q_w': _L1_attn_in['conv_q_w'], 'L1_attn_conv_k_w': _L1_attn_in['conv_k_w'], 'L1_attn_conv_v_w': _L1_attn_in['conv_v_w'], 'L1_attn_gnorm_w': _L1_attn_in['gnorm_w'], 'L1_attn_dt_bias': _L1_attn_in['dt_bias'], 'L1_ffn_norm1_w': _L1_ffn_in['norm1_w'], 'L1_ffn_norm2_w': _L1_ffn_in['norm2_w'], 'L1_ffn_wq': _L1_ffn_in['wq'], 'L1_ffn_wk': _L1_ffn_in['wk'], 'L1_ffn_wv': _L1_ffn_in['wv'], 'L1_ffn_wo': _L1_ffn_in['wo'], 'L1_ffn_router_w': _L1_ffn_in['router_w'], 'L1_ffn_sh_gate': _L1_ffn_in['sh_gate'], 'L1_ffn_sh_up': _L1_ffn_in['sh_up'], 'L1_ffn_sh_down': _L1_ffn_in['sh_down'], 'L1_ffn_e_gate': _L1_ffn_in['e_gate'], 'L1_ffn_e_up': _L1_ffn_in['e_up'], 'L1_ffn_e_down': _L1_ffn_in['e_down']}
    _x0 = _d['L0_attn_x']
    _d['L0_attn_x'] = jax.random.normal(jax.random.fold_in(jax.random.key(seed), 1), (8, 512, 256), dtype=_x0.dtype)
    del _x0
    return _d

def reference(L0_attn_x, L0_attn_time_mix_k, L0_attn_time_mix_v, L0_attn_time_mix_r, L0_attn_time_decay, L0_attn_time_first, L0_attn_Wk, L0_attn_Wv, L0_attn_Wr, L0_attn_Wo, L0_attn_ln_g, L0_attn_ln_b, L0_ffn_Wg, L0_ffn_W1, L0_ffn_W2, L0_ffn_Ws1, L0_ffn_Ws2, L1_attn_Wq, L1_attn_Wk, L1_attn_Wv, L1_attn_Wo, L1_attn_Wg, L1_attn_Wgk, L1_attn_Wb, L1_attn_bb, L1_attn_A_log, L1_attn_conv_q_w, L1_attn_conv_k_w, L1_attn_conv_v_w, L1_attn_gnorm_w, L1_attn_dt_bias, L1_ffn_norm1_w, L1_ffn_norm2_w, L1_ffn_wq, L1_ffn_wk, L1_ffn_wv, L1_ffn_wo, L1_ffn_router_w, L1_ffn_sh_gate, L1_ffn_sh_up, L1_ffn_sh_down, L1_ffn_e_gate, L1_ffn_e_up, L1_ffn_e_down):

    def _L0_attn_ref(x, time_mix_k, time_mix_v, time_mix_r, time_decay, time_first, Wk, Wv, Wr, Wo, ln_g, ln_b):
        import jax, jax.numpy as jnp
        import numpy as np
        B, T, C, H = (8, 512, 256, 16)
        S = C // H
        LN_EPS = 1e-05
        Bx, Tx, Cx = x.shape
        xx = jnp.pad(x, ((0, 0), (1, 0), (0, 0)))[:, :-1]
        xk = x * time_mix_k + xx * (1 - time_mix_k)
        xv = x * time_mix_v + xx * (1 - time_mix_v)
        xr = x * time_mix_r + xx * (1 - time_mix_r)
        proj = lambda z, W: jnp.einsum('btc,dc->btd', z, W).reshape(Bx, Tx, H, S)
        k = proj(xk, Wk)
        v = proj(xv, Wv)
        r = proj(xr, Wr)
        kv = k * v
        decay = jnp.exp(time_decay)

        def step(state, inp):
            kv_t, r_t = inp
            state = kv_t + decay * state
            o = r_t * (time_first * kv_t + state)
            return (state, o)
        kvT = jnp.swapaxes(kv, 0, 1)
        rT = jnp.swapaxes(r, 0, 1)
        _, outT = jax.lax.scan(step, jnp.zeros((Bx, H, S), x.dtype), (kvT, rT))
        out = jnp.swapaxes(outT, 0, 1).reshape(Bx, Tx, Cx)
        mu = out.mean(-1, keepdims=True)
        var = out.var(-1, keepdims=True)
        out = (out - mu) / jnp.sqrt(var + LN_EPS) * ln_g + ln_b
        return jnp.einsum('btc,dc->btd', out, Wo)

    def _L0_ffn_ref(x, Wg, W1, W2, Ws1, Ws2):
        import jax, jax.numpy as jnp
        import numpy as np
        B, S, D = (2, 256, 256)
        H = 128
        E = 16
        K = 2
        HS = 2 * H
        ROUTE_SCALE = 1.0

        def _gated_mlp_act(y):
            u, g = jnp.split(y, 2, axis=-1)
            return u * jax.nn.silu(g)
        x_shape = x.shape
        xf = x.reshape(-1, D)
        scores = jax.nn.softmax(xf @ Wg.T, axis=-1)
        wk, idx = jax.lax.top_k(scores, K)
        wk = wk * ROUTE_SCALE
        cw = jnp.sum(jax.nn.one_hot(idx, E, dtype=xf.dtype) * wk[..., None], axis=1)
        h = _gated_mlp_act(jnp.einsum('td,edh->teh', xf, W1))
        z = jnp.einsum('te,teh,ehd->td', cw, h, W2)
        ys = _gated_mlp_act(xf @ Ws1) @ Ws2
        return (z + ys).reshape(x_shape)

    def _L1_attn_ref(x, Wq, Wk, Wv, Wo, Wg, Wgk, Wb, bb, A_log, conv_q_w, conv_k_w, conv_v_w, gnorm_w, dt_bias):
        import jax, jax.numpy as jnp
        import numpy as np
        B, T, C, H = (2, 512, 256, 16)
        DK = DV = C // H
        CONV_K = 4
        EPS = 1e-05

        def _causal_depthwise_conv(x, w):
            K = w.shape[1]
            xp = jnp.pad(x, ((0, 0), (K - 1, 0), (0, 0)))
            y = jax.lax.conv_general_dilated(xp.transpose(0, 2, 1), w[:, None, :], window_strides=(1,), padding='VALID', feature_group_count=w.shape[0])
            return y.transpose(0, 2, 1)

        def _l2norm(x):
            return x * jax.lax.rsqrt(jnp.sum(x * x, axis=-1, keepdims=True) + 1e-06)

        def _rope(x, rot_dim, base=10000.0):
            t = x.shape[2]
            half = rot_dim // 2
            inv_freq = base ** (-jnp.arange(half, dtype=jnp.float32) / half)
            ang = jnp.arange(t, dtype=jnp.float32)[:, None] * inv_freq[None, :]
            cos, sin = (jnp.cos(ang), jnp.sin(ang))
            x1 = x[..., :half]
            x2 = x[..., half:rot_dim]
            xpass = x[..., rot_dim:]
            return jnp.concatenate([x1 * cos - x2 * sin, x2 * cos + x1 * sin, xpass], axis=-1)
        b, t, c = x.shape
        q = jax.nn.silu(_causal_depthwise_conv(x @ Wq, conv_q_w))
        k = jax.nn.silu(_causal_depthwise_conv(x @ Wk, conv_k_w))
        v = jax.nn.silu(_causal_depthwise_conv(x @ Wv, conv_v_w))
        gk = -jnp.exp(A_log) * jax.nn.softplus(x @ Wgk + dt_bias)
        beta = jax.nn.sigmoid(x @ Wb + bb)
        q = q.reshape(b, t, H, DK).transpose(0, 2, 1, 3)
        k = k.reshape(b, t, H, DK).transpose(0, 2, 1, 3)
        v = v.reshape(b, t, H, DV).transpose(0, 2, 1, 3)
        q = _rope(_l2norm(q), DK // 2)
        k = _rope(_l2norm(k), DK // 2)

        def step(S, ins):
            q_t, k_t, v_t, g_t, b_t = ins
            S = S * jnp.exp(g_t)[..., None, None]
            pred = jnp.einsum('bhk,bhkv->bhv', k_t, S)
            delta = b_t[..., None] * (v_t - pred)
            S = S + k_t[..., None] * delta[..., None, :]
            o_t = jnp.einsum('bhk,bhkv->bhv', q_t, S)
            return (S, o_t)
        S0 = jnp.zeros((b, H, DK, DV), jnp.float32)
        ins = (q.transpose(2, 0, 1, 3), k.transpose(2, 0, 1, 3), v.transpose(2, 0, 1, 3), gk.transpose(1, 0, 2), beta.transpose(1, 0, 2))
        _, o = jax.lax.scan(step, S0, ins)
        o = o.transpose(1, 0, 2, 3)
        g = (x @ Wg).reshape(b, t, H, DV)
        o = o * jax.lax.rsqrt(jnp.mean(o * o, axis=-1, keepdims=True) + EPS)
        o = o * gnorm_w * jax.nn.silu(g)
        return o.reshape(b, t, H * DV) @ Wo

    def _L1_ffn_ref(X, norm1_w, norm2_w, wq, wk, wv, wo, router_w, sh_gate, sh_up, sh_down, e_gate, e_up, e_down):
        import jax, jax.numpy as jnp
        import numpy as np
        D_MODEL = 256
        N_HEADS = 16
        D_HEAD = D_MODEL // N_HEADS
        N_EXPERTS = 8
        TOP_K = 2
        D_FF = 512
        EPS = 1e-06

        def rmsnorm(x, w):
            return x * jax.lax.rsqrt(jnp.mean(x * x, axis=-1, keepdims=True) + EPS) * w

        def swiglu(x, w_gate, w_up, w_down):
            return jax.nn.silu(x @ w_gate) * (x @ w_up) @ w_down
        B, S, d = X.shape
        scale = 1.0 / jnp.sqrt(jnp.asarray(D_HEAD, X.dtype))
        h = rmsnorm(X, norm1_w)
        q = (h @ wq).reshape(B, S, N_HEADS, D_HEAD)
        k = (h @ wk).reshape(B, S, N_HEADS, D_HEAD)
        v = (h @ wv).reshape(B, S, N_HEADS, D_HEAD)
        scores = jnp.einsum('bshd,bthd->bhst', q, k) * scale
        attn = jax.nn.softmax(scores, axis=-1)
        ctx = jnp.einsum('bhst,bthd->bshd', attn, v).reshape(B, S, d)
        X = X + ctx @ wo
        h2 = rmsnorm(X, norm2_w).reshape(B * S, d)
        logits = h2 @ router_w
        probs = jax.nn.softmax(logits, axis=-1)
        topw, topi = jax.lax.top_k(probs, TOP_K)
        topw = jax.nn.softmax(topw, axis=-1)
        combine = jnp.sum(jax.nn.one_hot(topi, N_EXPERTS, dtype=h2.dtype) * topw[..., None], axis=1)
        shared = swiglu(h2, sh_gate, sh_up, sh_down)
        gate = jnp.einsum('td,edf->etf', h2, e_gate)
        up = jnp.einsum('td,edf->etf', h2, e_up)
        eout = jnp.einsum('etf,efd->etd', jax.nn.silu(gate) * up, e_down)
        spec = jnp.einsum('etd,te->td', eout, combine)
        moe_out = (shared + spec).reshape(B, S, d)
        return X + moe_out
    x = L0_attn_x
    x = x + _L0_attn_ref(_layernorm(x, axis=-1), L0_attn_time_mix_k, L0_attn_time_mix_v, L0_attn_time_mix_r, L0_attn_time_decay, L0_attn_time_first, L0_attn_Wk, L0_attn_Wv, L0_attn_Wr, L0_attn_Wo, L0_attn_ln_g, L0_attn_ln_b)
    x = x + _L0_ffn_ref(_layernorm(x, axis=-1), L0_ffn_Wg, L0_ffn_W1, L0_ffn_W2, L0_ffn_Ws1, L0_ffn_Ws2)
    x = x + _L1_attn_ref(_layernorm(x, axis=-1), L1_attn_Wq, L1_attn_Wk, L1_attn_Wv, L1_attn_Wo, L1_attn_Wg, L1_attn_Wgk, L1_attn_Wb, L1_attn_bb, L1_attn_A_log, L1_attn_conv_q_w, L1_attn_conv_k_w, L1_attn_conv_v_w, L1_attn_gnorm_w, L1_attn_dt_bias)
    x = x + _L1_ffn_ref(_layernorm(x, axis=-1), L1_ffn_norm1_w, L1_ffn_norm2_w, L1_ffn_wq, L1_ffn_wk, L1_ffn_wv, L1_ffn_wo, L1_ffn_router_w, L1_ffn_sh_gate, L1_ffn_sh_up, L1_ffn_sh_down, L1_ffn_e_gate, L1_ffn_e_up, L1_ffn_e_down)
    return x

_drawn_inputs = setup_inputs


def setup_inputs(seed=0):
    import zlib

    import numpy as np

    out = dict(_drawn_inputs(seed))
    spreads = {'L0_attn_ln_g': (1.0, 0.2),
     'L0_attn_ln_b': (0.0, 0.1),
     'L1_attn_bb': (0.0, 0.8),
     'L1_attn_gnorm_w': (1.0, 0.6),
     'L1_ffn_norm1_w': (1.0, 0.6),
     'L1_ffn_norm2_w': (1.0, 0.6)}
    factors = {'L0_ffn_Wg': 8.0,
     'L0_ffn_W1': 8.0,
     'L0_ffn_W2': 8.0,
     'L0_ffn_Ws1': 3.471,
     'L0_ffn_Ws2': 3.46,
     'L1_attn_Wgk': 8.0,
     'L1_attn_Wb': 6.867,
     'L1_attn_A_log': 5.989,
     'L1_attn_dt_bias': 2.891,
     'L1_ffn_wq': 8.0,
     'L1_ffn_wk': 8.0,
     'L1_ffn_wv': 8.0,
     'L1_ffn_wo': 8.0,
     'L1_ffn_router_w': 7.17,
     'L1_ffn_sh_gate': 4.528,
     'L1_ffn_sh_up': 4.483,
     'L1_ffn_sh_down': 4.479,
     'L1_ffn_e_gate': 6.382,
     'L1_ffn_e_up': 6.296,
     'L1_ffn_e_down': 6.308}
    for name, (base, spread) in spreads.items():
        noise = np.random.default_rng([zlib.crc32(name.encode()), seed]).standard_normal(out[name].shape)
        drawn = base * np.exp(spread * noise) if base else spread * noise
        out[name] = jnp.asarray(drawn.astype(out[name].dtype))
    for name, factor in factors.items():
        out[name] = (out[name] * factor).astype(out[name].dtype)
    return out
```

```python
from contextlib import ExitStack

import numpy as np

import concourse.bass as bass
from concourse import mybir

F32 = mybir.dt.float32
BF16 = mybir.dt.bfloat16
U32 = mybir.dt.uint32
ALU = mybir.AluOpType
ACT = mybir.ActivationFunctionType
AX = mybir.AxisListType

P = 128
B, T, C = 8, 512, 256
HEADS, DH = 16, 16
TB = 64
NBLK = T // TB
COLS = B * TB
NT = COLS // P
KC = C // P
E0, H0 = 16, 128
E1, F1 = 8, 512
TAPS = 4
PADT = TB + TAPS - 1


class Tally:

    def __init__(self, sem, per_pass, unit=1, start=1):
        self.sem, self.per, self.unit, self.start = sem, per_pass, unit, start

    def at(self, i, k):
        return i * (self.per * self.unit) + (k * self.unit + self.start)


class Steps:

    def __init__(self, eng, sem):
        self.eng, self.sem, self.n = eng, sem, 0

    def mark(self, instruction):
        instruction.then_inc(self.sem, 1)
        self.n += 1
        return self.n

    def after(self, n):
        self.eng.wait_ge(self.sem, n)

    def link(self, instruction):
        self.after(self.mark(instruction))

    def reset(self):
        if self.n:
            self.after(self.n)
            self.eng.sem_inc(self.sem, -self.n)
            self.n = 0


N_SMALL = 7 + 3 + P // DH + 3
N_W = 2 + (E0 // 4) * (KC + 1) + 5 + 2


N_DW = 10


def rope_table():
    half = DH // 4
    freq = np.float32(10000.0) ** (-np.arange(half, dtype=np.float32) / np.float32(half))
    ang = np.arange(T, dtype=np.float32)[:, None] * freq[None, :].astype(np.float32)
    cos, sin = np.cos(ang).T, np.sin(ang).T
    tab = np.stack([np.concatenate([cos, cos]), np.concatenate([-sin, sin])]).astype(np.float32)
    return np.ascontiguousarray(tab.reshape(2, 2 * half, NBLK, TB).transpose(2, 0, 1, 3).reshape(NBLK, -1))


def two_layers(nc, a, out, scratch):
    ctx = ExitStack()
    with ctx:
        def sb(name, shape, dt=F32):
            return ctx.enter_context(nc.sbuf_tensor(name, shape, dt))

        def sem(name):
            return ctx.enter_context(nc.semaphore(name))

        def tally(name, per, unit=1, start=1):
            return Tally(sem(name), per, unit, start)

        PS = ctx.enter_context(nc.psum_tensor("PS", [P, 8, 512], F32))
        X = sb("X", [P, NBLK, NT, C])
        EXP = sb("EXP", [P, 24576])
        w1 = EXP[:, 0:8192].rearrange("p (e k n) -> p e k n", e=E0, k=KC)
        w2 = EXP[:, 8192:12288].rearrange("p (e n) -> p e n", e=E0)
        WORK = EXP[:, 12288:24576]
        used = [0]

        def work(n):
            used[0] += n
            assert used[0] <= 12288, used
            return WORK[:, used[0] - n:used[0]]

        ident = sb("ident", [P, P])
        mean_mat = sb("mean_mat", [P, P])
        iota = sb("iota", [P, E0])
        eps = sb("eps", [P, 4])
        WA = sb("WA", [P, 6912])
        taken = [0]

        def small(*shape):
            n = int(np.prod(shape))
            taken[0] += n
            assert taken[0] <= 6912
            names = "abcd"[:len(shape)]
            ap = WA[:, taken[0] - n:taken[0]]
            if len(shape) == 1:
                return ap
            return ap.rearrange(f"p ({' '.join(names)}) -> p {' '.join(names)}",
                                **{c: s for c, s in zip(names[:-1], shape[:-1])})

        wT = small(4, KC, C)
        wgT = small(KC, E0)
        ws1 = small(KC, 2 * C)
        ws2 = small(KC, C)
        wp = small(5, KC, C)
        wgb = small(KC, 48)
        vec0 = sb("vec0", [P, 8, KC])
        taps = sb("taps", [P, 3, KC, TAPS])
        gnorm = sb("gnorm", [P, 1])
        gpar = sb("gpar", [48, 4])
        stats = sb("stats", [P, NT, 6])
        mv = sb("mv", [P, NT, 2])
        sd = sb("sd", [P, NT])
        rs = sb("rs", [P, NT])
        xn = work(NT * C).rearrange("p (i n) -> p i n", i=NT)
        XN = work(KC * B * (TB + 1)).rearrange("p (h b t) -> p h b t", h=KC, b=B)
        DF = work(KC * COLS).rearrange("p (h b t) -> p h b t", h=KC, b=B)
        XMf = work(3 * KC * COLS)
        XM = XMf.rearrange("p (m h n) -> p m h n", m=3, h=KC)
        KV = work(KC * COLS).rearrange("p (h n) -> p h n", h=KC)
        FP = work(8 * DH * DH).rearrange("p (t v d) -> p t v d", t=8, v=DH)
        SQ = FP.rearrange("p t v d -> p (t v d)")[:, 0:DH * TB].rearrange("p (d t) -> p d t", d=DH)
        ROPE = work(2 * 8 * TB).rearrange("p (m d t) -> p m d t", m=2, d=8)
        raw = XMf[:, 0:2048].rearrange("p (m h n) -> p m h n", m=4, h=KC)
        rawg = XMf[:, 2048:2048 + C]
        DFf = DF.rearrange("p h b t -> p h (b t)")
        XF = DFf
        Hh = XMf[:, 0:1536].rearrange("p (r n) -> p r n", r=3)
        SG = XMf[:, 1536:2560].rearrange("p (r n) -> p r n", r=2)
        ZB = [KV.rearrange("p h n -> p (h n)"), xn.rearrange("p i n -> p (i n)")]
        CV = XM
        ST = work(KC * COLS).rearrange("p (h n) -> p h n", h=KC)
        GS = KV
        LG = sb("LG", [P, NT, E0])
        MX = sb("MX", [P, NT, 8])
        MI = sb("MI", [P, NT, 8], U32)
        MF = sb("MF", [P, NT, 8])
        NM = sb("NM", [P, NT])
        ZS = sb("ZS", [P, NT])
        E2 = sb("E2", [P, NT])
        W12 = sb("W12", [P, NT, 2])
        EX = sb("EX", [P, NT, E0])
        CW = sb("CW", [P, NT, E0])
        CT = sb("CT", [P, NT, E0])
        GB, GT1 = ZB[1][0:48, 0:COLS], ZB[1][0:48, COLS:2 * COLS]
        R2 = sb("R2", [P, 12512])
        cut = [0]

        def part(*shape):
            n = int(np.prod(shape))
            cut[0] += n
            assert cut[0] <= 12512, cut
            names = "abcde"[:len(shape)]
            ap = R2[:, cut[0] - n:cut[0]]
            return ap if len(shape) == 1 else ap.rearrange(
                f"p ({' '.join(names)}) -> p {' '.join(names)}", **{c: m for c, m in zip(names[:-1], shape[:-1])})

        PRE = part(3, KC, B, PADT)
        RX = part(3, DH, TB)
        RQ, RK, RV = RX[:, 0, :, :], RX[:, 1, :, :], RX[:, 2, :, :]
        EGB = part(3, TB)
        EG, BT, NBE = EGB[:, 0, :], EGB[:, 1, :], EGB[:, 2, :]
        RN = part(3, TB)
        OO = part(DH, TB)
        HIST = part(16, DH, DH)
        PR = part(DH, DH)
        UP = part(DH, DH)
        PD = sb("PD", [P, DH])
        DL = sb("DL", [P, DH])

        vec_step = sem("vec_step")
        loaded = sem("loaded")
        raw_loaded = sem("raw_loaded")
        x_loaded = sem("x_loaded")
        const_ready = sem("const_ready")
        wt_ready = sem("wt_ready")
        wt_kept = sem("wt_kept")
        setup_done = sem("setup_done")
        out_done = sem("out_done")
        first_loaded = sem("first_loaded")
        w_loaded = sem("w_loaded")
        tallies = []

        def tl(name, per, unit=1, start=1):
            tallies.append(tally(name, per, unit, start))
            return tallies[-1]

        stats_ready = tl("stats_ready", 3)
        std_ready = tl("std_ready", 3)
        norm_ready = tl("norm_ready", 3)
        turned = tl("turned", 3)
        xT_ready = tl("xT_ready", 6)
        mixed = tl("mixed", 3)
        proj_ready = tl("proj_ready", 3)
        k_kept = tl("k_kept", 2)
        o_ready = tl("o_ready", 1)
        mu_ready = tl("mu_ready", 1)
        centred = tl("centred", 2)
        squared = tl("squared", 2)
        var_ready = tl("var_ready", 1)
        ostd_ready = tl("ostd_ready", 1)
        y_scaled = tl("y_scaled", 2)
        y_ready = tl("y_ready", 2)
        attn0_ready = tl("attn0_ready", 1)
        attn0_added = tl("attn0_added", 1)
        logits_ready = tl("logits_ready", 1)
        logits_kept = tl("logits_kept", 1)
        max_ready = tl("max_ready", 1)
        exps_ready = tl("exps_ready", 1)
        cw_ready = tl("cw_ready", 1)
        NU = 2 + E0
        NJ = 1 + E0
        ug_ready = tl("ug_ready", NU)
        silu_ready = tl("silu_ready", NU)
        h_ready = tl("h_ready", NU)
        z_ready = tl("z_ready", NJ)
        z_kept = tl("z_kept", NJ)
        z_added = tl("z_added", NJ)
        pre_ready = tl("pre_ready", 3)
        pre_kept = tl("pre_kept", 6)
        gates_ready = tl("gates_ready", 1)
        gates_kept = tl("gates_kept", 2)
        relu_ready = tl("relu_ready", 1)
        softplus_ready = tl("softplus_ready", 1)
        decay_ready = tl("decay_ready", 1)
        beta_ready = tl("beta_ready", 1)
        gproj_ready = tl("gproj_ready", 1)
        gs_ready = tl("gs_ready", 2)
        conv_ready = tl("conv_ready", 6)
        cv_ready = tl("cv_ready", 6)
        stored = tl("stored", 9, 16)
        rec_loaded = tl("rec_loaded", 6, 16)
        sq_ready = tl("sq_ready", 3)
        ss_ready = tl("ss_ready", 3)
        rstd_ready = tl("rstd_ready", 3)
        rnorm_ready = tl("rnorm_ready", 3)
        rec_ready = tl("rec_ready", 1)
        hist_ready = tl("hist_ready", 8)
        hist_used = tl("hist_used", 8)
        o_written = tl("o_written", 1)
        o_scaled = tl("o_scaled", 1)
        o_stored = tl("o_stored", 1, 16)
        rec_done = sem("rec_done")
        og_loaded = tl("og_loaded", 3, 16)
        og_ready = tl("og_ready", 2)
        attn1_ready = tl("attn1_ready", 1)
        attn1_added = tl("attn1_added", 1)

        qkv_dram = scratch["qkv"]
        gb_dram = scratch["gb"]
        gate_dram = scratch["gate"]
        o_dram = scratch["o"]

        QPOS, KPOS = (0, 1, 0, 2, 0, 1), (0, 0, 1, 0, 2, 1)
        SROWS = len(QPOS) * DH
        NPAIR = B // 2
        KT = T // P
        NG = 2 * (HEADS // 4)
        NTOK = B * T // P
        FT = F1 // P
        ALL = E1 + 1
        taken[0] = 0
        wqkv, wo1 = small(3, KC, C), small(KC, C)
        wrt = small(KC, E1)
        shg, shu, shd = small(KC, F1), small(KC, F1), small(FT, C)
        n2b = small(C)
        n1w = small(KC)
        LGT = small(NTOK, E1)
        OH = small(2, NTOK, E1)
        CWS = small(NTOK, E1)
        CWB = small(NT, ALL)
        ZZ = small(NTOK)
        WW = small(2, NTOK)
        eg_w = EXP[:, 0:8192].rearrange("p (e k n) -> p e k n", e=E1, k=KC)
        eu_w = EXP[:, 8192:16384].rearrange("p (e k n) -> p e k n", e=E1, k=KC)
        ed_w = EXP[:, 16384:24576].rearrange("p (e k n) -> p e k n", e=E1, k=FT)
        XI = EXP[:, 16384:24576].rearrange("p (j i n) -> p j i n", j=NBLK, i=NT)
        EARLY = 12288 // (KC * F1) - E1
        used[0] = 0
        xnp = work(NBLK * C).rearrange("p (j n) -> p j n", j=NBLK)
        HT = work(KC * 2 * T).rearrange("p (h b n) -> p h b n", h=KC, b=2)
        R1 = work(4 * T).rearrange("p (m h n) -> p m h n", m=2, h=KC)
        SP3 = work(6 * T).bitcast(BF16).rearrange("p (m s h n) -> p m s h n", m=2, s=3, h=KC)
        cut[0] = 0
        VO = part(KT, HEADS, 32)
        SQX = part(C)
        SS1, SD1 = part(NBLK), part(NBLK)
        used[0] = 0
        QK = [work(2048).bitcast(BF16).rearrange("p (m h n) -> p m h n", m=2, h=4) for _ in range(4)]
        VA = [work(2048).rearrange("p (k h n) -> p k h n", k=KT, h=HEADS) for _ in range(2)]
        cut[0] = 0
        PT = [part(4, T) for _ in range(2)]
        CTX = part(KT, C)
        CTT = part(KC, NBLK, 2, TB)
        MXS = [part(DH), part(DH)]
        RC = part(DH)
        VT = part(T)
        MROW = part(P // 2).bitcast(BF16)
        cut[0] = 0
        HT2 = part(KC, NTOK, P)
        HSf = part(FT * COLS)
        SGf = part(2 * COLS)
        HS = HSf.rearrange("p (r n) -> p r n", r=FT)
        SG2 = SGf.rearrange("p (r n) -> p r n", r=2)
        XN2 = HSf[:, 0:NT * C].rearrange("p (i n) -> p i n", i=NT)
        HB2 = HSf[:, NT * C:2 * NT * C].rearrange("p (h n) -> p h n", h=KC)
        SQ2 = SGf[:, 0:C]
        SS2, SD2 = SGf[:, C:C + NT], SGf[:, C + NT:C + 2 * NT]
        MX2 = part(NTOK, 8)
        MF2 = part(NTOK, 8)
        MI2 = part(NTOK * 8).bitcast(U32).rearrange("p (g e) -> p g e", g=NTOK)
        EX2 = part(NTOK, E1)

        st_dram, v_dram, xi_dram = scratch["stack"], scratch["v"], scratch["xi"]

        d_w_loaded = sem("d_w_loaded")
        exp_loaded = sem("exp_loaded")
        up_loaded = sem("up_loaded")
        down_loaded = sem("down_loaded")
        xstats_ready = tl("xstats_ready", 1)
        xstd_ready = tl("xstd_ready", 1)
        xi_saved = tl("xi_saved", 1, 16)
        xi_loaded = sem("xi_loaded")
        xi_added = sem("xi_added")
        blocks_done = sem("blocks_done")
        d_const = sem("d_const")
        route_in = sem("route_in")
        route_exp = sem("route_exp")
        shares_ready = sem("shares_ready")
        d_step, a_step = sem("d_step"), sem("a_step")
        sstd_ready = tl("sstd_ready", 1)
        pn_ready = tl("pn_ready", 1)
        pturn_ready = tl("pturn_ready", 1)
        hT_ready = tl("hT_ready", 4)
        qk_ready = tl("qk_ready", 4)
        hi_ready = tl("hi_ready", 8)
        r1_ready = tl("r1_ready", 8)
        mid_ready = tl("mid_ready", 8)
        lo_ready = tl("lo_ready", 8, 1, 5)
        vproj_ready = tl("vproj_ready", 2)
        vo_ready = tl("vo_ready", 2)
        st_stored = tl("st_stored", 16, 16)
        st_free = tl("st_free", 2)
        vo_stored = tl("vo_stored", 2, 16)
        qk_loaded = [tl(f"qk_loaded{n}", 24, 16) for n in range(4)]
        va_loaded = tl("va_loaded", 2, 16)
        ms_ready = tl("ms_ready", 16 * NG)
        ms_used = tl("ms_used", 16 * NG, 1, 2)
        mt_ready = tl("mt_ready", NG, 1, 2)
        mrow_ready = tl("mrow_ready", NG)
        mrow_in = tl("mrow_in", NG, 16)
        sc_ready = tl("sc_ready", 8 * NG, 1, 25)
        exp_ready = tl("exp_ready", 8 * NG, 1, 2)
        pv_ready = tl("pv_ready", KT * NG, 1, 17)
        vt_ready = tl("vt_ready", NG)
        vtt_ready = tl("vtt_ready", NG)
        ctx_ready = tl("ctx_ready", NG)
        cx_ready = tl("cx_ready", 4)
        cx_kept = tl("cx_kept", 4)
        op_ready = tl("op_ready", 4)
        op_added = tl("op_added", 4)
        rstd2_ready = tl("rstd2_ready", 1)
        h2_ready = tl("h2_ready", 1)
        h2_turned = tl("h2_turned", 1)
        ht2_ready = tl("ht2_ready", 2)
        lg_ready = tl("lg_ready", 1)
        lg_kept = tl("lg_kept", 1)
        su_ready = tl("su_ready", FT * ALL)
        ss_silu = tl("ss_silu", FT * ALL)
        sh_ready = tl("sh_ready", FT * ALL, 1, 2)
        sz_ready = tl("sz_ready", ALL)
        sz_added = tl("sz_added", ALL, 1, 2)

        block = ctx.enter_context(nc.Block())

        waited = {}

        def apart(eng):
            if eng not in waited:
                waited[eng] = sem(f"waited{len(waited)}")
            eng.sem_inc(waited[eng], 1)

        def passes(eng, body):
            body(0, False, True)
            with eng.Fori(1, NBLK) as j:
                body(j, True, True)
            body(NBLK, True, False)

        @block.sync
        def _(sp):
            for t in tallies:
                sp.sem_inc(t.sem, t.start)
            for m, name in enumerate(("L0_attn_Wk", "L0_attn_Wv", "L0_attn_Wr", "L0_attn_Wo")):
                sp.dma_start(raw[:, m, :, :], a[name].rearrange("(h p) c -> p h c", p=P)).then_inc(raw_loaded, 16)
            sp.dma_start(rawg[0:E0, :], a["L0_ffn_Wg"]).then_inc(raw_loaded, 16)

            def load(dst, src, landed=loaded):
                sp.dma_start(dst, src, allow_slow_non_contiguous=True).then_inc(landed, 16)
            for n, name in enumerate(("L0_attn_time_mix_k", "L0_attn_time_mix_v", "L0_attn_time_mix_r")):
                load(vec0[:, n, :], a[name].rearrange("a b (h p) -> p (a b h)", p=P))
            for n, name in ((3, "L0_attn_time_decay"), (4, "L0_attn_time_first")):
                load(vec0[:, n, :], a[name].rearrange("(h u) s -> (u s) h", h=KC))
            for n, name in ((5, "L0_attn_ln_g"), (6, "L0_attn_ln_b")):
                load(vec0[:, n, :], a[name].rearrange("(h p) -> p h", p=P))
            for m, name in enumerate(("L1_attn_conv_q_w", "L1_attn_conv_k_w", "L1_attn_conv_v_w")):
                load(taps[:, m, :, :], a[name].rearrange("(h p) k -> p h k", p=P))
            for g in range(P // DH):
                load(gnorm[g * DH:(g + 1) * DH, :], a["L1_attn_gnorm_w"].rearrange("(d a) -> d a", a=1))
            load(gpar[0:HEADS, 0:1], a["L1_attn_dt_bias"].rearrange("(d a) -> d a", a=1))
            load(gpar[32:48, 0:1], a["L1_attn_bb"].rearrange("(d a) -> d a", a=1))
            load(gpar[0:HEADS, 1:2], a["L1_attn_A_log"].rearrange("(d a) -> d a", a=1))
            for j0, j1 in ((0, 1), (1, NBLK)):
                for b in range(B):
                    load(X[TB * (b % 2):TB * (b % 2) + TB, j0:j1, b // 2, :],
                         a["L0_attn_x"][b].rearrange("(j t) c -> t j c", t=TB)[:, j0:j1, :], x_loaded)
            load(ws1, a["L0_ffn_Ws1"].rearrange("(k p) n -> p k n", p=P), w_loaded)
            load(ws2, a["L0_ffn_Ws2"].rearrange("(k p) n -> p k n", p=P), w_loaded)
            for e in range(0, E0, 4):
                for k in range(KC):
                    load(w1[:, e:e + 4, k, :], a["L0_ffn_W1"][e:e + 4, k * P:k * P + P, :].rearrange("e p n -> p e n"),
                         w_loaded)
                load(w2[:, e:e + 4, :], a["L0_ffn_W2"][e:e + 4].rearrange("e p n -> p e n"), w_loaded)
            for m, name in enumerate(("L1_attn_Wq", "L1_attn_Wk", "L1_attn_Wv", "L1_attn_Wg", "L1_attn_Wo")):
                load(wp[:, m, :, :], a[name].rearrange("(k p) n -> p k n", p=P), w_loaded)
            sp.wait_ge(const_ready, 1)
            load(wgb[:, :, 0:HEADS], a["L1_attn_Wgk"].rearrange("(k p) n -> p k n", p=P), w_loaded)
            load(wgb[:, :, 32:48], a["L1_attn_Wb"].rearrange("(k p) n -> p k n", p=P), w_loaded)

            def body(j, rec, blk):
                if blk:
                    for m in range(2):
                        r = 32 * m
                        sp.wait_ge((decay_ready, beta_ready)[m].sem, (decay_ready, beta_ready)[m].at(j, 1))
                        sp.dma_start(gb_dram[j, m].rearrange("b h t -> h b t"),
                                     GB[r:r + HEADS, :].rearrange("h (b t) -> h b t", b=B)).then_inc(stored.sem, 16)
                    sp.wait_ge(gs_ready.sem, gs_ready.at(j, 2))
                    sp.dma_start(gate_dram[j], GS[:, :, :].rearrange("p h n -> p (h n)")).then_inc(stored.sem, 16)
                    for m in range(3):
                        for h in range(KC):
                            sp.wait_ge(cv_ready.sem, cv_ready.at(j, 2 * m + h + 1))
                            sp.dma_start(qkv_dram[j, m, :, h * P:h * P + P, :].rearrange("b p t -> p b t"),
                                         CV[:, m, h, :].rearrange("p (b t) -> p b t", b=B)).then_inc(stored.sem, 16)
                if rec:
                    sp.wait_ge(o_scaled.sem, o_scaled.at(j - 1, 1))
                    sp.dma_start(o_dram[j - 1].rearrange("b h v t -> (b h) (v t)"),
                                 OO[:, :, :].rearrange("p v t -> p (v t)")).then_inc(o_stored.sem, 16)
                if blk:
                    sp.wait_ge(stored.sem, stored.at(j, 9))
                    if rec:
                        sp.wait_ge(o_stored.sem, o_stored.at(j - 1, 1))
                    for m in range(3):
                        sp.dma_start(RX[:, m, :, :].rearrange("p d t -> p (d t)"),
                                     qkv_dram[j, m].rearrange("b (h d) t -> (b h) (d t)", d=DH))\
                            .then_inc(rec_loaded.sem, 16)
                    for m in range(2):
                        sp.dma_start(EGB[:, m, :], gb_dram[j, m].rearrange("b h t -> (b h) t"))\
                            .then_inc(rec_loaded.sem, 16)
                    sp.dma_start(ROPE.rearrange("p m d t -> p (m d t)"), a["rope"][j].partition_broadcast(P))\
                        .then_inc(rec_loaded.sem, 16)
            passes(sp, body)
            sp.wait_ge(o_stored.sem, o_stored.at(NBLK - 1, 1))
            with sp.Fori(0, NBLK) as j:
                sp.wait_ge(og_ready.sem, og_ready.at(j, 0))
                for h in range(KC):
                    sp.dma_start(KV[:, h, :].rearrange("p (b t) -> p b t", b=B),
                                 o_dram[j, :, h * 8:h * 8 + 8].rearrange("b g v t -> (g v) b t"))\
                        .then_inc(og_loaded.sem, 16)
                sp.dma_start(XM[:, 1, :, :].rearrange("p h n -> p (h n)"), gate_dram[j]).then_inc(og_loaded.sem, 16)
                sp.wait_ge(attn1_added.sem, attn1_added.at(j, 1))
                sp.dma_start(xi_dram[j], X[:, j, :, :].rearrange("p i n -> p (i n)")).then_inc(xi_saved.sem, 16)

            sp.wait_ge(blocks_done, 1)
            for m, name in enumerate(("L1_ffn_wq", "L1_ffn_wk", "L1_ffn_wv")):
                load(wqkv[:, m, :, :], a[name].rearrange("(k p) n -> p k n", p=P), d_w_loaded)
            load(n1w, a["L1_ffn_norm1_w"].rearrange("(h p) -> p h", p=P), d_w_loaded)
            load(wo1, a["L1_ffn_wo"].rearrange("(k p) n -> p k n", p=P), d_w_loaded)
            load(wrt, a["L1_ffn_router_w"].rearrange("(k p) n -> p k n", p=P), d_w_loaded)
            load(shg, a["L1_ffn_sh_gate"].rearrange("(k p) n -> p k n", p=P), d_w_loaded)
            load(shu, a["L1_ffn_sh_up"].rearrange("(k p) n -> p k n", p=P), d_w_loaded)
            load(shd, a["L1_ffn_sh_down"].rearrange("(k p) n -> p k n", p=P), d_w_loaded)
            load(n2b, a["L1_ffn_norm2_w"].partition_broadcast(P), d_w_loaded)
            for e in range(E1):
                load(eg_w[:, e, :, :], a["L1_ffn_e_gate"][e].rearrange("(k p) n -> p k n", p=P), exp_loaded)
            for e in range(EARLY):
                load(eu_w[:, e, :, :], a["L1_ffn_e_up"][e].rearrange("(k p) n -> p k n", p=P), exp_loaded)
            with sp.Fori(0, NPAIR) as i:
                for b2 in range(2):
                    sp.wait_ge(vo_ready.sem, vo_ready.at(i, b2 + 1))
                    sp.dma_start(v_dram[i, b2], VO.rearrange("p k h n -> p (k h n)")).then_inc(vo_stored.sem, 16)
                    for m in range(2):
                        for h in range(KC):
                            sp.wait_ge(lo_ready.sem, lo_ready.at(i, 4 * b2 + 2 * m + h + 1))
                            for g2 in range(2):
                                sp.dma_start(st_dram[m, i, b2, 2 * h + g2].rearrange("s p n -> p s n"),
                                             SP3[64 * g2:64 * g2 + 64, m, :, h, :]).then_inc(st_stored.sem, 16)
                    sp.wait_ge(st_stored.sem, st_stored.at(i, 8 * b2 + 8))
                    sp.sem_inc(st_free.sem, 1)
            sp.wait_ge(vo_stored.sem, vo_stored.at(NPAIR, 0))

            def load_qk(i, n):
                sp.wait_ge(sc_ready.sem, sc_ready.at(i, 8 * (n - 3)))
                for m, pos in enumerate((QPOS, KPOS)):
                    for r, s in enumerate(pos):
                        sp.dma_start(QK[n % 4][DH * r:DH * r + DH, m, :, :],
                                     st_dram[m, i, n // 4, n % 4, s].rearrange("(h d) n -> d h n", d=DH))\
                            .then_inc(qk_loaded[n % 4].sem, 16)

            def load_values(i, b2):
                sp.wait_ge(pv_ready.sem, pv_ready.at(i, 4 * KT * (b2 - 1)))
                sp.dma_start(VA[b2].rearrange("p k h n -> p (k h n)"), v_dram[i, b2]).then_inc(va_loaded.sem, 16)

            def groups(i, last):
                for n in range(NG):
                    sp.wait_ge(mrow_ready.sem, mrow_ready.at(i, n + 1))
                    sp.dma_start(QK[n % 4][SROWS:SROWS + 1, 0, :, :], MROW[0:DH, :]).then_inc(mrow_in.sem, 16)
                    if n == 1:
                        load_values(i, 1)
                    if n == 5 and not last:
                        load_values(i + 1, 0)
                    if n + 3 < NG:
                        load_qk(i, n + 3)
                    elif not last:
                        load_qk(i + 1, n + 3 - NG)
            load_values(0, 0)
            for n in range(3):
                load_qk(0, n)
            with sp.Fori(0, NPAIR - 1) as i:
                groups(i, False)
            groups(NPAIR - 1, True)
            sp.wait_ge(op_added.sem, op_added.at(NPAIR, 0))
            sp.wait_ge(xi_saved.sem, xi_saved.at(NBLK, 0))
            sp.dma_start(XI.rearrange("p j i n -> p j (i n)"), xi_dram.rearrange("j p n -> p j n")).then_inc(xi_loaded, 16)
            for e in range(EARLY, E1):
                load(eu_w[:, e, :, :], a["L1_ffn_e_up"][e].rearrange("(k p) n -> p k n", p=P), up_loaded)
            sp.wait_ge(xi_added, NBLK)
            for e in range(E1):
                load(ed_w[:, e, :, :], a["L1_ffn_e_down"][e].rearrange("(k p) n -> p k n", p=P), down_loaded)
            rows = out.rearrange("(i b) t c -> b t i c", b=2)
            with sp.Fori(0, NBLK) as j:
                sp.wait_ge(sz_added.sem, sz_added.at(j, ALL))
                for b2 in range(2):
                    sp.dma_start(rows[b2, bass.ds(j * TB, TB), :, :],
                                 X[TB * b2:TB * b2 + TB, bass.ds(j, 1), :, :].rearrange("p j i n -> p (j i) n"))\
                        .then_inc(out_done, 16)
            sp.wait_ge(out_done, 16 * 2 * NBLK)

        @block.gpsimd
        def _(pool):
            steps = Steps(pool, sem("pool_step"))
            steps.link(pool.memset(ident[:, :], 0.0))
            steps.link(pool.affine_select(out=ident[:, :], in_=ident[:, :], compare_op=ALU.not_equal, fill=1.0,
                                          base=0, pattern=[[-1, P]], channel_multiplier=1))
            steps.reset()
            pool.memset(mean_mat[:, :], 1.0 / C)
            pool.memset(eps[:, 0:1], 1e-5)
            pool.memset(eps[:, 1:2], 1e-6)
            pool.memset(XN, 0.0)
            pool.memset(wgb, 0.0)
            pool.memset(ST, 0.0)
            pool.memset(PRE[:, :, :, :, :], 0.0)
            pool.memset(HIST[:, 15, :, :], 0.0)
            pool.iota(iota[:, :], pattern=[[1, E0]], base=0, channel_multiplier=0,
                      allow_small_or_imprecise_dtypes=True).then_inc(const_ready, 1)

            def fold(x, n):
                while n > 1:
                    n //= 2
                    steps.link(pool.tensor_tensor(x[:, 0:n, :], x[:, 0:n, :], x[:, n:2 * n, :], ALU.add))

            def body(j, rec, blk):
                if rec:
                    r = j - 1
                    for m in range(2):
                        pool.wait_ge(sq_ready.sem, sq_ready.at(r, m + 1))
                        src = (SQ, OO)[m]
                        n = DH // 2
                        while n > 1:
                            steps.link(pool.tensor_tensor(src[:, 0:n, :], src[:, 0:n, :], src[:, n:2 * n, :], ALU.add))
                            n //= 2
                        pool.tensor_tensor(RN[:, m, :], src[:, 0, :], src[:, 1, :], ALU.add)\
                            .then_inc(ss_ready.sem, 1)
                    for m in range(2):
                        pool.wait_ge(rnorm_ready.sem, rnorm_ready.at(r, m + 1))
                        x = RX[:, m, :, :]
                        steps.link(pool.tensor_tensor(x, x, RN[:, m, :].unsqueeze(1).to_broadcast([P, DH, TB]),
                                                      ALU.mult))
                        steps.mark(pool.tensor_tensor(SQ[:, 0:8, :], x[:, 0:8, :], ROPE[:, 0, :, :], ALU.mult))
                        steps.mark(pool.tensor_tensor(SQ[:, 8:12, :], x[:, 4:8, :], ROPE[:, 1, 0:4, :], ALU.mult))
                        steps.link(pool.tensor_tensor(SQ[:, 12:16, :], x[:, 0:4, :], ROPE[:, 1, 4:8, :], ALU.mult))
                        steps.link(pool.tensor_tensor(x[:, 0:8, :], SQ[:, 0:8, :], SQ[:, 8:16, :], ALU.add))
                    steps.mark(pool.tensor_tensor(RV, RV, BT.unsqueeze(1).to_broadcast([P, DH, TB]), ALU.mult))
                    steps.link(pool.tensor_tensor(NBE, BT, EG, ALU.mult))
                    pool.tensor_scalar(NBE, NBE, -1.0, None, ALU.mult).then_inc(rec_ready.sem, 1)

                def add_z(k):
                    pool.wait_ge(z_kept.sem, z_kept.at(j, k + 1))
                    if k:
                        pool.wait_ge(z_added.sem, z_added.at(j, k))
                    x = X[:, j, :, :]
                    apart(pool)
                    pool.tensor_tensor(x, x, ZB[k % 2].rearrange("p (i n) -> p i n", i=NT), ALU.add)\
                        .then_inc(z_added.sem, 1)

                def outputs(g):
                    pool.wait_ge(hist_ready.sem, hist_ready.at(j - 1, g + 1))
                    q = RQ[:, :, 8 * g:8 * g + 8].rearrange("p d t -> p t d").unsqueeze(2)\
                        .to_broadcast([P, 8, DH, DH])
                    steps.after(steps.n) if steps.n else None
                    pool.tensor_tensor(FP, HIST[:, 8 * (g % 2):8 * (g % 2) + 8, :, :], q, ALU.mult)\
                        .then_inc(hist_used.sem, 1)
                    pool.wait_ge(hist_used.sem, hist_used.at(j - 1, g + 1))
                    n = DH // 2
                    while n > 1:
                        steps.link(pool.tensor_tensor(FP[:, :, :, 0:n], FP[:, :, :, 0:n], FP[:, :, :, n:2 * n],
                                                      ALU.add))
                        n //= 2
                    steps.mark(pool.tensor_tensor(OO[:, :, 8 * g:8 * g + 8].rearrange("p v t -> p t v"),
                                                  FP[:, :, :, 0], FP[:, :, :, 1], ALU.add))

                for n in range(NU):
                    if rec and n >= 3 and n % 2 == 1:
                        outputs((n - 3) // 2)
                    if blk and n >= 1:
                        add_z(n - 1)
                if rec:
                    r = j - 1
                    steps.after(steps.n)
                    pool.sem_inc(o_written.sem, 1)
                    pool.wait_ge(sq_ready.sem, sq_ready.at(r, 3))
                    n = DH // 2
                    while n > 1:
                        steps.link(pool.tensor_tensor(SQ[:, 0:n, :], SQ[:, 0:n, :], SQ[:, n:2 * n, :], ALU.add))
                        n //= 2
                    pool.tensor_tensor(RN[:, 2, :], SQ[:, 0, :], SQ[:, 1, :], ALU.add).then_inc(ss_ready.sem, 1)
                    pool.wait_ge(rnorm_ready.sem, rnorm_ready.at(r, 3))
                    pool.tensor_tensor(OO[:, :, :], OO[:, :, :], RN[:, 2, :].unsqueeze(1).to_broadcast([P, DH, TB]),
                                       ALU.mult).then_inc(o_scaled.sem, 1)
                steps.reset()
            passes(pool, body)
            pool.wait_ge(blocks_done, 1)
            pool.memset(VO, 1.0).then_inc(d_const, 1)
            with pool.Fori(0, NPAIR) as i:
                for n in range(8):
                    m, h = (n // 2) % 2, n % 2
                    pool.wait_ge(mid_ready.sem, mid_ready.at(i, n + 1))
                    pool.tensor_tensor(SP3[:, m, 2, h, :], R1[:, m, h, :], SP3[:, m, 1, h, :], ALU.subtract)\
                        .then_inc(lo_ready.sem, 1)
            pool.wait_ge(st_stored.sem, st_stored.at(NPAIR, 0))
            for q in QK:
                pool.memset(q[SROWS:SROWS + 1, 1, :, :], 1.0).then_inc(d_const, 1)

        @block.tensor
        def _(pe):
            pe.wait_ge(const_ready, 1)
            pe.wait_ge(raw_loaded, 80)
            for m in range(4):
                for h in range(KC):
                    for r in range(KC):
                        last = nc.tensor.transpose(PS[:, m, h * C + r * P:h * C + r * P + P],
                                                   raw[:, m, r, h * P:h * P + P], ident[:, :])
            last.then_inc(wt_ready, 1)
            for h in range(KC):
                last = nc.tensor.transpose(PS[:, 4, h * E0:h * E0 + E0], rawg[0:E0, h * P:h * P + P],
                                           ident[0:E0, 0:E0])
            last.then_inc(wt_ready, 1)
            pe.wait_ge(setup_done, 1)

            def turn(j, n, bank):
                pe.wait_ge(norm_ready.sem, norm_ready.at(j, n + 1))
                for h in range(KC):
                    for i in range(NT):
                        last = nc.tensor.transpose(PS[:, bank + h, i * P:i * P + P], xn[:, i, h * P:h * P + P],
                                                   ident[:, :])
                last.then_inc(turned.sem, 1)

            def project(bank, w, x, n=C):
                for d in range(KC):
                    for h in range(KC):
                        last = nc.tensor.matmul(PS[:, bank + d, :], lhsT=w[:, h, d * P:d * P + P],
                                                rhs=x[:, h, :], start=h == 0, stop=h == KC - 1)
                return last

            def body(j, rec, blk):
                if not blk:
                    return
                if rec:
                    pe.wait_ge(gs_ready.sem, gs_ready.at(j, 0))
                turn(j, 0, 0)
                if rec:
                    pe.wait_ge(pre_kept.sem, pre_kept.at(j, 0))
                    pe.wait_ge(gates_kept.sem, gates_kept.at(j, 0))
                for m in range(3):
                    pe.wait_ge(mixed.sem, mixed.at(j, m + 1))
                    project(2 + 2 * m, wT[:, m, :, :], XM[:, m, :, :]).then_inc(proj_ready.sem, 1)
                pe.wait_ge(o_ready.sem, o_ready.at(j, 1))
                for h in range(KC):
                    last = nc.tensor.matmul(PS[:, 0, :], lhsT=mean_mat[:, :], rhs=KV[:, h, :],
                                            start=h == 0, stop=h == KC - 1)
                last.then_inc(mu_ready.sem, 1)
                pe.wait_ge(squared.sem, squared.at(j, 2))
                for h in range(KC):
                    last = nc.tensor.matmul(PS[:, 1, :], lhsT=mean_mat[:, :], rhs=XM[:, 0, h, :],
                                            start=h == 0, stop=h == KC - 1)
                last.then_inc(var_ready.sem, 1)
                pe.wait_ge(y_ready.sem, y_ready.at(j, 2))
                for i in range(NT):
                    for h in range(KC):
                        last = nc.tensor.matmul(PS[:, 2 + i // 2, (i % 2) * C:(i % 2) * C + C],
                                                lhsT=XM[:, 2, h, i * P:i * P + P], rhs=wT[:, 3, h, :],
                                                start=h == 0, stop=h == KC - 1)
                last.then_inc(attn0_ready.sem, 1)
                turn(j, 1, 4)
                pe.wait_ge(xT_ready.sem, xT_ready.at(j, 4))
                for i in range(NT):
                    for h in range(KC):
                        last = nc.tensor.matmul(PS[:, 6, i * E0:i * E0 + E0], lhsT=XF[:, h, i * P:i * P + P],
                                                rhs=wgT[:, h, :], start=h == 0, stop=h == KC - 1)
                last.then_inc(logits_ready.sem, 1)
                if not rec:
                    pe.wait_ge(w_loaded, 16 * N_W)

                def ug(n):
                    if n >= 2:
                        pe.wait_ge(h_ready.sem, h_ready.at(j, n - 1))
                    for g in range(2):
                        for h in range(KC):
                            w = ws1[:, h, g * C + n * P:g * C + n * P + P] if n < 2 else \
                                w1[:, n - 2, h, g * P:g * P + P]
                            last = nc.tensor.matmul(PS[:, 2 * (n % 2) + g, :], lhsT=w, rhs=XF[:, h, :],
                                                    start=h == 0, stop=h == KC - 1)
                    last.then_inc(ug_ready.sem, 1)

                def z(k):
                    pe.wait_ge(h_ready.sem, h_ready.at(j, k + 2))
                    if k >= 2:
                        pe.wait_ge(z_kept.sem, z_kept.at(j, k - 1))
                    elif k == 1:
                        pe.wait_ge(logits_kept.sem, logits_kept.at(j, 1))
                    tiles = ((0, ws2[:, 0, :]), (1, ws2[:, 1, :])) if k == 0 else (((k + 1) % 3, w2[:, k - 1, :]),)
                    for i in range(NT):
                        for r, w in tiles:
                            last = nc.tensor.matmul(PS[:, 4 + 2 * (k % 2) + i // 2, (i % 2) * C:(i % 2) * C + C],
                                                    lhsT=Hh[:, r, i * P:i * P + P], rhs=w,
                                                    start=r == tiles[0][0], stop=r == tiles[-1][0])
                    last.then_inc(z_ready.sem, 1)

                for n in range(NU):
                    ug(n)
                    if n >= 2:
                        z(n - 2)
                z(NJ - 1)
                turn(j, 2, 6)
                pe.wait_ge(xT_ready.sem, xT_ready.at(j, 6))
                for m in range(3):
                    project(2 * m, wp[:, m, :, :], XF).then_inc(pre_ready.sem, 1)
                for h in range(KC):
                    last = nc.tensor.matmul(PS[0:48, 6, :], lhsT=wgb[:, h, :], rhs=XF[:, h, :], start=h == 0,
                                            stop=h == KC - 1)
                last.then_inc(gates_ready.sem, 1)
                pe.wait_ge(pre_kept.sem, pre_kept.at(j, 2))
                project(0, wp[:, 3, :, :], XF).then_inc(gproj_ready.sem, 1)
            passes(pe, body)
            with pe.Fori(0, NBLK) as j:
                pe.wait_ge(og_ready.sem, og_ready.at(j, 2))
                for i in range(NT):
                    for h in range(KC):
                        last = nc.tensor.matmul(PS[:, 2 + i // 2, (i % 2) * C:(i % 2) * C + C],
                                                lhsT=XM[:, 0, h, i * P:i * P + P], rhs=wp[:, 4, h, :],
                                                start=h == 0, stop=h == KC - 1)
                last.then_inc(attn1_ready.sem, 1)
            pe.wait_ge(d_w_loaded, 16 * N_DW)
            with pe.Fori(0, NPAIR) as i:
                pe.wait_ge(pn_ready.sem, pn_ready.at(i, 1))
                for h in range(KC):
                    for j in range(NBLK):
                        last = nc.tensor.transpose(PS[:, 2 * h + j // 4, (j % 4) * P:(j % 4) * P + P],
                                                   xnp[:, j, h * P:h * P + P], ident[:, :])
                last.then_inc(pturn_ready.sem, 1)
                pe.wait_ge(hT_ready.sem, hT_ready.at(i, 4))
                for b2 in range(2):
                    pe.wait_ge(vo_ready.sem, vo_ready.at(i, b2))
                    for kt in range(KT):
                        for h in range(KC):
                            last = nc.tensor.matmul(PS[:, 4 + kt // 2, (kt % 2) * C:(kt % 2) * C + C],
                                                    lhsT=HT[:, h, b2, kt * P:kt * P + P], rhs=wqkv[:, 2, h, :],
                                                    start=h == 0, stop=h == KC - 1)
                    last.then_inc(vproj_ready.sem, 1)
                    for m in range(2):
                        if b2:
                            pe.wait_ge(r1_ready.sem, r1_ready.at(i, 2 * m + 2))
                        project(2 * m, wqkv[:, m, :, :], HT[:, :, b2, :]).then_inc(qk_ready.sem, 1)
                pe.wait_ge(r1_ready.sem, r1_ready.at(i, 8))
            pe.wait_ge(d_const, 5)
            pe.wait_ge(vo_ready.sem, vo_ready.at(NPAIR, 0))

            def max_scores(i, n, hh):
                if hh == 0:
                    pe.wait_ge(qk_loaded[n % 4].sem, qk_loaded[n % 4].at(i, 12 * (n // 4 + 1)))
                q = QK[n % 4]
                for qt in range(KT):
                    s = 16 * n + 4 * hh + qt
                    pe.wait_ge(ms_used.sem, ms_used.at(i, s - 1))
                    nc.tensor.matmul(PS[:, s % 2, :], lhsT=q[0:SROWS, 0, hh, qt * P:qt * P + P],
                                     rhs=q[0:SROWS, 1, hh, :], start=True, stop=True).then_inc(ms_ready.sem, 1)

            def max_row(i, n):
                pe.wait_ge(ms_used.sem, ms_used.at(i, 16 * (n + 1)))
                nc.tensor.transpose(PS[0:DH, 2, 0:P], MXS[n % 2], ident[:, :]).then_inc(mt_ready.sem, 1)

            def scores(i, n, kt):
                if kt == 0:
                    pe.wait_ge(mrow_in.sem, mrow_in.at(i, n + 1))
                q = QK[n % 4]
                for hh in range(4):
                    s = 4 * kt + hh
                    if hh % 2 == 0:
                        pe.wait_ge(exp_ready.sem, exp_ready.at(i, 8 * n + s // 2 - 1))
                    last = nc.tensor.matmul(PS[:, 3 + s % 4, :], lhsT=q[0:SROWS + 1, 1, hh, kt * P:kt * P + P],
                                            rhs=q[0:SROWS + 1, 0, hh, :], start=True, stop=True)
                    if hh % 2 == 1:
                        last.then_inc(sc_ready.sem, 1)

            def values(i, n, kt):
                if kt == 0:
                    pe.wait_ge(va_loaded.sem, va_loaded.at(i, n // 4 + 1))
                    pe.wait_ge(vt_ready.sem, vt_ready.at(i, n))
                pe.wait_ge(exp_ready.sem, exp_ready.at(i, 8 * n + 2 * kt + 2))
                for hh in range(4):
                    last = nc.tensor.matmul(PS[32 * hh:32 * hh + 32, 7, :],
                                            lhsT=VA[n // 4][:, kt, 4 * (n % 4) + hh, :],
                                            rhs=PT[kt % 2][:, hh, :], start=kt == 0, stop=kt == KT - 1,
                                            tile_position=(0, 32 * hh))
                last.then_inc(pv_ready.sem, 1)

            def groups(i, end):
                for n in range(NG):
                    nxt = (i, n + 1) if n + 1 < NG else None if end else (i + 1, 0)
                    for s in range(4):
                        if nxt:
                            max_scores(*nxt, s)
                        scores(i, n, s)
                        if s:
                            values(i, n, s - 1)
                    values(i, n, 3)
                    if nxt:
                        max_row(*nxt)
                        pe.wait_ge(mrow_ready.sem, mrow_ready.at(nxt[0], nxt[1] + 1))
                    pe.wait_ge(vt_ready.sem, vt_ready.at(i, n + 1))
                    for qt in range(KT):
                        last = nc.tensor.transpose(PS[:, 2, qt * P:qt * P + P], VT[:, qt * P:qt * P + P], ident[:, :])
                    last.then_inc(vtt_ready.sem, 1)
                    pe.wait_ge(ctx_ready.sem, ctx_ready.at(i, n + 1))
                    if n % 4 == 3:
                        for h in range(KC):
                            if h:
                                pe.wait_ge(cx_kept.sem, cx_kept.at(i, 2 * (n // 4) + h))
                            for qt in range(KT):
                                last = nc.tensor.transpose(PS[:, 2, qt * P:qt * P + P],
                                                           CTX[:, qt, h * P:h * P + P], ident[:, :])
                            last.then_inc(cx_ready.sem, 1)
                        pe.wait_ge(cx_kept.sem, cx_kept.at(i, 2 * (n // 4) + 2))
                for jj in range(NBLK // 2):
                    if jj:
                        pe.wait_ge(op_added.sem, op_added.at(i, jj))
                    for j in (2 * jj, 2 * jj + 1):
                        for h in range(KC):
                            last = nc.tensor.matmul(PS[:, 2, (j % 2) * C:(j % 2) * C + C],
                                                    lhsT=CTT[:, h, j, :, :].rearrange("p b t -> p (b t)"), rhs=wo1[:, h, :],
                                                    start=h == 0, stop=h == KC - 1)
                    last.then_inc(op_ready.sem, 1)
                pe.wait_ge(op_added.sem, op_added.at(i, 4))
            for hh in range(4):
                max_scores(0, 0, hh)
            max_row(0, 0)
            with pe.Fori(0, NPAIR - 1) as i:
                groups(i, False)
            groups(NPAIR - 1, True)
            with pe.Fori(0, NBLK) as j:
                pe.wait_ge(h2_ready.sem, h2_ready.at(j, 1))
                for h in range(KC):
                    for i in range(NT):
                        last = nc.tensor.transpose(PS[:, h, i * P:i * P + P], XN2[:, i, h * P:h * P + P], ident[:, :])
                last.then_inc(h2_turned.sem, 1)
                pe.wait_ge(ht2_ready.sem, ht2_ready.at(j, 2))
                pe.wait_ge(lg_kept.sem, lg_kept.at(j, 0))
                for i in range(NT):
                    for h in range(KC):
                        last = nc.tensor.matmul(PS[:, 2, i * E1:i * E1 + E1], lhsT=HB2[:, h, i * P:i * P + P],
                                                rhs=wrt[:, h, :], start=h == 0, stop=h == KC - 1)
                last.then_inc(lg_ready.sem, 1)
            pe.wait_ge(exp_loaded, 16 * (E1 + EARLY))
            pe.wait_ge(lg_kept.sem, lg_kept.at(NBLK, 0))

            def hidden(j, u):
                e, n = u // FT, u % FT
                pe.wait_ge(sh_ready.sem, sh_ready.at(j, u - 1))
                if u == FT * (EARLY + 1):
                    pe.wait_ge(up_loaded, 16 * (E1 - EARLY))
                pair = (shg, shu) if e == 0 else (eg_w[:, e - 1, :, :], eu_w[:, e - 1, :, :])
                for g in range(2):
                    for h in range(KC):
                        last = nc.tensor.matmul(PS[:, 2 * (u % 2) + g, :], lhsT=pair[g][:, h, n * P:n * P + P],
                                                rhs=HT2[:, h, bass.ds(j * NT, NT), :].rearrange("p i n -> p (i n)"),
                                                start=h == 0, stop=h == KC - 1)
                last.then_inc(su_ready.sem, 1)

            def down(j, e):
                w = shd if e == 0 else ed_w[:, e - 1, :, :]
                pe.wait_ge(sh_ready.sem, sh_ready.at(j, FT * e + FT))
                if e == 1:
                    pe.wait_ge(down_loaded, 16 * E1)
                pe.wait_ge(sz_added.sem, sz_added.at(j, max(e - 1, 0)))
                for i in range(NT):
                    for r in range(FT):
                        last = nc.tensor.matmul(PS[:, 4 + 2 * (e % 2) + i // 2, (i % 2) * C:(i % 2) * C + C],
                                                lhsT=HS[:, r, i * P:i * P + P], rhs=w[:, r, :],
                                                start=r == 0, stop=r == FT - 1)
                last.then_inc(sz_ready.sem, 1)
            with pe.Fori(0, NBLK) as j:
                for u in range(FT * ALL):
                    hidden(j, u)
                    if u % FT == 0 and u:
                        down(j, u // FT - 1)
                down(j, ALL - 1)

        @block.scalar
        def _(act):
            act.wait_ge(wt_ready, 1)
            act.activation(wT[:, 0:2, :, :], PS[:, 0:2, :].rearrange("p m (h n) -> p m h n", h=KC), ACT.Copy)\
                .then_inc(wt_kept, 1)
            act.wait_ge(loaded, 16 * N_SMALL)
            act.activation(vec0[:, 3, :], vec0[:, 3, :], ACT.Exp).then_inc(wt_kept, 1)
            act.activation(gpar[0:HEADS, 1:2], gpar[0:HEADS, 1:2], ACT.Exp).then_inc(wt_kept, 1)
            act.wait_ge(setup_done, 1)
            asteps = Steps(act, sem("act_step"))

            def ln(j, n, bank, dst):
                act.wait_ge(stats_ready.sem, stats_ready.at(j, n + 1))
                act.activation(sd[:, :], mv[:, :, 1], ACT.Sqrt, bias=eps[:, 0:1]).then_inc(std_ready.sem, 1)
                act.wait_ge(turned.sem, turned.at(j, n + 1))
                for h in range(KC):
                    act.activation(dst(h), PS[:, bank + h, :].rearrange("p (b t) -> p b t", b=B), ACT.Copy)\
                        .then_inc(xT_ready.sem, 1)

            def body(j, rec, blk):
                r = j - 1
                if blk:
                    if rec:
                        act.wait_ge(mixed.sem, mixed.at(j, 0))
                    ln(j, 0, 0, lambda h: XN[:, h, :, 1:TB + 1])
                    act.wait_ge(proj_ready.sem, proj_ready.at(j, 1))
                    act.wait_ge(mixed.sem, mixed.at(j, 3))
                    for h in range(KC):
                        act.activation(DFf[:, h, :], PS[:, 2 + h, :], ACT.Copy).then_inc(k_kept.sem, 1)
                if rec:
                    act.wait_ge(rec_loaded.sem, rec_loaded.at(r, 6))
                    act.activation(SQ, RQ, ACT.Square).then_inc(sq_ready.sem, 1)
                    act.activation(OO[:, :, :], RK, ACT.Square).then_inc(sq_ready.sem, 1)
                if blk:
                    for h in range(KC):
                        act.wait_ge(centred.sem, centred.at(j, h + 1))
                        act.activation(XM[:, 0, h, :], XM[:, 1, h, :], ACT.Square).then_inc(squared.sem, 1)
                    act.wait_ge(var_ready.sem, var_ready.at(j, 1))
                    act.activation(DFf[:, 0, :], PS[:, 1, :], ACT.Sqrt, bias=eps[:, 0:1]).then_inc(ostd_ready.sem, 1)
                if rec:
                    for m in range(2):
                        act.wait_ge(ss_ready.sem, ss_ready.at(r, m + 1))
                        act.activation(RN[:, m, :], RN[:, m, :], ACT.Sqrt, bias=eps[:, 1:2])\
                            .then_inc(rstd_ready.sem, 1)
                if blk:
                    for h in range(KC):
                        act.wait_ge(y_scaled.sem, y_scaled.at(j, h + 1))
                        act.activation(XM[:, 2, h, :], XM[:, 0, h, :], ACT.Identity, bias=vec0[:, 6, h:h + 1])\
                            .then_inc(y_ready.sem, 1)
                    ln(j, 1, 4, lambda h: XF[:, h, :].rearrange("p (b t) -> p b t", b=B))
                    act.wait_ge(logits_ready.sem, logits_ready.at(j, 1))
                    act.activation(LG[:, :, :], PS[:, 6, 0:NT * E0].rearrange("p (i e) -> p i e", i=NT), ACT.Copy)\
                        .then_inc(logits_kept.sem, 1)
                    act.wait_ge(max_ready.sem, max_ready.at(j, 1))
                    for i in range(NT):
                        asteps.mark(act.activation(EX[:, i, :], LG[:, i, :], ACT.Exp, bias=NM[:, i:i + 1],
                                                   accum_out=ZS[:, i:i + 1]))
                    asteps.after(asteps.n)
                    act.activation(E2[:, :], E2[:, :], ACT.Exp).then_inc(exps_ready.sem, 1)

                    def keep_z(k):
                        act.wait_ge(z_ready.sem, z_ready.at(j, k + 1))
                        if k >= 2:
                            act.wait_ge(z_added.sem, z_added.at(j, k - 1))
                        elif k == 0:
                            act.wait_ge(cw_ready.sem, cw_ready.at(j, 1))
                        zb = ZB[k % 2].rearrange("p (i n) -> p i n", i=NT)
                        zp = PS[:, 4 + 2 * (k % 2):6 + 2 * (k % 2), :].rearrange("p s (i n) -> p (s i) n", i=2)
                        if k == 0:
                            act.activation(zb, zp, ACT.Copy).then_inc(z_kept.sem, 1)
                            return
                        for i in range(NT):
                            last = act.activation(zb[:, i, :], zp[:, i, :], ACT.Identity,
                                                  scale=CW[:, i, k - 1:k])
                            if i < NT - 1:
                                asteps.mark(last)
                        last.then_inc(z_kept.sem, 1)

                    for n in range(NU):
                        act.wait_ge(ug_ready.sem, ug_ready.at(j, n + 1))
                        if n >= 2:
                            act.wait_ge(h_ready.sem, h_ready.at(j, n - 1))
                        act.activation(SG[:, n % 2, :], PS[:, 2 * (n % 2) + 1, :], ACT.Silu)\
                            .then_inc(silu_ready.sem, 1)
                        if n >= 3:
                            keep_z(n - 3)
                    keep_z(NJ - 2)
                    keep_z(NJ - 1)
                    ln(j, 2, 6, lambda h: XF[:, h, :].rearrange("p (b t) -> p b t", b=B))
                    act.wait_ge(gates_ready.sem, gates_ready.at(j, 1))
                    if rec:
                        act.wait_ge(stored.sem, stored.at(j, 0))
                    asteps.link(act.activation(GT1[0:HEADS, :], PS[0:HEADS, 6, :], ACT.Abs, bias=gpar[0:HEADS, 0:1]))
                    act.activation(GT1[32:48, :], PS[32:48, 6, :], ACT.Tanh, bias=gpar[32:48, 0:1], scale=0.5)\
                        .then_inc(gates_kept.sem, 1)
                    asteps.link(act.activation(GT1[0:HEADS, :], GT1[0:HEADS, :], ACT.Exp, scale=-1.0))
                    act.activation(GT1[0:HEADS, :], GT1[0:HEADS, :], ACT.Ln, bias=1.0).then_inc(softplus_ready.sem, 1)
                    for m in range(3):
                        act.wait_ge(pre_ready.sem, pre_ready.at(j, m + 1))
                        if rec and m == 0:
                            act.wait_ge(conv_ready.sem, conv_ready.at(j, 0))
                        for h in range(KC):
                            act.activation(PRE[:, m, h, :, TAPS - 1:], PS[:, 2 * m + h, :]
                                           .rearrange("p (b t) -> p b t", b=B), ACT.Copy).then_inc(pre_kept.sem, 1)
                    act.wait_ge(relu_ready.sem, relu_ready.at(j, 1))
                    act.activation(GB[0:HEADS, :], GT1[0:HEADS, :], ACT.Exp, scale=gpar[0:HEADS, 1:2])\
                        .then_inc(decay_ready.sem, 1)
                    act.wait_ge(gproj_ready.sem, gproj_ready.at(j, 1))
                    for h in range(KC):
                        act.activation(GS[:, h, :], PS[:, h, :], ACT.Silu).then_inc(gs_ready.sem, 1)
                if rec:
                    act.wait_ge(o_written.sem, o_written.at(r, 1))
                    act.activation(SQ, OO[:, :, :], ACT.Square).then_inc(sq_ready.sem, 1)
                for m in range(3):
                    for h in range(KC):
                        if blk:
                            act.wait_ge(conv_ready.sem, conv_ready.at(j, 2 * m + h + 1))
                            act.activation(CV[:, m, h, :], CV[:, m, h, :], ACT.Silu).then_inc(cv_ready.sem, 1)
                    if rec and m == 1:
                        act.wait_ge(ss_ready.sem, ss_ready.at(r, 3))
                        act.activation(RN[:, 2, :], RN[:, 2, :], ACT.Sqrt, bias=eps[:, 0:1], scale=1.0 / DH)\
                            .then_inc(rstd_ready.sem, 1)
                asteps.reset()
            passes(act, body)
            with act.Fori(0, NBLK) as j:
                act.wait_ge(xstats_ready.sem, xstats_ready.at(j, 1))
                act.activation(sd[:, :], mv[:, :, 1], ACT.Sqrt, bias=eps[:, 0:1]).then_inc(xstd_ready.sem, 1)
            asteps = Steps(act, a_step)
            act.wait_ge(blocks_done, 1)
            act.wait_ge(d_w_loaded, 16 * N_DW)
            act.wait_ge(d_const, 1)
            with act.Fori(0, NPAIR) as i:
                for j in range(NBLK):
                    asteps.link(act.activation(SQX, X[:, j, bass.ds(i, 1), :].rearrange("p i n -> p (i n)"), ACT.Square,
                                               accum_out=SS1[:, j:j + 1]))
                act.activation(SD1, SS1, ACT.Sqrt, bias=eps[:, 1:2], scale=1.0 / C).then_inc(sstd_ready.sem, 1)
                act.wait_ge(pturn_ready.sem, pturn_ready.at(i, 1))
                for h in range(KC):
                    for jh in range(2):
                        act.activation(HT[:, h, :, jh * C:jh * C + C].rearrange("p b (j t) -> p j b t", t=TB),
                                       PS[:, 2 * h + jh, :].rearrange("p (j b t) -> p j b t", j=4, b=2),
                                       ACT.Identity, scale=n1w[:, h:h + 1]).then_inc(hT_ready.sem, 1)
                for b2 in range(2):
                    act.wait_ge(vproj_ready.sem, vproj_ready.at(i, b2 + 1))
                    act.wait_ge(vo_stored.sem, vo_stored.at(i, b2))
                    act.activation(VO[:, :, :, 0:DH].rearrange("p k h d -> p (k h) d"),
                                   PS[:, 4:6, :].rearrange("p s (k d) -> p (s k) d", d=DH),
                                   ACT.Copy).then_inc(vo_ready.sem, 1)
                    act.wait_ge(st_free.sem, st_free.at(i, b2))
                    for m in range(2):
                        act.wait_ge(qk_ready.sem, qk_ready.at(i, 2 * b2 + m + 1))
                        for h in range(KC):
                            act.activation(SP3[:, m, 0, h, :], PS[:, 2 * m + h, :], ACT.Copy).then_inc(hi_ready.sem, 1)
                    for m in range(2):
                        for h in range(KC):
                            act.wait_ge(r1_ready.sem, r1_ready.at(i, 4 * b2 + 2 * m + h + 1))
                            act.activation(SP3[:, m, 1, h, :], R1[:, m, h, :], ACT.Copy).then_inc(mid_ready.sem, 1)
                asteps.reset()

            def max_row_out(i, n):
                act.wait_ge(mt_ready.sem, mt_ready.at(i, n + 1))
                act.wait_ge(mrow_in.sem, mrow_in.at(i, n))
                act.activation(MROW[0:DH, :], PS[0:DH, 2, 0:P], ACT.Copy, scale=-1.0).then_inc(mrow_ready.sem, 1)

            def groups(i, last):
                for n in range(NG):
                    for kt in range(KT):
                        act.wait_ge(pv_ready.sem, pv_ready.at(i, KT * n + kt - 1))
                        for hp in range(2):
                            act.wait_ge(sc_ready.sem, sc_ready.at(i, 8 * n + 2 * kt + hp + 1))
                            act.activation(PT[kt % 2][:, 2 * hp:2 * hp + 2, :], PS[:, 3 + 2 * hp:5 + 2 * hp, :],
                                           ACT.Exp, scale=DH ** -0.5).then_inc(exp_ready.sem, 1)
                    if n + 1 < NG:
                        max_row_out(i, n + 1)
                    elif not last:
                        max_row_out(i + 1, 0)
                    act.wait_ge(pv_ready.sem, pv_ready.at(i, KT * (n + 1)))
                    act.activation(VT, PS[:, 7, :], ACT.Copy).then_inc(vt_ready.sem, 1)
                    if n % 4 == 3:
                        for h in range(KC):
                            act.wait_ge(cx_ready.sem, cx_ready.at(i, 2 * (n // 4) + h + 1))
                            act.activation(CTT[:, h, :, n // 4, :], PS[:, 2, :].rearrange("p (j t) -> p j t", t=TB),
                                           ACT.Copy).then_inc(cx_kept.sem, 1)
            act.wait_ge(vo_stored.sem, vo_stored.at(NPAIR, 0))
            max_row_out(0, 0)
            with act.Fori(0, NPAIR - 1) as i:
                groups(i, False)
            groups(NPAIR - 1, True)
            act.wait_ge(op_added.sem, op_added.at(NPAIR, 0))
            with act.Fori(0, NBLK) as j:
                for i in range(NT):
                    asteps.link(act.activation(SQ2, X[:, j, i, :], ACT.Square, accum_out=SS2[:, i:i + 1]))
                act.activation(SD2, SS2, ACT.Sqrt, bias=eps[:, 1:2], scale=1.0 / C).then_inc(rstd2_ready.sem, 1)
                act.wait_ge(h2_turned.sem, h2_turned.at(j, 1))
                for h in range(KC):
                    act.activation(HB2[:, h, :], PS[:, h, :], ACT.Copy).then_inc(ht2_ready.sem, 1)
                act.wait_ge(ht2_ready.sem, ht2_ready.at(j, 2))
                apart(act)
                for h in range(KC):
                    last = act.activation(HT2[:, h, bass.ds(j * NT, NT), :],
                                          HB2[:, h, :].rearrange("p (i n) -> p i n", i=NT), ACT.Copy)
                asteps.link(last)
                act.wait_ge(lg_ready.sem, lg_ready.at(j, 1))
                apart(act)
                act.activation(LGT[:, bass.ds(j * NT, NT), :], PS[:, 2, 0:NT * E1].rearrange("p (i e) -> p i e", i=NT),
                               ACT.Copy).then_inc(lg_kept.sem, 1)
                asteps.reset()
            act.wait_ge(route_in, 1)
            act.activation(EX2, EX2, ACT.Exp)
            act.activation(WW[:, 1, :], WW[:, 1, :], ACT.Exp).then_inc(route_exp, 1)
            act.wait_ge(route_in, 2)
            act.activation(WW[:, 1, :], WW[:, 1, :], ACT.Exp).then_inc(route_exp, 1)
            with act.Fori(0, NBLK) as j:
                for u in range(FT * ALL):
                    act.wait_ge(su_ready.sem, su_ready.at(j, u + 1))
                    act.wait_ge(sh_ready.sem, sh_ready.at(j, u - 1))
                    act.activation(SG2[:, u % 2, :], PS[:, 2 * (u % 2), :], ACT.Silu).then_inc(ss_silu.sem, 1)

        @block.vector
        def _(dve):
            steps = Steps(dve, vec_step)
            dve.wait_ge(wt_ready, 2)
            dve.tensor_copy(wT[:, 2:4, :, :], PS[:, 2:4, :].rearrange("p m (h n) -> p m h n", h=KC))\
                .then_inc(wt_kept, 1)
            dve.tensor_copy(wgT[:, :, :], PS[:, 4, 0:KC * E0].rearrange("p (h n) -> p h n", h=KC))\
                .then_inc(wt_kept, 1)
            dve.wait_ge(wt_kept, 5)
            dve.wait_ge(loaded, 16 * N_SMALL)
            steps.mark(dve.tensor_scalar(gpar[0:HEADS, 1:2], gpar[0:HEADS, 1:2], -1.0, None, ALU.mult))
            steps.mark(dve.tensor_scalar(gpar[32:48, 0:1], gpar[32:48, 0:1], 0.5, None, ALU.mult))
            steps.after(steps.n)
            steps.reset()
            dve.wait_ge(x_loaded, 16 * 2 * B)
            dve.sem_inc(setup_done, 1)

            def ln(j, n):
                apart(dve)
                for i in range(NT):
                    steps.mark(dve.bn_stats(stats[:, i, :], X[:, j, i, :]))
                steps.after(steps.n)
                for i in range(NT):
                    last = dve.bn_aggr(mv[:, i, :], stats[:, i, :])
                    if i < NT - 1:
                        steps.mark(last)
                last.then_inc(stats_ready.sem, 1)
                dve.wait_ge(std_ready.sem, std_ready.at(j, n + 1))
                steps.link(dve.reciprocal(rs[:, :], sd[:, :]))
                for i in range(NT):
                    last = dve.tensor_scalar(xn[:, i, :], X[:, j, i, :], mv[:, i, 0:1], rs[:, i:i + 1],
                                             ALU.subtract, ALU.mult)
                    if i < NT - 1:
                        steps.mark(last)
                last.then_inc(norm_ready.sem, 1)

            def recur(j, t0, n):
                for t in range(t0, t0 + n):
                    before, now = HIST[:, (t - 1) % 16, :, :], HIST[:, t % 16, :, :]
                    k = RK[:, :, t].unsqueeze(1).to_broadcast([P, DH, DH])
                    if t % 8 == 0 and t >= 16:
                        dve.wait_ge(hist_used.sem, hist_used.at(j - 1, t // 8 - 1))
                    steps.link(dve.tensor_tensor(PR[:, :, :], before, k, ALU.mult))
                    steps.link(dve.tensor_reduce(PD[:, :], PR[:, :, :], AX.X, ALU.add))
                    steps.link(dve.scalar_tensor_tensor(DL[:, :], in0=PD[:, :], scalar=NBE[:, t:t + 1],
                                                        in1=RV[:, :, t], op0=ALU.mult, op1=ALU.add))
                    steps.link(dve.tensor_tensor(UP[:, :, :], DL[:, :].unsqueeze(2).to_broadcast([P, DH, DH]), k,
                                                 ALU.mult))
                    last = dve.scalar_tensor_tensor(now, in0=before, scalar=EG[:, t:t + 1], in1=UP[:, :, :],
                                                    op0=ALU.mult, op1=ALU.add)
                    if t % 8 == 7:
                        last.then_inc(hist_ready.sem, 1)
                        dve.wait_ge(hist_ready.sem, hist_ready.at(j - 1, t // 8 + 1))
                    else:
                        steps.link(last)

            def body(j, rec, blk):
                if blk:
                    if rec:
                        dve.wait_ge(stored.sem, stored.at(j, 0))
                    ln(j, 0)
                    dve.wait_ge(xT_ready.sem, xT_ready.at(j, 2))
                    steps.link(dve.tensor_tensor(DF, XN[:, :, :, 1:TB + 1], XN[:, :, :, 0:TB], ALU.subtract))
                    for m in range(3):
                        for h in range(KC):
                            last = dve.scalar_tensor_tensor(
                                XM[:, m, h, :].rearrange("p (b t) -> p b t", b=B), in0=DF[:, h, :, :],
                                scalar=vec0[:, m, h:h + 1], in1=XN[:, h, :, 0:TB], op0=ALU.mult, op1=ALU.add)
                            if h == 0:
                                steps.mark(last)
                        if m < 2:
                            last.then_inc(mixed.sem, 1)
                        else:
                            steps.link(last)
                    dve.tensor_copy(XN[:, :, :, 0:1], XN[:, :, :, TB:TB + 1]).then_inc(mixed.sem, 1)
                    dve.wait_ge(k_kept.sem, k_kept.at(j, 2))
                    dve.wait_ge(proj_ready.sem, proj_ready.at(j, 2))
                    for h in range(KC):
                        steps.mark(dve.tensor_tensor(KV[:, h, :], DFf[:, h, :], PS[:, 4 + h, :], ALU.mult))
                    steps.after(steps.n)
                    for h in range(KC):
                        for b in range(B):
                            steps.mark(dve.tensor_tensor_scan(
                                ST[:, h, b * TB:(b + 1) * TB], data0=vec0[:, 3, h:h + 1].to_broadcast([P, TB]),
                                data1=KV[:, h, b * TB:(b + 1) * TB], initial=ST[:, h, (b + 1) * TB - 1:(b + 1) * TB],
                                op0=ALU.mult, op1=ALU.add))
                    steps.after(steps.n)
                    for h in range(KC):
                        steps.mark(dve.scalar_tensor_tensor(KV[:, h, :], in0=KV[:, h, :], scalar=vec0[:, 4, h:h + 1],
                                                            in1=ST[:, h, :], op0=ALU.mult, op1=ALU.add))
                    steps.after(steps.n)
                    dve.wait_ge(proj_ready.sem, proj_ready.at(j, 3))
                    steps.mark(dve.tensor_tensor(KV[:, 0, :], KV[:, 0, :], PS[:, 6, :], ALU.mult))
                    dve.tensor_tensor(KV[:, 1, :], KV[:, 1, :], PS[:, 7, :], ALU.mult).then_inc(o_ready.sem, 1)
                    dve.wait_ge(mu_ready.sem, mu_ready.at(j, 1))
                    for h in range(KC):
                        dve.tensor_tensor(XM[:, 1, h, :], KV[:, h, :], PS[:, 0, :], ALU.subtract)\
                            .then_inc(centred.sem, 1)
                    dve.wait_ge(ostd_ready.sem, ostd_ready.at(j, 1))
                    steps.link(dve.reciprocal(DFf[:, 1, :], DFf[:, 0, :]))
                    for h in range(KC):
                        dve.scalar_tensor_tensor(XM[:, 0, h, :], in0=XM[:, 1, h, :], scalar=vec0[:, 5, h:h + 1],
                                                 in1=DFf[:, 1, :], op0=ALU.mult, op1=ALU.mult)\
                            .then_inc(y_scaled.sem, 1)
                if rec:
                    for m in range(2):
                        dve.wait_ge(rstd_ready.sem, rstd_ready.at(j - 1, m + 1))
                        dve.reciprocal(RN[:, m, :], RN[:, m, :]).then_inc(rnorm_ready.sem, 1)
                if blk:
                    dve.wait_ge(attn0_ready.sem, attn0_ready.at(j, 1))
                    steps.mark(dve.tensor_tensor(X[:, j, 0:2, :], X[:, j, 0:2, :],
                                                 PS[:, 2, :].rearrange("p (i n) -> p i n", i=2), ALU.add))
                    dve.tensor_tensor(X[:, j, 2:4, :], X[:, j, 2:4, :],
                                      PS[:, 3, :].rearrange("p (i n) -> p i n", i=2), ALU.add)\
                        .then_inc(attn0_added.sem, 1)
                    dve.wait_ge(attn0_added.sem, attn0_added.at(j, 1))
                    ln(j, 1)
                    dve.wait_ge(logits_kept.sem, logits_kept.at(j, 1))
                    apart(dve)
                    for i in range(NT):
                        steps.mark(dve.max(MX[:, i, :], LG[:, i, :]))
                    steps.after(steps.n)
                    for i in range(NT):
                        steps.mark(dve.max_index(MI[:, i, :], MX[:, i, :], LG[:, i, :]))
                    steps.mark(dve.tensor_scalar(NM[:, :], MX[:, :, 0], -1.0, None, ALU.mult))
                    dve.tensor_tensor(E2[:, :], MX[:, :, 1], MX[:, :, 0], ALU.subtract).then_inc(max_ready.sem, 1)
                    steps.after(steps.n)
                    steps.mark(dve.tensor_copy(MF[:, :, :], MI[:, :, :]))
                    dve.wait_ge(exps_ready.sem, exps_ready.at(j, 1))
                    steps.link(dve.reciprocal(W12[:, :, 0], ZS[:, :]))
                    steps.link(dve.tensor_tensor(W12[:, :, 1], E2[:, :], W12[:, :, 0], ALU.mult))
                    for i in range(NT):
                        steps.mark(dve.tensor_scalar(CW[:, i, :], iota[:, :], MF[:, i, 0:1], W12[:, i, 0:1],
                                                     ALU.is_equal, ALU.mult))
                        steps.mark(dve.tensor_scalar(CT[:, i, :], iota[:, :], MF[:, i, 1:2], W12[:, i, 1:2],
                                                     ALU.is_equal, ALU.mult))
                    steps.after(steps.n)
                    dve.tensor_tensor(CW[:, :, :], CW[:, :, :], CT[:, :, :], ALU.add).then_inc(cw_ready.sem, 1)
                if rec:
                    dve.wait_ge(rec_ready.sem, rec_ready.at(j - 1, 1))
                for n in range(NU):
                    if blk:
                        dve.wait_ge(silu_ready.sem, silu_ready.at(j, n + 1))
                        if n >= 4:
                            dve.wait_ge(z_ready.sem, z_ready.at(j, n - 3))
                        elif n == 3:
                            dve.wait_ge(z_ready.sem, z_ready.at(j, 1))
                        dve.tensor_tensor(Hh[:, n % 3, :], SG[:, n % 2, :], PS[:, 2 * (n % 2), :], ALU.mult)\
                            .then_inc(h_ready.sem, 1)
                    if rec and 1 <= n <= 16:
                        recur(j, 4 * (n - 1), 4)
                if blk:
                    dve.wait_ge(z_added.sem, z_added.at(j, NJ))
                    ln(j, 2)
                    dve.wait_ge(gates_kept.sem, gates_kept.at(j, 1))
                    steps.mark(dve.tensor_scalar(GB[32:48, :], GT1[32:48, :], 0.5, 0.5, ALU.mult, ALU.add))
                    steps.link(dve.tensor_scalar(GB[0:HEADS, :], PS[0:HEADS, 6, :], gpar[0:HEADS, 0:1], 0.0,
                                                 ALU.add, ALU.max))
                    dve.sem_inc(gates_kept.sem, 1)
                    dve.sem_inc(beta_ready.sem, 1)
                    dve.wait_ge(softplus_ready.sem, softplus_ready.at(j, 1))
                    dve.tensor_tensor(GT1[0:HEADS, :], GT1[0:HEADS, :], GB[0:HEADS, :], ALU.add)\
                        .then_inc(relu_ready.sem, 1)
                for m in range(3):
                    if rec and m == 2:
                        dve.wait_ge(rstd_ready.sem, rstd_ready.at(j - 1, 3))
                        dve.reciprocal(RN[:, 2, :], RN[:, 2, :]).then_inc(rnorm_ready.sem, 1)
                    if blk:
                        for h in range(KC):
                            dve.wait_ge(pre_kept.sem, pre_kept.at(j, 2 * m + h + 1))
                            y = CV[:, m, h, :].rearrange("p (b t) -> p b t", b=B)
                            for tap in range(TAPS):
                                x, w = PRE[:, m, h, :, tap:tap + TB], taps[:, m, h, tap:tap + 1]
                                if tap == 0:
                                    steps.link(dve.tensor_scalar(y, x, w, None, ALU.mult))
                                    continue
                                last = dve.scalar_tensor_tensor(y, in0=x, scalar=w, in1=y, op0=ALU.mult, op1=ALU.add)
                                if tap < TAPS - 1:
                                    steps.link(last)
                            if (m, h) == (2, 1):
                                steps.link(last)
                                dve.tensor_copy(
                                    PRE[:, :, :, :, 0:TAPS - 1].rearrange("p m h b t -> p (m h b) t"),
                                    PRE[:, :, :, :, TB:PADT].rearrange("p m h b t -> p (m h b) t"))\
                                    .then_inc(conv_ready.sem, 1)
                            else:
                                last.then_inc(conv_ready.sem, 1)
                steps.reset()
            passes(dve, body)
            with dve.Fori(0, NBLK) as j:
                dve.wait_ge(og_loaded.sem, og_loaded.at(j, 3))
                for h in range(KC):
                    dve.scalar_tensor_tensor(XM[:, 0, h, :], in0=KV[:, h, :], scalar=gnorm[:, :], in1=XM[:, 1, h, :],
                                             op0=ALU.mult, op1=ALU.mult).then_inc(og_ready.sem, 1)
                dve.wait_ge(attn1_ready.sem, attn1_ready.at(j, 1))
                steps.mark(dve.tensor_tensor(X[:, j, 0:2, :], X[:, j, 0:2, :],
                                             PS[:, 2, :].rearrange("p (i n) -> p i n", i=2), ALU.add))
                dve.tensor_tensor(X[:, j, 2:4, :], X[:, j, 2:4, :],
                                  PS[:, 3, :].rearrange("p (i n) -> p i n", i=2), ALU.add)\
                    .then_inc(attn1_added.sem, 1)
                dve.wait_ge(attn1_added.sem, attn1_added.at(j, 1))
                apart(dve)
                for i in range(NT):
                    last = dve.bn_stats(stats[:, i, :], X[:, j, i, :])
                steps.link(last)
                for i in range(NT):
                    last = dve.bn_aggr(mv[:, i, :], stats[:, i, :])
                last.then_inc(xstats_ready.sem, 1)
                dve.wait_ge(xstd_ready.sem, xstd_ready.at(j, 1))
                steps.link(dve.reciprocal(rs[:, :], sd[:, :]))
                dve.wait_ge(xi_saved.sem, xi_saved.at(j, 1))
                apart(dve)
                for i in range(NT):
                    last = dve.tensor_scalar(X[:, j, i, :], X[:, j, i, :], mv[:, i, 0:1], rs[:, i:i + 1],
                                             ALU.subtract, ALU.mult)
                steps.link(last)
                steps.reset()
            dve.sem_inc(blocks_done, 1)
            dsteps = Steps(dve, d_step)
            with dve.Fori(0, NPAIR) as i:
                dve.wait_ge(sstd_ready.sem, sstd_ready.at(i, 1))
                dve.wait_ge(pturn_ready.sem, pturn_ready.at(i, 0))
                dsteps.link(dve.reciprocal(SD1, SD1))
                for j in range(NBLK):
                    last = dve.tensor_scalar(xnp[:, j, :], X[:, j, bass.ds(i, 1), :].rearrange("p i n -> p (i n)"),
                                             SD1[:, j:j + 1], None, ALU.mult)
                last.then_inc(pn_ready.sem, 1)
                for n in range(8):
                    m, h = (n // 2) % 2, n % 2
                    dve.wait_ge(hi_ready.sem, hi_ready.at(i, n + 1))
                    dve.wait_ge(lo_ready.sem, lo_ready.at(i, n - 3))
                    dve.tensor_tensor(R1[:, m, h, :], PS[:, 2 * m + h, :], SP3[:, m, 0, h, :], ALU.subtract)\
                        .then_inc(r1_ready.sem, 1)
                dsteps.reset()

            def maxima(i, n):
                dve.wait_ge(mt_ready.sem, mt_ready.at(i, n - 1))
                for s in range(16):
                    dve.wait_ge(ms_ready.sem, ms_ready.at(i, 16 * n + s + 1))
                    dve.tensor_reduce(MXS[n % 2][:, s:s + 1], PS[:, s % 2, :], AX.X, ALU.max)\
                        .then_inc(ms_used.sem, 1)

            def groups(i, last):
                for n in range(NG):
                    if n + 1 < NG:
                        maxima(i, n + 1)
                    elif not last:
                        maxima(i + 1, 0)
                    dve.wait_ge(vtt_ready.sem, vtt_ready.at(i, n + 1))
                    v = PS[:, 2, :].rearrange("p (q n) -> p q n", n=32)
                    dsteps.link(dve.reciprocal(RC.unsqueeze(2), v[:, :, DH:DH + 1]))
                    g = 64 * (n % 4)
                    for qt in range(KT):
                        last_op = dve.tensor_tensor(
                            CTX[:, qt, g:g + 64].rearrange("p (h d) -> p h d", h=4),
                            v[:, 4 * qt:4 * qt + 4, 0:DH],
                            RC[:, 4 * qt:4 * qt + 4].unsqueeze(2).to_broadcast([P, 4, DH]), ALU.mult)
                    last_op.then_inc(ctx_ready.sem, 1)
                for jj in range(NBLK // 2):
                    dve.wait_ge(op_ready.sem, op_ready.at(i, jj + 1))
                    x = X[:, 2 * jj:2 * jj + 2, bass.ds(i, 1), :].rearrange("p j i n -> p (j i) n") \
                        if not last else X[:, 2 * jj:2 * jj + 2, i, :]
                    dve.tensor_tensor(x, x, PS[:, 2, :].rearrange("p (j n) -> p j n", j=2), ALU.add)\
                        .then_inc(op_added.sem, 1)
                dsteps.reset()
            maxima(0, 0)
            with dve.Fori(0, NPAIR - 1) as i:
                groups(i, False)
            groups(NPAIR - 1, True)
            dve.wait_ge(op_added.sem, op_added.at(NPAIR, 0))
            with dve.Fori(0, NBLK) as j:
                dve.wait_ge(rstd2_ready.sem, rstd2_ready.at(j, 1))
                dve.wait_ge(h2_turned.sem, h2_turned.at(j, 0))
                dsteps.link(dve.reciprocal(SD2, SD2))
                for i in range(NT):
                    last = dve.scalar_tensor_tensor(XN2[:, i, :], in0=X[:, j, i, :], scalar=SD2[:, i:i + 1], in1=n2b,
                                                    op0=ALU.mult, op1=ALU.mult)
                last.then_inc(h2_ready.sem, 1)
                dve.wait_ge(h2_ready.sem, h2_ready.at(j, 1))
                dve.wait_ge(xi_loaded, 16)
                x = X[:, bass.ds(j, 1), :, :].rearrange("p j i n -> p (j i) n")
                dve.tensor_tensor(x, x, XI[:, bass.ds(j, 1), :, :].rearrange("p j i n -> p (j i) n"), ALU.add)\
                    .then_inc(xi_added, 1)
                dsteps.reset()
            dve.wait_ge(lg_kept.sem, lg_kept.at(NBLK, 0))
            for g in range(NTOK):
                last = dve.max(MX2[:, g, :], LGT[:, g, :])
            dsteps.link(last)
            for g in range(NTOK):
                last = dve.max_index(MI2[:, g, :], MX2[:, g, :], LGT[:, g, :])
            dsteps.mark(last)
            dve.tensor_tensor(EX2, LGT, MX2[:, :, 0:1].to_broadcast([P, NTOK, E1]), ALU.subtract)
            dve.tensor_tensor(WW[:, 1, :], MX2[:, :, 1], MX2[:, :, 0], ALU.subtract).then_inc(route_in, 1)
            dsteps.after(dsteps.n)
            dsteps.link(dve.tensor_copy(MF2, MI2))
            for m in range(2):
                last = dve.tensor_tensor(OH[:, m, :, :], MF2[:, :, m:m + 1].to_broadcast([P, NTOK, E1]),
                                         iota[:, 0:E1].unsqueeze(1).to_broadcast([P, NTOK, E1]), ALU.is_equal)
            dsteps.mark(last)
            dve.wait_ge(route_exp, 1)
            dsteps.link(dve.tensor_reduce(ZZ, EX2, AX.X, ALU.add))
            dsteps.link(dve.reciprocal(ZZ, ZZ))
            dsteps.link(dve.tensor_tensor(WW[:, 1, :], WW[:, 1, :], ZZ, ALU.mult))
            dve.tensor_tensor(WW[:, 1, :], WW[:, 1, :], ZZ, ALU.subtract).then_inc(route_in, 1)
            dve.wait_ge(route_exp, 2)
            dsteps.link(dve.tensor_scalar(WW[:, 0, :], WW[:, 1, :], 1.0, None, ALU.add))
            dsteps.link(dve.reciprocal(WW[:, 0, :], WW[:, 0, :]))
            dsteps.link(dve.tensor_tensor(WW[:, 1, :], WW[:, 1, :], WW[:, 0, :], ALU.mult))
            for m in range(2):
                last = dve.tensor_tensor(OH[:, m, :, :], OH[:, m, :, :],
                                         WW[:, m, :].unsqueeze(2).to_broadcast([P, NTOK, E1]), ALU.mult)
            dsteps.link(last)
            dve.memset(CWB, 1.0)
            dsteps.link(dve.tensor_tensor(CWS, OH[:, 0, :, :], OH[:, 1, :, :], ALU.add))
            dsteps.reset()
            def add(j, e):
                dve.wait_ge(sz_ready.sem, sz_ready.at(j, e + 1))
                dve.wait_ge(sz_added.sem, sz_added.at(j, e))
                for i in range(NT):
                    last = dve.scalar_tensor_tensor(
                        X[:, j, i, :], in0=PS[:, 4 + 2 * (e % 2) + i // 2, (i % 2) * C:(i % 2) * C + C],
                        scalar=CWB[:, i, e:e + 1], in1=X[:, j, i, :], op0=ALU.mult, op1=ALU.add)
                last.then_inc(sz_added.sem, 1)
            with dve.Fori(0, NBLK) as j:
                dve.wait_ge(sz_added.sem, sz_added.at(j, 0))
                apart(dve)
                dsteps.link(dve.tensor_copy(CWB[:, :, 1:ALL], CWS[:, bass.ds(j * NT, NT), :]))
                for u in range(FT * ALL):
                    e, n = u // FT, u % FT
                    dve.wait_ge(ss_silu.sem, ss_silu.at(j, u + 1))
                    dve.wait_ge(sz_ready.sem, sz_ready.at(j, e))
                    dve.tensor_tensor(HS[:, n, :], SG2[:, u % 2, :], PS[:, 2 * (u % 2) + 1, :], ALU.mult)\
                        .then_inc(sh_ready.sem, 1)
                    if n == 0 and e:
                        add(j, e - 1)
                add(j, ALL - 1)
                dsteps.reset()


def kernel(**inputs):
    import numpy as _np
    import concourse.bacc as _bacc
    from concourse import mybir as _mybir
    from concourse.bass_utils import run_bass_kernel_spmd as _run

    nc = _bacc.Bacc("TRN2", target_bir_lowering=False, num_devices=1)
    arrays, aps = {}, {}
    for name, value in inputs.items():
        v = _np.ascontiguousarray(value)
        arrays[name] = v
        aps[name] = nc.dram_tensor(name, v.shape, _mybir.dt.from_np(v.dtype), kind="ExternalInput").ap()
    arrays["rope"] = rope_table()
    aps["rope"] = nc.dram_tensor("rope", arrays["rope"].shape, F32, kind="ExternalInput").ap()
    scratch = {
        "qkv": nc.dram_tensor("qkv", (NBLK, 3, B, C, TB), F32, kind="Internal").ap(),
        "gb": nc.dram_tensor("gb", (NBLK, 2, B, HEADS, TB), F32, kind="Internal").ap(),
        "gate": nc.dram_tensor("gate", (NBLK, P, KC * COLS), F32, kind="Internal").ap(),
        "stack": nc.dram_tensor("stack", (2, B // 2, 2, HEADS // 4, 3, 4 * DH, T), BF16, kind="Internal").ap(),
        "xi": nc.dram_tensor("xi", (NBLK, P, NT * C), F32, kind="Internal").ap(),
        "v": nc.dram_tensor("v", (B // 2, 2, P, T // P * HEADS * 2 * DH), F32, kind="Internal").ap(),
        "o": nc.dram_tensor("o", (NBLK, B, HEADS, DH, TB), F32, kind="Internal").ap(),
    }
    res = nc.dram_tensor("result", (B, T, C), F32, kind="ExternalOutput").ap()
    two_layers(nc, aps, res, scratch)
    r = _run(nc, [arrays], core_ids=[0])
    return r.results[0]["result"]
```

```python
from contextlib import ExitStack

import numpy as np

import concourse.bass as bass
from concourse import mybir

F32 = mybir.dt.float32
BF16 = mybir.dt.bfloat16
U32 = mybir.dt.uint32
ALU = mybir.AluOpType
ACT = mybir.ActivationFunctionType
AX = mybir.AxisListType

P = 128
B, T, C = 8, 512, 256
HEADS, DH = 16, 16
TB = 64
NBLK = T // TB
COLS = B * TB
NT = COLS // P
KC = C // P
E0, H0 = 16, 128
E1, F1 = 8, 512
TAPS = 4
PADT = TB + TAPS - 1


class Tally:

    def __init__(self, sem, per_pass, unit=1, start=1):
        self.sem, self.per, self.unit, self.start = sem, per_pass, unit, start

    def at(self, i, k):
        return i * (self.per * self.unit) + (k * self.unit + self.start)


class Steps:

    def __init__(self, eng, sem):
        self.eng, self.sem, self.n = eng, sem, 0

    def mark(self, instruction):
        instruction.then_inc(self.sem, 1)
        self.n += 1
        return self.n

    def after(self, n):
        self.eng.wait_ge(self.sem, n)

    def link(self, instruction):
        self.after(self.mark(instruction))

    def reset(self):
        if self.n:
            self.after(self.n)
            self.eng.sem_inc(self.sem, -self.n)
            self.n = 0


N_SMALL = 7 + 3 + P // DH + 3
N_W = 2 + (E0 // 4) * (KC + 1) + 5 + 2


OUT_AT = (1, 4, 7, 9, 12)
NZ = 4
N_DW = 10


def rope_table():
    half = DH // 4
    freq = np.float32(10000.0) ** (-np.arange(half, dtype=np.float32) / np.float32(half))
    ang = np.arange(T, dtype=np.float32)[:, None] * freq[None, :].astype(np.float32)
    cos, sin = np.cos(ang).T, np.sin(ang).T
    tab = np.stack([np.concatenate([cos, cos]), np.concatenate([-sin, sin])]).astype(np.float32)
    return np.ascontiguousarray(tab.reshape(2, 2 * half, NBLK, TB).transpose(2, 0, 1, 3).reshape(NBLK, -1))


def two_layers(nc, a, out, scratch):
    ctx = ExitStack()
    with ctx:
        def sb(name, shape, dt=F32):
            return ctx.enter_context(nc.sbuf_tensor(name, shape, dt))

        def sem(name):
            return ctx.enter_context(nc.semaphore(name))

        def tally(name, per, unit=1, start=1):
            return Tally(sem(name), per, unit, start)

        PS = ctx.enter_context(nc.psum_tensor("PS", [P, 8, 512], F32))
        X = sb("X", [P, NBLK, NT, C])
        EXP = sb("EXP", [P, 24576])
        w1 = EXP[:, 0:8192].rearrange("p (e k n) -> p e k n", e=E0, k=KC)
        w2 = EXP[:, 8192:12288].rearrange("p (e n) -> p e n", e=E0)
        WORK = EXP[:, 12288:24576]
        used = [0]

        def work(n):
            used[0] += n
            assert used[0] <= 12288, used
            return WORK[:, used[0] - n:used[0]]

        ident = sb("ident", [P, P])
        mean_mat = sb("mean_mat", [P, P])
        iota = sb("iota", [P, E0])
        eps = sb("eps", [P, 4])
        WA = sb("WA", [P, 6912])
        taken = [0]

        def small(*shape):
            n = int(np.prod(shape))
            taken[0] += n
            assert taken[0] <= 6912
            names = "abcd"[:len(shape)]
            ap = WA[:, taken[0] - n:taken[0]]
            if len(shape) == 1:
                return ap
            return ap.rearrange(f"p ({' '.join(names)}) -> p {' '.join(names)}",
                                **{c: s for c, s in zip(names[:-1], shape[:-1])})

        wT = small(4, KC, C)
        wgT = small(KC, E0)
        ws1 = small(KC, 2 * C)
        ws2 = small(KC, C)
        wp = small(5, KC, C)
        wgb = small(KC, 48)
        zeros = small(C)
        vec0 = sb("vec0", [P, 8, KC])
        taps = sb("taps", [P, 3, KC, TAPS])
        gnorm = sb("gnorm", [P, 1])
        gpar = sb("gpar", [48, 4])
        stats = sb("stats", [P, NT, 6])
        mv = sb("mv", [P, NT, 2])
        sd = sb("sd", [P, NT])
        rs = sb("rs", [P, NT])
        xn = work(NT * C).rearrange("p (i n) -> p i n", i=NT)
        XN = work(KC * B * (TB + 1)).rearrange("p (h b t) -> p h b t", h=KC, b=B)
        DF = work(KC * COLS).rearrange("p (h b t) -> p h b t", h=KC, b=B)
        XMf = work(3 * KC * COLS)
        XM = XMf.rearrange("p (m h n) -> p m h n", m=3, h=KC)
        KV = work(KC * COLS).rearrange("p (h n) -> p h n", h=KC)
        FP = work(8 * DH * DH).rearrange("p (t v d) -> p t v d", t=8, v=DH)
        SQ = FP.rearrange("p t v d -> p (t v d)")[:, 0:DH * TB].rearrange("p (d t) -> p d t", d=DH)
        ROPE = work(2 * 8 * TB).rearrange("p (m d t) -> p m d t", m=2, d=8)
        raw = XMf[:, 0:2048].rearrange("p (m h n) -> p m h n", m=4, h=KC)
        rawg = XMf[:, 2048:2048 + C]
        DFf = DF.rearrange("p h b t -> p h (b t)")
        XF = DFf
        Hh = XMf[:, 0:1536].rearrange("p (r n) -> p r n", r=3)
        SG = XMf[:, 1536:2560].rearrange("p (r n) -> p r n", r=2)
        ZB = [KV.rearrange("p h n -> p (h n)"), xn.rearrange("p i n -> p (i n)")]
        CV = XM
        ST = work(KC * COLS).rearrange("p (h n) -> p h n", h=KC)
        GS = KV
        LG = sb("LG", [P, NT, E0])
        MX = sb("MX", [P, NT, 8])
        MI = sb("MI", [P, NT, 8], U32)
        MF = sb("MF", [P, NT, 8])
        NM = sb("NM", [P, NT])
        ZS = sb("ZS", [P, NT])
        E2 = sb("E2", [P, NT])
        W12 = sb("W12", [P, NT, 2])
        EX = sb("EX", [P, NT, E0])
        CW = sb("CW", [P, NT, E0])
        CT = sb("CT", [P, NT, E0])
        GB, GT1 = ZB[1][0:48, 0:COLS], ZB[1][0:48, COLS:2 * COLS]
        R2 = sb("R2", [P, 12512])
        cut = [0]

        def part(*shape):
            n = int(np.prod(shape))
            cut[0] += n
            assert cut[0] <= 12512, cut
            names = "abcde"[:len(shape)]
            ap = R2[:, cut[0] - n:cut[0]]
            return ap if len(shape) == 1 else ap.rearrange(
                f"p ({' '.join(names)}) -> p {' '.join(names)}", **{c: m for c, m in zip(names[:-1], shape[:-1])})

        PRE = part(3, KC, B, PADT)
        RX = part(3, DH, TB)
        RQ, RK, RV = RX[:, 0, :, :], RX[:, 1, :, :], RX[:, 2, :, :]
        EGB = part(3, TB)
        EG, BT, NBE = EGB[:, 0, :], EGB[:, 1, :], EGB[:, 2, :]
        RN = part(3, TB)
        OO = part(DH, TB)
        HIST = part(16, DH, DH)
        PR = part(DH, DH)
        UP = part(DH, DH)
        PD = sb("PD", [P, DH])
        DL = sb("DL", [P, DH])

        vec_step = sem("vec_step")
        loaded = sem("loaded")
        raw_loaded = sem("raw_loaded")
        x_loaded = sem("x_loaded")
        const_ready = sem("const_ready")
        wt_ready = sem("wt_ready")
        wt_kept = sem("wt_kept")
        setup_done = sem("setup_done")
        out_done = sem("out_done")
        w_loaded = sem("w_loaded")
        tallies = []

        def tl(name, per, unit=1, start=1):
            tallies.append(tally(name, per, unit, start))
            return tallies[-1]

        stats_ready = tl("stats_ready", 3)
        std_ready = tl("std_ready", 3)
        norm_ready = tl("norm_ready", 3)
        turned = tl("turned", 3)
        xT_ready = tl("xT_ready", 6)
        mixed = tl("mixed", 3)
        proj_ready = tl("proj_ready", 3)
        k_kept = tl("k_kept", 2)
        o_ready = tl("o_ready", 1)
        mu_ready = tl("mu_ready", 1)
        centred = tl("centred", 2)
        squared = tl("squared", 2)
        var_ready = tl("var_ready", 1)
        ostd_ready = tl("ostd_ready", 1)
        y_scaled = tl("y_scaled", 2)
        y_ready = tl("y_ready", 2)
        attn0_ready = tl("attn0_ready", 1)
        attn0_added = tl("attn0_added", 1)
        logits_ready = tl("logits_ready", 1)
        logits_kept = tl("logits_kept", 1)
        max_ready = tl("max_ready", 1)
        exps_ready = tl("exps_ready", 1)
        cw_ready = tl("cw_ready", 1)
        NU = 2 + E0
        NJ = 1 + E0
        ug_ready = tl("ug_ready", NU)
        silu_ready = tl("silu_ready", NU)
        h_ready = tl("h_ready", NU)
        z_ready = tl("z_ready", NJ)
        z_kept = tl("z_kept", NJ)
        z_added = tl("z_added", NJ)
        pre_ready = tl("pre_ready", 3)
        pre_kept = tl("pre_kept", 6)
        gates_ready = tl("gates_ready", 1)
        gates_kept = tl("gates_kept", 2)
        relu_ready = tl("relu_ready", 1)
        softplus_ready = tl("softplus_ready", 1)
        decay_ready = tl("decay_ready", 1)
        beta_ready = tl("beta_ready", 1)
        gproj_ready = tl("gproj_ready", 1)
        gs_ready = tl("gs_ready", 2)
        conv_ready = tl("conv_ready", 6)
        cv_ready = tl("cv_ready", 6)
        gb_stored = tl("gb_stored", 2, 16)
        stored = tl("stored", 7, 16)
        rec_loaded = tl("rec_loaded", 6, 16)
        sq_ready = tl("sq_ready", 3)
        ss_ready = tl("ss_ready", 3)
        rstd_ready = tl("rstd_ready", 3)
        rnorm_ready = tl("rnorm_ready", 3)
        rec_ready = tl("rec_ready", 1)
        hist_ready = tl("hist_ready", 8)
        hist_used = tl("hist_used", 8)
        o_written = tl("o_written", 1)
        o_scaled = tl("o_scaled", 1)
        o_stored = tl("o_stored", 1, 16)
        zeroed = sem("zeroed")
        og_loaded = tl("og_loaded", 3, 16)
        og_ready = tl("og_ready", 2)
        attn1_ready = tl("attn1_ready", 1)
        attn1_added = tl("attn1_added", 1)

        qkv_dram = scratch["qkv"]
        gb_dram = scratch["gb"]
        gate_dram = scratch["gate"]
        o_dram = scratch["o"]

        QPOS, KPOS = (0, 1, 0, 2, 0, 1), (0, 0, 1, 0, 2, 1)
        SROWS = len(QPOS) * DH
        NPAIR = B // 2
        KT = T // P
        NG = 2 * (HEADS // 4)
        MAX_TILES = (2, 1, 2, 1) + 2 * (2, 1, 1, 1) + (0, 0, 0, 0)
        NTOK = B * T // P
        FT = F1 // P
        NTILE = 2 * NTOK + E1
        taken[0] = 0
        wqkv, wo1 = small(3, KC, C), small(KC, C)
        wrt = small(KC, E1)
        shg, shu, shd = small(KC, F1), small(KC, F1), small(FT, C)
        n2b = small(C)
        n1w = small(KC)
        LGT = small(NTOK, E1)
        OH = small(2, NTOK, E1)
        IOT = small(NTILE)
        IOG = small(NTOK)
        PI = small(2 * NTOK).bitcast(U32).rearrange("p (m g) -> p m g", m=2)
        TEI = small(NTILE).bitcast(mybir.dt.int32)
        ZZ = small(NTOK)
        WW = small(2, NTOK)
        eg_w = EXP[:, 0:8192].rearrange("p (e k n) -> p e k n", e=E1, k=KC)
        eu_w = EXP[:, 8192:16384].rearrange("p (e k n) -> p e k n", e=E1, k=KC)
        ed_w = EXP[:, 16384:24576].rearrange("p (e k n) -> p e k n", e=E1, k=FT)
        EARLY = 12288 // (KC * F1) - E1
        used[0] = 0
        xnp = work(NBLK * C).rearrange("p (j n) -> p j n", j=NBLK)
        HT = work(KC * 2 * T).rearrange("p (h b n) -> p h b n", h=KC, b=2)
        R1 = work(4 * T).rearrange("p (m h n) -> p m h n", m=2, h=KC)
        SP3 = work(6 * T).bitcast(BF16).rearrange("p (m s h n) -> p m s h n", m=2, s=3, h=KC)
        cut[0] = 0
        VO = part(KT, HEADS, 32)
        MSQ = sb("MSQ", [P, NBLK, NT])
        used[0] = 0
        QK = [work(2048).bitcast(BF16).rearrange("p (m h n) -> p m h n", m=2, h=4) for _ in range(4)]
        VA = [work(2048).rearrange("p (k h n) -> p k h n", k=KT, h=HEADS) for _ in range(2)]
        cut[0] = 0
        PT = [part(4, T) for _ in range(2)]
        CTX = part(KT, C)
        CTT = part(KC, NBLK, 2, TB)
        MXS = [part(DH), part(DH)]
        RC = part(DH)
        VT = part(T)
        MROW = part(P // 2).bitcast(BF16)
        used[0] = cut[0] = 0
        H2 = work(NTOK * C).rearrange("p (g n) -> p g n", g=NTOK)
        TRI = work(P)
        ONE = work(P)
        MM = work(NTOK * E1).rearrange("p (g e) -> p g e", g=NTOK)
        CNT = work(NTOK * E1).rearrange("p (g e) -> p g e", g=NTOK)
        PO = work(NTOK * E1).rearrange("p (g e) -> p g e", g=NTOK)
        SEL = work(2 * NTOK * E1).rearrange("p (m g e) -> p m g e", m=2, g=NTOK)
        CMP = work(NTILE * E1).rearrange("p (t e) -> p t e", t=NTILE)
        CM2 = work(E1 * NTOK).rearrange("p (e g) -> p e g", e=E1)
        TE, ENDS, OFF = work(E1), work(E1), work(E1)
        PF = work(2 * NTOK).rearrange("p (m g) -> p m g", m=2)
        TEF = work(NTILE)
        HT2 = part(KC, NTOK, P)
        HSf = part(FT * COLS)
        SGf = part(2 * COLS)
        HS = HSf.rearrange("p (r n) -> p r n", r=FT)
        SG2 = SGf.rearrange("p (r n) -> p r n", r=2)
        XN2 = HSf[:, 0:NT * C].rearrange("p (i n) -> p i n", i=NT)
        HB2 = HSf[:, NT * C:2 * NT * C].rearrange("p (h n) -> p h n", h=KC)
        SQ2 = SGf[:, 0:C]
        SS2, SD2 = SGf[:, C:C + NTOK], SGf[:, C + NTOK:C + 2 * NTOK]
        MX2 = part(NTOK, 8)
        MF2 = part(NTOK, 8)
        MI2 = part(NTOK * 8).bitcast(U32).rearrange("p (g e) -> p g e", g=NTOK)
        EX2 = part(NTOK, E1)
        cut[0] = 0
        XI = part(NBLK, NT, C)
        XST = [part(KC, P) for _ in range(2)]
        SGT = [part(F1) for _ in range(2)]
        HTK = [part(F1) for _ in range(2)]
        HTT = [part(FT, P) for _ in range(2)]
        XS = [shg[:, 0, 0:C], shg[:, 0, C:2 * C]]
        YS = [shg[:, 1, 0:C], shg[:, 1, C:2 * C]]
        YG = [HTK[0][:, 0:C], HTK[0][:, C:2 * C], HTK[1][:, 0:C], HTK[1][:, C:2 * C]]

        st_dram, v_dram, xi_dram = scratch["stack"], scratch["v"], scratch["xi"]
        xs_dram, ys_dram = scratch["xs"], scratch["ys"]

        d_w_loaded = sem("d_w_loaded")
        exp_loaded = sem("exp_loaded")
        exp2_loaded = sem("exp2_loaded")
        xstats_ready = tl("xstats_ready", 1)
        xstd_ready = tl("xstd_ready", 1)
        xi_saved = tl("xi_saved", 1, 16)
        xi_loaded = sem("xi_loaded")
        d_iota = sem("d_iota")
        blocks_done = sem("blocks_done")
        d_const = sem("d_const")
        route_in = sem("route_in")
        route_exp = sem("route_exp")
        masks_ready = sem("masks_ready")
        ranks_ready = sem("ranks_ready")
        pos_ready = sem("pos_ready")
        scattered = sem("scattered")
        x_final = sem("x_final")
        sstd_ready = sem("sstd_ready")
        pn_ready = tl("pn_ready", 1)
        pturn_ready = tl("pturn_ready", 1)
        hT_ready = tl("hT_ready", 4)
        qk_ready = tl("qk_ready", 4)
        hi_ready = tl("hi_ready", 8)
        r1_ready = tl("r1_ready", 8)
        mid_ready = tl("mid_ready", 8)
        lo_ready = tl("lo_ready", 8, 1, 5)
        vproj_ready = tl("vproj_ready", 2)
        vo_ready = tl("vo_ready", 2)
        st_stored = tl("st_stored", 16, 16)
        st_free = tl("st_free", 2)
        vo_stored = tl("vo_stored", 2, 16)
        qk_loaded = [tl(f"qk_loaded{n}", 24, 16) for n in range(4)]
        va_loaded = tl("va_loaded", 2, 16)
        ms_ready = tl("ms_ready", 16 * NG)
        ms_used = tl("ms_used", 16 * NG, 1, 2)
        mt_ready = tl("mt_ready", NG, 1, 2)
        mrow_ready = tl("mrow_ready", NG)
        mrow_in = tl("mrow_in", NG, 16)
        sc_ready = tl("sc_ready", 8 * NG, 1, 25)
        exp_ready = tl("exp_ready", 8 * NG, 1, 2)
        pv_ready = tl("pv_ready", KT * NG, 1, 17)
        vt_ready = tl("vt_ready", NG)
        vtt_ready = tl("vtt_ready", NG)
        ctx_ready = tl("ctx_ready", NG)
        cx_ready = tl("cx_ready", 4)
        cx_kept = tl("cx_kept", 4)
        op_ready = tl("op_ready", 4)
        op_added = tl("op_added", 4)
        rstd2_ready = sem("rstd2_ready")
        h2_ready = tl("h2_ready", 1)
        h2_kept = tl("h2_kept", 1)
        h2_turned = tl("h2_turned", 1)
        ht2_ready = tl("ht2_ready", 2)
        lg_ready = tl("lg_ready", 1)
        lg_kept = tl("lg_kept", 1)
        su_ready = tl("su_ready", FT)
        ss_silu = tl("ss_silu", FT)
        sh_ready = tl("sh_ready", FT, 1, 2)
        sz_ready = tl("sz_ready", 1)
        sz_added = tl("sz_added", 1)
        xs_loaded = [tl(f"xs_loaded{n}", 1, 16) for n in range(2)]
        xs_turned = tl("xs_turned", 2)
        xst_ready = tl("xst_ready", 2)
        gate_ready = tl("gate_ready", 2)
        gsilu_ready = tl("gsilu_ready", 2)
        up_ready = tl("up_ready", 2)
        hk_ready = tl("hk_ready", 2, 1, 2)
        hk_turned = tl("hk_turned", 2, 1, 2)
        htt_ready = tl("htt_ready", 2, 1, 2)
        y_out = tl("y_out", 2)
        ys_ready = tl("ys_ready", 2, 1, 2)
        ys_stored = [tl(f"ys_stored{n}", 1, 16, 17) for n in range(2)]
        yg_loaded = [sem(f"yg_loaded{n}") for n in range(4)]
        yg_used = sem("yg_used")

        block = ctx.enter_context(nc.Block())

        waited = {}

        def apart(eng):
            if eng not in waited:
                waited[eng] = sem(f"waited{len(waited)}")
            eng.sem_inc(waited[eng], 1)

        def passes(eng, body):
            body(0, False, True)
            with eng.Fori(1, NBLK) as j:
                body(j, True, True)
            body(NBLK, True, False)

        @block.sync
        def _(sp):
            for t in tallies:
                sp.sem_inc(t.sem, t.start)
            for m, name in enumerate(("L0_attn_Wk", "L0_attn_Wv", "L0_attn_Wr", "L0_attn_Wo")):
                sp.dma_start(raw[:, m, :, :], a[name].rearrange("(h p) c -> p h c", p=P)).then_inc(raw_loaded, 16)
            sp.dma_start(rawg[0:E0, :], a["L0_ffn_Wg"]).then_inc(raw_loaded, 16)

            def load(dst, src, landed=loaded):
                sp.dma_start(dst, src, allow_slow_non_contiguous=True).then_inc(landed, 16)
            for n, name in enumerate(("L0_attn_time_mix_k", "L0_attn_time_mix_v", "L0_attn_time_mix_r")):
                load(vec0[:, n, :], a[name].rearrange("a b (h p) -> p (a b h)", p=P))
            for n, name in ((3, "L0_attn_time_decay"), (4, "L0_attn_time_first")):
                load(vec0[:, n, :], a[name].rearrange("(h u) s -> (u s) h", h=KC))
            for n, name in ((5, "L0_attn_ln_g"), (6, "L0_attn_ln_b")):
                load(vec0[:, n, :], a[name].rearrange("(h p) -> p h", p=P))
            for m, name in enumerate(("L1_attn_conv_q_w", "L1_attn_conv_k_w", "L1_attn_conv_v_w")):
                load(taps[:, m, :, :], a[name].rearrange("(h p) k -> p h k", p=P))
            for g in range(P // DH):
                load(gnorm[g * DH:(g + 1) * DH, :], a["L1_attn_gnorm_w"].rearrange("(d a) -> d a", a=1))
            load(gpar[0:HEADS, 0:1], a["L1_attn_dt_bias"].rearrange("(d a) -> d a", a=1))
            load(gpar[32:48, 0:1], a["L1_attn_bb"].rearrange("(d a) -> d a", a=1))
            load(gpar[0:HEADS, 1:2], a["L1_attn_A_log"].rearrange("(d a) -> d a", a=1))
            for j0, j1 in ((0, 1), (1, NBLK)):
                for b in range(B):
                    load(X[TB * (b % 2):TB * (b % 2) + TB, j0:j1, b // 2, :],
                         a["L0_attn_x"][b].rearrange("(j t) c -> t j c", t=TB)[:, j0:j1, :], x_loaded)
            load(ws1, a["L0_ffn_Ws1"].rearrange("(k p) n -> p k n", p=P), w_loaded)
            load(ws2, a["L0_ffn_Ws2"].rearrange("(k p) n -> p k n", p=P), w_loaded)
            for e in range(0, E0, 4):
                for k in range(KC):
                    load(w1[:, e:e + 4, k, :], a["L0_ffn_W1"][e:e + 4, k * P:k * P + P, :].rearrange("e p n -> p e n"),
                         w_loaded)
                load(w2[:, e:e + 4, :], a["L0_ffn_W2"][e:e + 4].rearrange("e p n -> p e n"), w_loaded)
            for m, name in enumerate(("L1_attn_Wq", "L1_attn_Wk", "L1_attn_Wv", "L1_attn_Wg", "L1_attn_Wo")):
                load(wp[:, m, :, :], a[name].rearrange("(k p) n -> p k n", p=P), w_loaded)
            sp.wait_ge(const_ready, 1)
            load(wgb[:, :, 0:HEADS], a["L1_attn_Wgk"].rearrange("(k p) n -> p k n", p=P), w_loaded)
            load(wgb[:, :, 32:48], a["L1_attn_Wb"].rearrange("(k p) n -> p k n", p=P), w_loaded)

            def load_output(j):
                sp.wait_ge(og_ready.sem, og_ready.at(j, 0))
                for h in range(KC):
                    sp.dma_start(KV[:, h, :].rearrange("p (b t) -> p b t", b=B),
                                 o_dram[j, :, h * 8:h * 8 + 8].rearrange("b g v t -> (g v) b t"))\
                        .then_inc(og_loaded.sem, 16)
                sp.dma_start(XM[:, 1, :, :].rearrange("p h n -> p (h n)"), gate_dram[j]).then_inc(og_loaded.sem, 16)

            def save_input(j):
                sp.wait_ge(attn1_added.sem, attn1_added.at(j, 1))
                sp.dma_start(xi_dram[j], X[:, j, :, :].rearrange("p i n -> p (i n)")).then_inc(xi_saved.sem, 16)

            def body(j, rec, blk):
                if not blk:
                    load_output(0)
                    with sp.Fori(0, NBLK - 2) as b:
                        load_output(b + 1)
                        save_input(b)
                    save_input(NBLK - 2)
                if blk:
                    for m in range(2):
                        r = 32 * m
                        sp.wait_ge((decay_ready, beta_ready)[m].sem, (decay_ready, beta_ready)[m].at(j, 1))
                        sp.dma_start(gb_dram[j, m].rearrange("b h t -> h b t"),
                                     GB[r:r + HEADS, :].rearrange("h (b t) -> h b t", b=B)).then_inc(gb_stored.sem, 16)
                    sp.wait_ge(gs_ready.sem, gs_ready.at(j, 2))
                    sp.dma_start(gate_dram[j], GS[:, :, :].rearrange("p h n -> p (h n)")).then_inc(stored.sem, 16)
                    for m in range(3):
                        for h in range(KC):
                            sp.wait_ge(cv_ready.sem, cv_ready.at(j, 2 * m + h + 1))
                            sp.dma_start(qkv_dram[j, m, :, h * P:h * P + P, :].rearrange("b p t -> p b t"),
                                         CV[:, m, h, :].rearrange("p (b t) -> p b t", b=B)).then_inc(stored.sem, 16)
                if rec:
                    sp.wait_ge(o_scaled.sem, o_scaled.at(j - 1, 1))
                    sp.dma_start(o_dram[j - 1].rearrange("b h v t -> (b h) (v t)"),
                                 OO[:, :, :].rearrange("p v t -> p (v t)")).then_inc(o_stored.sem, 16)
                if blk:
                    sp.wait_ge(gb_stored.sem, gb_stored.at(j, 2))
                    sp.wait_ge(stored.sem, stored.at(j, 7))
                    if rec:
                        sp.wait_ge(o_stored.sem, o_stored.at(j - 1, 1))
                    for m in range(3):
                        sp.dma_start(RX[:, m, :, :].rearrange("p d t -> p (d t)"),
                                     qkv_dram[j, m].rearrange("b (h d) t -> (b h) (d t)", d=DH))\
                            .then_inc(rec_loaded.sem, 16)
                    for m in range(2):
                        sp.dma_start(EGB[:, m, :], gb_dram[j, m].rearrange("b h t -> (b h) t"))\
                            .then_inc(rec_loaded.sem, 16)
                    sp.dma_start(ROPE.rearrange("p m d t -> p (m d t)"), a["rope"][j].partition_broadcast(P))\
                        .then_inc(rec_loaded.sem, 16)
                if not rec:
                    for z in range(NZ):
                        n = NTILE // NZ
                        sp.dma_start(xs_dram[z * n:z * n + n].rearrange("t p n -> p t n"),
                                     zeros.unsqueeze(1).to_broadcast([P, n, C])).then_inc(zeroed, 16)
            passes(sp, body)
            sp.wait_ge(o_stored.sem, o_stored.at(NBLK - 1, 1))
            load_output(NBLK - 1)
            save_input(NBLK - 1)

            sp.wait_ge(blocks_done, 1)
            for m, name in enumerate(("L1_ffn_wq", "L1_ffn_wk", "L1_ffn_wv")):
                load(wqkv[:, m, :, :], a[name].rearrange("(k p) n -> p k n", p=P), d_w_loaded)
            load(n1w, a["L1_ffn_norm1_w"].rearrange("(h p) -> p h", p=P), d_w_loaded)
            load(wo1, a["L1_ffn_wo"].rearrange("(k p) n -> p k n", p=P), d_w_loaded)
            load(wrt, a["L1_ffn_router_w"].rearrange("(k p) n -> p k n", p=P), d_w_loaded)
            load(shg, a["L1_ffn_sh_gate"].rearrange("(k p) n -> p k n", p=P), d_w_loaded)
            load(shu, a["L1_ffn_sh_up"].rearrange("(k p) n -> p k n", p=P), d_w_loaded)
            load(shd, a["L1_ffn_sh_down"].rearrange("(k p) n -> p k n", p=P), d_w_loaded)
            load(n2b, a["L1_ffn_norm2_w"].partition_broadcast(P), d_w_loaded)
            for e in range(E1):
                load(eg_w[:, e, :, :], a["L1_ffn_e_gate"][e].rearrange("(k p) n -> p k n", p=P), exp_loaded)
            for e in range(EARLY):
                load(eu_w[:, e, :, :], a["L1_ffn_e_up"][e].rearrange("(k p) n -> p k n", p=P), exp_loaded)
            with sp.Fori(0, NPAIR) as i:
                for b2 in range(2):
                    sp.wait_ge(vo_ready.sem, vo_ready.at(i, b2 + 1))
                    sp.dma_start(v_dram[i, b2], VO.rearrange("p k h n -> p (k h n)")).then_inc(vo_stored.sem, 16)
                    for m in range(2):
                        for h in range(KC):
                            sp.wait_ge(lo_ready.sem, lo_ready.at(i, 4 * b2 + 2 * m + h + 1))
                            for g2 in range(2):
                                sp.dma_start(st_dram[m, i, b2, 2 * h + g2].rearrange("s p n -> p s n"),
                                             SP3[64 * g2:64 * g2 + 64, m, :, h, :]).then_inc(st_stored.sem, 16)
                    sp.wait_ge(st_stored.sem, st_stored.at(i, 8 * b2 + 8))
                    sp.sem_inc(st_free.sem, 1)
            sp.wait_ge(vo_stored.sem, vo_stored.at(NPAIR, 0))

            def load_qk(i, n):
                sp.wait_ge(sc_ready.sem, sc_ready.at(i, 8 * (n - 3)))
                for m, pos in enumerate((QPOS, KPOS)):
                    for r, s in enumerate(pos):
                        sp.dma_start(QK[n % 4][DH * r:DH * r + DH, m, :, :],
                                     st_dram[m, i, n // 4, n % 4, s].rearrange("(h d) n -> d h n", d=DH))\
                            .then_inc(qk_loaded[n % 4].sem, 16)

            def load_values(i, b2):
                sp.wait_ge(pv_ready.sem, pv_ready.at(i, 4 * KT * (b2 - 1)))
                sp.dma_start(VA[b2].rearrange("p k h n -> p (k h n)"), v_dram[i, b2]).then_inc(va_loaded.sem, 16)

            def groups(i, last):
                for n in range(NG):
                    sp.wait_ge(mrow_ready.sem, mrow_ready.at(i, n + 1))
                    sp.dma_start(QK[n % 4][SROWS:SROWS + 1, 0, :, :], MROW[0:DH, :]).then_inc(mrow_in.sem, 16)
                    if n == 1:
                        load_values(i, 1)
                    if n == 5 and not last:
                        load_values(i + 1, 0)
                    if n + 3 < NG:
                        load_qk(i, n + 3)
                    elif not last:
                        load_qk(i + 1, n + 3 - NG)
            load_values(0, 0)
            for n in range(3):
                load_qk(0, n)
            with sp.Fori(0, NPAIR - 1) as i:
                groups(i, False)
            groups(NPAIR - 1, True)
            sp.wait_ge(scattered, 16 * 2 * NTOK)
            for e in range(EARLY, E1):
                load(eu_w[:, e, :, :], a["L1_ffn_e_up"][e].rearrange("(k p) n -> p k n", p=P), exp2_loaded)
            for e in range(E1):
                load(ed_w[:, e, :, :], a["L1_ffn_e_down"][e].rearrange("(k p) n -> p k n", p=P), exp2_loaded)

            def rows_in(q, k, first=False):
                if not first:
                    sp.wait_ge(xs_turned.sem, xs_turned.at(q, k - 1))
                sp.dma_start(XS[k % 2], xs_dram[2 * q + k]).then_inc(xs_loaded[k % 2].sem, 16)

            def rows_out(q, k):
                sp.wait_ge(ys_ready.sem, ys_ready.at(q, k + 1))
                sp.dma_start(ys_dram[2 * q + k], YS[k % 2]).then_inc(ys_stored[k % 2].sem, 16)
            sp.wait_ge(sz_added.sem, sz_added.at(NBLK, 0))
            rows_in(0, 0, True)
            rows_in(0, 1, True)
            sp.wait_ge(xi_saved.sem, xi_saved.at(NBLK, 0))
            sp.dma_start(XI.rearrange("p j i n -> p j (i n)"), xi_dram.rearrange("j p n -> p j n"))\
                .then_inc(xi_loaded, 16)
            rows_in(0, 2)
            with sp.Fori(0, NTILE // 2 - 2) as q:
                for u in range(2):
                    rows_in(q, u + 3)
                    rows_out(q, u)
            last = NTILE // 2 - 2
            rows_in(last, 3)
            for k in range(4):
                rows_out(last, k)
            rows = out.rearrange("(i b) t c -> b t i c", b=2)
            for j in range(NBLK):
                sp.wait_ge(x_final, j + 1)
                for b2 in range(2):
                    sp.dma_start(rows[b2, j * TB:j * TB + TB, :, :], X[TB * b2:TB * b2 + TB, j, :, :])\
                        .then_inc(out_done, 16)
            sp.wait_ge(out_done, 16 * 2 * NBLK)

        @block.gpsimd
        def _(pool):
            steps = Steps(pool, sem("pool_step"))
            steps.link(pool.memset(ident[:, :], 0.0))
            steps.link(pool.affine_select(out=ident[:, :], in_=ident[:, :], compare_op=ALU.not_equal, fill=1.0,
                                          base=0, pattern=[[-1, P]], channel_multiplier=1))
            steps.reset()
            pool.memset(mean_mat[:, :], 1.0 / C)
            pool.memset(eps[:, 0:1], 1e-5)
            pool.memset(eps[:, 1:2], 1e-6)
            pool.memset(XN, 0.0)
            pool.memset(wgb, 0.0)
            pool.memset(zeros, 0.0)
            pool.memset(ST, 0.0)
            pool.memset(PRE[:, :, :, :, :], 0.0)
            pool.memset(HIST[:, 15, :, :], 0.0)
            pool.iota(iota[:, :], pattern=[[1, E0]], base=0, channel_multiplier=0,
                      allow_small_or_imprecise_dtypes=True).then_inc(const_ready, 1)

            def fold(x, n):
                while n > 1:
                    n //= 2
                    steps.link(pool.tensor_tensor(x[:, 0:n, :], x[:, 0:n, :], x[:, n:2 * n, :], ALU.add))

            def body(j, rec, blk):
                if rec:
                    r = j - 1
                    for m in range(2):
                        pool.wait_ge(sq_ready.sem, sq_ready.at(r, m + 1))
                        src = (SQ, OO)[m]
                        n = DH // 2
                        while n > 1:
                            steps.link(pool.tensor_tensor(src[:, 0:n, :], src[:, 0:n, :], src[:, n:2 * n, :], ALU.add))
                            n //= 2
                        pool.tensor_tensor(RN[:, m, :], src[:, 0, :], src[:, 1, :], ALU.add)\
                            .then_inc(ss_ready.sem, 1)
                    for m in range(2):
                        pool.wait_ge(rnorm_ready.sem, rnorm_ready.at(r, m + 1))
                        x = RX[:, m, :, :]
                        steps.link(pool.tensor_tensor(x, x, RN[:, m, :].unsqueeze(1).to_broadcast([P, DH, TB]),
                                                      ALU.mult))
                        steps.mark(pool.tensor_tensor(SQ[:, 0:8, :], x[:, 0:8, :], ROPE[:, 0, :, :], ALU.mult))
                        steps.mark(pool.tensor_tensor(SQ[:, 8:12, :], x[:, 4:8, :], ROPE[:, 1, 0:4, :], ALU.mult))
                        steps.link(pool.tensor_tensor(SQ[:, 12:16, :], x[:, 0:4, :], ROPE[:, 1, 4:8, :], ALU.mult))
                        steps.link(pool.tensor_tensor(x[:, 0:8, :], SQ[:, 0:8, :], SQ[:, 8:16, :], ALU.add))
                    steps.mark(pool.tensor_tensor(RV, RV, BT.unsqueeze(1).to_broadcast([P, DH, TB]), ALU.mult))
                    steps.link(pool.tensor_tensor(NBE, BT, EG, ALU.mult))
                    pool.tensor_scalar(NBE, NBE, -1.0, None, ALU.mult).then_inc(rec_ready.sem, 1)

                def add_z(k):
                    pool.wait_ge(z_kept.sem, z_kept.at(j, k + 1))
                    if k:
                        pool.wait_ge(z_added.sem, z_added.at(j, k))
                    x = X[:, j, :, :]
                    apart(pool)
                    pool.tensor_tensor(x, x, ZB[k % 2].rearrange("p (i n) -> p i n", i=NT), ALU.add)\
                        .then_inc(z_added.sem, 1)

                def outputs(g):
                    pool.wait_ge(hist_ready.sem, hist_ready.at(j - 1, g + 1))
                    q = RQ[:, :, 8 * g:8 * g + 8].rearrange("p d t -> p t d").unsqueeze(2)\
                        .to_broadcast([P, 8, DH, DH])
                    if steps.n:
                        steps.after(steps.n)
                    pool.tensor_tensor(FP, HIST[:, 8 * (g % 2):8 * (g % 2) + 8, :, :], q, ALU.mult)\
                        .then_inc(hist_used.sem, 1)
                    pool.wait_ge(hist_used.sem, hist_used.at(j - 1, g + 1))
                    n = DH // 2
                    while n > 1:
                        steps.link(pool.tensor_tensor(FP[:, :, :, 0:n], FP[:, :, :, 0:n], FP[:, :, :, n:2 * n],
                                                      ALU.add))
                        n //= 2
                    steps.mark(pool.tensor_tensor(OO[:, :, 8 * g:8 * g + 8].rearrange("p v t -> p t v"),
                                                  FP[:, :, :, 0], FP[:, :, :, 1], ALU.add))

                for n in range(NU):
                    if rec and n in OUT_AT:
                        outputs(OUT_AT.index(n))
                    if blk and n >= 1:
                        add_z(n - 1)
                if rec:
                    r = j - 1
                    for g in range(len(OUT_AT), TB // 8):
                        outputs(g)
                    steps.after(steps.n)
                    pool.sem_inc(o_written.sem, 1)
                    pool.wait_ge(sq_ready.sem, sq_ready.at(r, 3))
                    n = DH // 2
                    while n > 1:
                        steps.link(pool.tensor_tensor(SQ[:, 0:n, :], SQ[:, 0:n, :], SQ[:, n:2 * n, :], ALU.add))
                        n //= 2
                    pool.tensor_tensor(RN[:, 2, :], SQ[:, 0, :], SQ[:, 1, :], ALU.add).then_inc(ss_ready.sem, 1)
                    pool.wait_ge(rnorm_ready.sem, rnorm_ready.at(r, 3))
                    pool.tensor_tensor(OO[:, :, :], OO[:, :, :], RN[:, 2, :].unsqueeze(1).to_broadcast([P, DH, TB]),
                                       ALU.mult).then_inc(o_scaled.sem, 1)
                steps.reset()
            passes(pool, body)
            pool.wait_ge(blocks_done, 1)
            pool.memset(VO, 1.0).then_inc(d_const, 1)
            pool.iota(IOT, pattern=[[1, NTILE]], base=0, channel_multiplier=0, allow_small_or_imprecise_dtypes=True)
            pool.iota(IOG, pattern=[[P, NTOK]], base=0, channel_multiplier=0, allow_small_or_imprecise_dtypes=True)\
                .then_inc(d_iota, 1)
            with pool.Fori(0, NPAIR) as i:
                for n in range(8):
                    m, h = (n // 2) % 2, n % 2
                    pool.wait_ge(mid_ready.sem, mid_ready.at(i, n + 1))
                    pool.tensor_tensor(SP3[:, m, 2, h, :], R1[:, m, h, :], SP3[:, m, 1, h, :], ALU.subtract)\
                        .then_inc(lo_ready.sem, 1)
            pool.wait_ge(st_stored.sem, st_stored.at(NPAIR, 0))
            for q in QK:
                pool.memset(q[SROWS:SROWS + 1, 1, :, :], 1.0).then_inc(d_const, 1)
            pool.wait_ge(op_added.sem, op_added.at(NPAIR, 0))
            pool.memset(ONE, 1.0)
            pool.memset(TRI, 1.0).then_inc(d_iota, 1)
            pool.wait_ge(d_iota, 2)
            pool.affine_select(out=TRI, in_=TRI, compare_op=ALU.is_gt, fill=0.0, base=0,
                               pattern=[[1, P]], channel_multiplier=-1).then_inc(d_iota, 1)
            pool.wait_ge(pos_ready, 1)
            pool.wait_ge(zeroed, 16 * NZ)
            for g in range(NTOK):
                for m in range(2):
                    pool.indirect_dma_start(
                        out=xs_dram.rearrange("t p n -> (t p) n"),
                        out_offset=bass.IndirectOffsetOnAxis(ap=PI[:, m, g:g + 1], axis=0),
                        in_=H2[:, g, :], in_offset=None).then_inc(scattered, 16)
            for b in range(2):
                pool.wait_ge(ys_stored[b].sem, ys_stored[b].at(NTILE // 2, 0))
            for g in range(NTOK):
                for m in range(2):
                    n = 2 * g + m
                    if n >= 4:
                        pool.wait_ge(yg_used, n - 3)
                    pool.indirect_dma_start(
                        out=YG[n % 4], out_offset=None, in_=ys_dram.rearrange("t p n -> (t p) n"),
                        in_offset=bass.IndirectOffsetOnAxis(ap=PI[:, m, g:g + 1], axis=0))\
                        .then_inc(yg_loaded[n % 4], 16)

        @block.tensor
        def _(pe):
            pe.wait_ge(const_ready, 1)
            pe.wait_ge(raw_loaded, 80)
            for m in range(4):
                for h in range(KC):
                    for r in range(KC):
                        last = nc.tensor.transpose(PS[:, m, h * C + r * P:h * C + r * P + P],
                                                   raw[:, m, r, h * P:h * P + P], ident[:, :])
            last.then_inc(wt_ready, 1)
            for h in range(KC):
                last = nc.tensor.transpose(PS[:, 4, h * E0:h * E0 + E0], rawg[0:E0, h * P:h * P + P],
                                           ident[0:E0, 0:E0])
            last.then_inc(wt_ready, 1)
            pe.wait_ge(setup_done, 1)

            def turn(j, n, bank):
                pe.wait_ge(norm_ready.sem, norm_ready.at(j, n + 1))
                for h in range(KC):
                    for i in range(NT):
                        last = nc.tensor.transpose(PS[:, bank + h, i * P:i * P + P], xn[:, i, h * P:h * P + P],
                                                   ident[:, :])
                last.then_inc(turned.sem, 1)

            def project(bank, w, x, n=C):
                for d in range(KC):
                    for h in range(KC):
                        last = nc.tensor.matmul(PS[:, bank + d, :], lhsT=w[:, h, d * P:d * P + P],
                                                rhs=x[:, h, :], start=h == 0, stop=h == KC - 1)
                return last

            def body(j, rec, blk):
                if not blk:
                    return
                if rec:
                    pe.wait_ge(gs_ready.sem, gs_ready.at(j, 0))
                turn(j, 0, 0)
                if rec:
                    pe.wait_ge(pre_kept.sem, pre_kept.at(j, 0))
                    pe.wait_ge(gates_kept.sem, gates_kept.at(j, 0))
                for m in range(3):
                    pe.wait_ge(mixed.sem, mixed.at(j, m + 1))
                    project(2 + 2 * m, wT[:, m, :, :], XM[:, m, :, :]).then_inc(proj_ready.sem, 1)
                pe.wait_ge(o_ready.sem, o_ready.at(j, 1))
                for h in range(KC):
                    last = nc.tensor.matmul(PS[:, 0, :], lhsT=mean_mat[:, :], rhs=KV[:, h, :],
                                            start=h == 0, stop=h == KC - 1)
                last.then_inc(mu_ready.sem, 1)
                pe.wait_ge(squared.sem, squared.at(j, 2))
                for h in range(KC):
                    last = nc.tensor.matmul(PS[:, 1, :], lhsT=mean_mat[:, :], rhs=XM[:, 0, h, :],
                                            start=h == 0, stop=h == KC - 1)
                last.then_inc(var_ready.sem, 1)
                pe.wait_ge(y_ready.sem, y_ready.at(j, 2))
                for i in range(NT):
                    for h in range(KC):
                        last = nc.tensor.matmul(PS[:, 2 + i // 2, (i % 2) * C:(i % 2) * C + C],
                                                lhsT=XM[:, 2, h, i * P:i * P + P], rhs=wT[:, 3, h, :],
                                                start=h == 0, stop=h == KC - 1)
                last.then_inc(attn0_ready.sem, 1)
                turn(j, 1, 4)
                pe.wait_ge(xT_ready.sem, xT_ready.at(j, 4))
                for i in range(NT):
                    for h in range(KC):
                        last = nc.tensor.matmul(PS[:, 6, i * E0:i * E0 + E0], lhsT=XF[:, h, i * P:i * P + P],
                                                rhs=wgT[:, h, :], start=h == 0, stop=h == KC - 1)
                last.then_inc(logits_ready.sem, 1)
                if not rec:
                    pe.wait_ge(w_loaded, 16 * N_W)

                def ug(n):
                    if n >= 2:
                        pe.wait_ge(h_ready.sem, h_ready.at(j, n - 1))
                    for g in range(2):
                        for h in range(KC):
                            w = ws1[:, h, g * C + n * P:g * C + n * P + P] if n < 2 else \
                                w1[:, n - 2, h, g * P:g * P + P]
                            last = nc.tensor.matmul(PS[:, 2 * (n % 2) + g, :], lhsT=w, rhs=XF[:, h, :],
                                                    start=h == 0, stop=h == KC - 1)
                    last.then_inc(ug_ready.sem, 1)

                def z(k):
                    pe.wait_ge(h_ready.sem, h_ready.at(j, k + 2))
                    if k >= 2:
                        pe.wait_ge(z_kept.sem, z_kept.at(j, k - 1))
                    elif k == 1:
                        pe.wait_ge(logits_kept.sem, logits_kept.at(j, 1))
                    tiles = ((0, ws2[:, 0, :]), (1, ws2[:, 1, :])) if k == 0 else (((k + 1) % 3, w2[:, k - 1, :]),)
                    for i in range(NT):
                        for r, w in tiles:
                            last = nc.tensor.matmul(PS[:, 4 + 2 * (k % 2) + i // 2, (i % 2) * C:(i % 2) * C + C],
                                                    lhsT=Hh[:, r, i * P:i * P + P], rhs=w,
                                                    start=r == tiles[0][0], stop=r == tiles[-1][0])
                    last.then_inc(z_ready.sem, 1)

                for n in range(NU):
                    ug(n)
                    if n >= 2:
                        z(n - 2)
                z(NJ - 1)
                turn(j, 2, 6)
                pe.wait_ge(xT_ready.sem, xT_ready.at(j, 6))
                for m in range(3):
                    project(2 * m, wp[:, m, :, :], XF).then_inc(pre_ready.sem, 1)
                for h in range(KC):
                    last = nc.tensor.matmul(PS[0:48, 6, :], lhsT=wgb[:, h, :], rhs=XF[:, h, :], start=h == 0,
                                            stop=h == KC - 1)
                last.then_inc(gates_ready.sem, 1)
                pe.wait_ge(pre_kept.sem, pre_kept.at(j, 2))
                project(0, wp[:, 3, :, :], XF).then_inc(gproj_ready.sem, 1)
            passes(pe, body)
            with pe.Fori(0, NBLK) as j:
                pe.wait_ge(og_ready.sem, og_ready.at(j, 2))
                for i in range(NT):
                    for h in range(KC):
                        last = nc.tensor.matmul(PS[:, 2 + i // 2, (i % 2) * C:(i % 2) * C + C],
                                                lhsT=XM[:, 0, h, i * P:i * P + P], rhs=wp[:, 4, h, :],
                                                start=h == 0, stop=h == KC - 1)
                last.then_inc(attn1_ready.sem, 1)
            pe.wait_ge(d_w_loaded, 16 * N_DW)
            with pe.Fori(0, NPAIR) as i:
                pe.wait_ge(pn_ready.sem, pn_ready.at(i, 1))
                for h in range(KC):
                    for j in range(NBLK):
                        last = nc.tensor.transpose(PS[:, 2 * h + j // 4, (j % 4) * P:(j % 4) * P + P],
                                                   xnp[:, j, h * P:h * P + P], ident[:, :])
                last.then_inc(pturn_ready.sem, 1)
                pe.wait_ge(hT_ready.sem, hT_ready.at(i, 4))
                for b2 in range(2):
                    pe.wait_ge(vo_ready.sem, vo_ready.at(i, b2))
                    for kt in range(KT):
                        for h in range(KC):
                            last = nc.tensor.matmul(PS[:, 4 + kt // 2, (kt % 2) * C:(kt % 2) * C + C],
                                                    lhsT=HT[:, h, b2, kt * P:kt * P + P], rhs=wqkv[:, 2, h, :],
                                                    start=h == 0, stop=h == KC - 1)
                    last.then_inc(vproj_ready.sem, 1)
                    for m in range(2):
                        if b2:
                            pe.wait_ge(r1_ready.sem, r1_ready.at(i, 2 * m + 2))
                        project(2 * m, wqkv[:, m, :, :], HT[:, :, b2, :]).then_inc(qk_ready.sem, 1)
                pe.wait_ge(r1_ready.sem, r1_ready.at(i, 8))
            pe.wait_ge(d_const, 5)
            pe.wait_ge(vo_ready.sem, vo_ready.at(NPAIR, 0))

            def max_scores(i, n, s):
                if s == 0:
                    pe.wait_ge(qk_loaded[n % 4].sem, qk_loaded[n % 4].at(i, 12 * (n // 4 + 1)))
                q, hh, qt = QK[n % 4], s // KT, s % KT
                pe.wait_ge(ms_used.sem, ms_used.at(i, 16 * n + s - 1))
                nc.tensor.matmul(PS[:, s % 2, :], lhsT=q[0:SROWS, 0, hh, qt * P:qt * P + P],
                                 rhs=q[0:SROWS, 1, hh, :], start=True, stop=True).then_inc(ms_ready.sem, 1)

            def max_row(i, n):
                pe.wait_ge(ms_used.sem, ms_used.at(i, 16 * (n + 1)))
                nc.tensor.transpose(PS[0:DH, 2, 0:P], MXS[n % 2], ident[:, :]).then_inc(mt_ready.sem, 1)

            def scores(i, n, kt, hp):
                if kt == hp == 0:
                    pe.wait_ge(mrow_in.sem, mrow_in.at(i, n + 1))
                    pe.wait_ge(op_added.sem, op_added.at(i, 0))
                q = QK[n % 4]
                pe.wait_ge(exp_ready.sem, exp_ready.at(i, 8 * n + 2 * kt + hp - 1))
                for hh in (2 * hp, 2 * hp + 1):
                    last = nc.tensor.matmul(PS[:, 3 + hh, :], lhsT=q[0:SROWS + 1, 1, hh, kt * P:kt * P + P],
                                            rhs=q[0:SROWS + 1, 0, hh, :], start=True, stop=True)
                last.then_inc(sc_ready.sem, 1)

            def values(i, n, kt, hp):
                if hp == 0:
                    if kt == 0:
                        pe.wait_ge(va_loaded.sem, va_loaded.at(i, n // 4 + 1))
                        pe.wait_ge(vt_ready.sem, vt_ready.at(i, n))
                    pe.wait_ge(exp_ready.sem, exp_ready.at(i, 8 * n + 2 * kt + 2))
                for hh in (2 * hp, 2 * hp + 1):
                    last = nc.tensor.matmul(PS[32 * hh:32 * hh + 32, 7, :],
                                            lhsT=VA[n // 4][:, kt, 4 * (n % 4) + hh, :],
                                            rhs=PT[kt % 2][:, hh, :], start=kt == 0, stop=kt == KT - 1,
                                            tile_position=(0, 32 * hh))
                if hp == 1:
                    last.then_inc(pv_ready.sem, 1)

            def finish(i, n, row_out):
                if row_out:
                    pe.wait_ge(mrow_ready.sem, mrow_ready.at(*row_out))
                pe.wait_ge(vt_ready.sem, vt_ready.at(i, n + 1))
                pe.wait_ge(ctx_ready.sem, ctx_ready.at(i, n))
                for qt in range(KT):
                    last = nc.tensor.transpose(PS[:, 2, qt * P:qt * P + P], VT[:, qt * P:qt * P + P], ident[:, :])
                last.then_inc(vtt_ready.sem, 1)
                if n % 4 == 3:
                    for h in range(KC):
                        pe.wait_ge(ctx_ready.sem, ctx_ready.at(i, n + 1))
                        pe.wait_ge(cx_kept.sem, cx_kept.at(i, 2 * (n // 4) + h))
                        for qt in range(KT):
                            last = nc.tensor.transpose(PS[:, 2, qt * P:qt * P + P],
                                                       CTX[:, qt, h * P:h * P + P], ident[:, :])
                        last.then_inc(cx_ready.sem, 1)

            def groups(i, end):
                for n in range(NG):
                    nxt = (i, n + 1) if n + 1 < NG else None if end else (i + 1, 0)
                    tile = 0
                    for s in range(KT):
                        for quarter in range(4):
                            for _ in range(MAX_TILES[4 * s + quarter]):
                                if nxt:
                                    max_scores(*nxt, tile)
                                tile += 1
                            if quarter % 2 == 0:
                                scores(i, n, s, quarter // 2)
                            elif s:
                                values(i, n, s - 1, quarter // 2)
                            elif n:
                                values(i, n - 1, KT - 1, quarter // 2)
                            if s == KT - 1 and quarter == 0 and nxt:
                                pe.wait_ge(ctx_ready.sem, ctx_ready.at(i, n))
                                pe.wait_ge(cx_kept.sem, cx_kept.at(i, 2 * (n // 4)))
                                max_row(*nxt)
                        if s == 1 and n:
                            finish(i, n - 1, (i, n + 1))
                for hp in range(2):
                    values(i, NG - 1, KT - 1, hp)
                finish(i, NG - 1, None if end else (i + 1, 1))
                pe.wait_ge(cx_kept.sem, cx_kept.at(i, 4))
                for jj in range(NBLK // 2):
                    for j in (2 * jj, 2 * jj + 1):
                        for h in range(KC):
                            last = nc.tensor.matmul(PS[:, 3 + jj, (j % 2) * C:(j % 2) * C + C],
                                                    lhsT=CTT[:, h, j, :, :].rearrange("p b t -> p (b t)"),
                                                    rhs=wo1[:, h, :],
                                                    start=h == 0, stop=h == KC - 1)
                    last.then_inc(op_ready.sem, 1)
            for s in range(16):
                max_scores(0, 0, s)
            max_row(0, 0)
            with pe.Fori(0, NPAIR - 1) as i:
                groups(i, False)
            groups(NPAIR - 1, True)
            pe.wait_ge(op_added.sem, op_added.at(NPAIR, 0))
            with pe.Fori(0, NBLK) as j:
                pe.wait_ge(h2_ready.sem, h2_ready.at(j, 1))
                for h in range(KC):
                    for i in range(NT):
                        last = nc.tensor.transpose(PS[:, h, i * P:i * P + P], XN2[:, i, h * P:h * P + P], ident[:, :])
                last.then_inc(h2_turned.sem, 1)
                pe.wait_ge(ht2_ready.sem, ht2_ready.at(j, 2))
                pe.wait_ge(lg_kept.sem, lg_kept.at(j, 0))
                for i in range(NT):
                    for h in range(KC):
                        last = nc.tensor.matmul(PS[:, 2, i * E1:i * E1 + E1], lhsT=HB2[:, h, i * P:i * P + P],
                                                rhs=wrt[:, h, :], start=h == 0, stop=h == KC - 1)
                last.then_inc(lg_ready.sem, 1)
            pe.wait_ge(d_iota, 3)
            pe.wait_ge(masks_ready, 1)
            for bank, w in ((0, TRI), (1, ONE)):
                last = nc.tensor.matmul(PS[:, bank, 0:NTOK * E1], lhsT=w, rhs=MM.rearrange("p g e -> p (g e)"),
                                        start=True, stop=True)
            last.then_inc(ranks_ready, 1)
            pe.wait_ge(pos_ready, 1)
            with pe.Fori(0, NBLK) as j:
                for n in range(FT):
                    pe.wait_ge(sh_ready.sem, sh_ready.at(j, n - 1))
                    for g, w in ((0, shg), (1, shu)):
                        for h in range(KC):
                            last = nc.tensor.matmul(PS[:, 2 * (n % 2) + g, :], lhsT=w[:, h, n * P:n * P + P],
                                                    rhs=HT2[:, h, bass.ds(j * NT, NT), :].rearrange("p i n -> p (i n)"),
                                                    start=h == 0, stop=h == KC - 1)
                    last.then_inc(su_ready.sem, 1)
                pe.wait_ge(sh_ready.sem, sh_ready.at(j, FT))
                pe.wait_ge(sz_added.sem, sz_added.at(j, 0))
                for i in range(NT):
                    for r in range(FT):
                        last = nc.tensor.matmul(PS[:, 4 + i // 2, (i % 2) * C:(i % 2) * C + C],
                                                lhsT=HS[:, r, i * P:i * P + P], rhs=shd[:, r, :],
                                                start=r == 0, stop=r == FT - 1)
                last.then_inc(sz_ready.sem, 1)
            pe.wait_ge(exp_loaded, 16 * (E1 + EARLY))
            pe.wait_ge(exp2_loaded, 16 * (2 * E1 - EARLY))
            pe.wait_ge(sz_added.sem, sz_added.at(NBLK, 0))

            def expert_of(q, u):
                return pe.value_load(TEI[0:1, bass.ds(2 * q + u, 1)], min_val=0, max_val=E1 - 1)

            def turn_rows(q, u):
                b = u % 2
                pe.wait_ge(xs_loaded[b].sem, xs_loaded[b].at(q, u // 2 + 1))
                for h in range(KC):
                    last = nc.tensor.transpose(PS[:, b, h * P:h * P + P], XS[b][:, h * P:h * P + P], ident[:, :])
                last.then_inc(xs_turned.sem, 1)

            def hidden(u, w, bank, e, done):
                for h in range(KC):
                    last = nc.tensor.matmul(PS[:, bank, :], lhsT=XST[u][:, h, :],
                                            rhs=w[:, bass.ds(e, 1), h, :].rearrange("p e n -> p (e n)"),
                                            start=h == 0, stop=h == KC - 1)
                last.then_inc(done.sem, 1)

            def turn_hidden(q, u):
                pe.wait_ge(hk_ready.sem, hk_ready.at(q, u))
                pe.wait_ge(htt_ready.sem, htt_ready.at(q, u - 1))
                for r in range(FT):
                    last = nc.tensor.transpose(PS[:, 6, r * P:r * P + P], HTK[1 - u][:, r * P:r * P + P], ident[:, :])
                last.then_inc(hk_turned.sem, 1)

            def down(q, u):
                e = expert_of(q, u - 1)
                pe.wait_ge(htt_ready.sem, htt_ready.at(q, u))
                pe.wait_ge(ys_ready.sem, ys_ready.at(q, u - 1))
                for r in range(FT):
                    last = nc.tensor.matmul(PS[:, 7, 0:C], lhsT=HTT[1 - u][:, r, :],
                                            rhs=ed_w[:, bass.ds(e, 1), r, :].rearrange("p e n -> p (e n)"),
                                            start=r == 0, stop=r == FT - 1)
                last.then_inc(y_out.sem, 1)

            def tile(q, u, first=False, final=False):
                e = expert_of(q, u)
                if not final:
                    turn_rows(q, u + 1)
                pe.wait_ge(xst_ready.sem, xst_ready.at(q, u + 1))
                pe.wait_ge(hk_ready.sem, hk_ready.at(q, u - 1))
                hidden(u, eg_w, 2 + 2 * u, e, gate_ready)
                if not first:
                    turn_hidden(q, u)
                hidden(u, eu_w, 3 + 2 * u, e, up_ready)
                if not first:
                    down(q, u)
            turn_rows(0, 0)
            tile(0, 0, first=True)
            tile(0, 1)
            with pe.Fori(1, NTILE // 2 - 1) as q:
                tile(q, 0)
                tile(q, 1)
            tile(NTILE // 2 - 1, 0)
            tile(NTILE // 2 - 1, 1, final=True)
            turn_hidden(NTILE // 2, 0)
            down(NTILE // 2, 0)

        @block.scalar
        def _(act):
            act.wait_ge(wt_ready, 1)
            act.activation(wT[:, 0:2, :, :], PS[:, 0:2, :].rearrange("p m (h n) -> p m h n", h=KC), ACT.Copy)\
                .then_inc(wt_kept, 1)
            act.wait_ge(loaded, 16 * N_SMALL)
            act.activation(vec0[:, 3, :], vec0[:, 3, :], ACT.Exp).then_inc(wt_kept, 1)
            act.activation(gpar[0:HEADS, 1:2], gpar[0:HEADS, 1:2], ACT.Exp).then_inc(wt_kept, 1)
            act.wait_ge(setup_done, 1)
            asteps = Steps(act, sem("act_step"))

            def ln(j, n, bank, dst):
                act.wait_ge(stats_ready.sem, stats_ready.at(j, n + 1))
                act.activation(sd[:, :], mv[:, :, 1], ACT.Sqrt, bias=eps[:, 0:1]).then_inc(std_ready.sem, 1)
                act.wait_ge(turned.sem, turned.at(j, n + 1))
                for h in range(KC):
                    act.activation(dst(h), PS[:, bank + h, :].rearrange("p (b t) -> p b t", b=B), ACT.Copy)\
                        .then_inc(xT_ready.sem, 1)

            def input_std(j):
                act.wait_ge(xstats_ready.sem, xstats_ready.at(j, 1))
                act.activation(sd[:, :], mv[:, :, 1], ACT.Sqrt, bias=eps[:, 0:1]).then_inc(xstd_ready.sem, 1)

            def body(j, rec, blk):
                r = j - 1
                if blk:
                    if rec:
                        act.wait_ge(mixed.sem, mixed.at(j, 0))
                    ln(j, 0, 0, lambda h: XN[:, h, :, 1:TB + 1])
                if rec:
                    act.wait_ge(rec_loaded.sem, rec_loaded.at(r, 6))
                    act.activation(SQ, RQ, ACT.Square).then_inc(sq_ready.sem, 1)
                    act.activation(OO[:, :, :], RK, ACT.Square).then_inc(sq_ready.sem, 1)
                if blk:
                    act.wait_ge(proj_ready.sem, proj_ready.at(j, 1))
                    act.wait_ge(mixed.sem, mixed.at(j, 3))
                    for h in range(KC):
                        act.activation(DFf[:, h, :], PS[:, 2 + h, :], ACT.Copy).then_inc(k_kept.sem, 1)
                if rec:
                    for m in range(2):
                        act.wait_ge(ss_ready.sem, ss_ready.at(r, m + 1))
                        act.activation(RN[:, m, :], RN[:, m, :], ACT.Sqrt, bias=eps[:, 1:2])\
                            .then_inc(rstd_ready.sem, 1)
                if blk:
                    for h in range(KC):
                        act.wait_ge(centred.sem, centred.at(j, h + 1))
                        act.activation(XM[:, 0, h, :], XM[:, 1, h, :], ACT.Square).then_inc(squared.sem, 1)
                    act.wait_ge(var_ready.sem, var_ready.at(j, 1))
                    act.activation(DFf[:, 0, :], PS[:, 1, :], ACT.Sqrt, bias=eps[:, 0:1]).then_inc(ostd_ready.sem, 1)
                    for h in range(KC):
                        act.wait_ge(y_scaled.sem, y_scaled.at(j, h + 1))
                        act.activation(XM[:, 2, h, :], XM[:, 0, h, :], ACT.Identity, bias=vec0[:, 6, h:h + 1])\
                            .then_inc(y_ready.sem, 1)
                    ln(j, 1, 4, lambda h: XF[:, h, :].rearrange("p (b t) -> p b t", b=B))
                    act.wait_ge(logits_ready.sem, logits_ready.at(j, 1))
                    act.activation(LG[:, :, :], PS[:, 6, 0:NT * E0].rearrange("p (i e) -> p i e", i=NT), ACT.Copy)\
                        .then_inc(logits_kept.sem, 1)
                    act.wait_ge(max_ready.sem, max_ready.at(j, 1))
                    for i in range(NT):
                        asteps.mark(act.activation(EX[:, i, :], LG[:, i, :], ACT.Exp, bias=NM[:, i:i + 1],
                                                   accum_out=ZS[:, i:i + 1]))
                    asteps.after(asteps.n)
                    act.activation(E2[:, :], E2[:, :], ACT.Exp).then_inc(exps_ready.sem, 1)

                    def keep_z(k):
                        act.wait_ge(z_ready.sem, z_ready.at(j, k + 1))
                        if k >= 2:
                            act.wait_ge(z_added.sem, z_added.at(j, k - 1))
                        elif k == 0:
                            act.wait_ge(cw_ready.sem, cw_ready.at(j, 1))
                        zb = ZB[k % 2].rearrange("p (i n) -> p i n", i=NT)
                        zp = PS[:, 4 + 2 * (k % 2):6 + 2 * (k % 2), :].rearrange("p s (i n) -> p (s i) n", i=2)
                        if k == 0:
                            act.activation(zb, zp, ACT.Copy).then_inc(z_kept.sem, 1)
                            return
                        for i in range(NT):
                            last = act.activation(zb[:, i, :], zp[:, i, :], ACT.Identity,
                                                  scale=CW[:, i, k - 1:k])
                            if i < NT - 1:
                                asteps.mark(last)
                        last.then_inc(z_kept.sem, 1)

                    for n in range(NU):
                        act.wait_ge(ug_ready.sem, ug_ready.at(j, n + 1))
                        if n >= 2:
                            act.wait_ge(h_ready.sem, h_ready.at(j, n - 1))
                        act.activation(SG[:, n % 2, :], PS[:, 2 * (n % 2) + 1, :], ACT.Silu)\
                            .then_inc(silu_ready.sem, 1)
                        if n >= 3:
                            keep_z(n - 3)
                    keep_z(NJ - 2)
                    keep_z(NJ - 1)
                    ln(j, 2, 6, lambda h: XF[:, h, :].rearrange("p (b t) -> p b t", b=B))
                    act.wait_ge(gates_ready.sem, gates_ready.at(j, 1))
                    if rec:
                        act.wait_ge(gb_stored.sem, gb_stored.at(j, 0))
                    asteps.link(act.activation(GT1[0:HEADS, :], PS[0:HEADS, 6, :], ACT.Abs, bias=gpar[0:HEADS, 0:1]))
                    act.activation(GT1[32:48, :], PS[32:48, 6, :], ACT.Tanh, bias=gpar[32:48, 0:1], scale=0.5)\
                        .then_inc(gates_kept.sem, 1)
                    asteps.link(act.activation(GT1[0:HEADS, :], GT1[0:HEADS, :], ACT.Exp, scale=-1.0))
                    act.activation(GT1[0:HEADS, :], GT1[0:HEADS, :], ACT.Ln, bias=1.0).then_inc(softplus_ready.sem, 1)
                    for m in range(3):
                        act.wait_ge(pre_ready.sem, pre_ready.at(j, m + 1))
                        if rec and m == 0:
                            act.wait_ge(conv_ready.sem, conv_ready.at(j, 0))
                        for h in range(KC):
                            act.activation(PRE[:, m, h, :, TAPS - 1:], PS[:, 2 * m + h, :]
                                           .rearrange("p (b t) -> p b t", b=B), ACT.Copy).then_inc(pre_kept.sem, 1)
                    act.wait_ge(relu_ready.sem, relu_ready.at(j, 1))
                    act.activation(GB[0:HEADS, :], GT1[0:HEADS, :], ACT.Exp, scale=gpar[0:HEADS, 1:2])\
                        .then_inc(decay_ready.sem, 1)
                    act.wait_ge(gproj_ready.sem, gproj_ready.at(j, 1))
                    for h in range(KC):
                        act.activation(GS[:, h, :], PS[:, h, :], ACT.Silu).then_inc(gs_ready.sem, 1)
                if not blk:
                    with act.Fori(0, NBLK - 1) as b:
                        input_std(b)
                if rec:
                    act.wait_ge(o_written.sem, o_written.at(r, 1))
                    act.activation(SQ, OO[:, :, :], ACT.Square).then_inc(sq_ready.sem, 1)
                for m in range(3):
                    for h in range(KC):
                        if blk:
                            act.wait_ge(conv_ready.sem, conv_ready.at(j, 2 * m + h + 1))
                            act.activation(CV[:, m, h, :], CV[:, m, h, :], ACT.Silu).then_inc(cv_ready.sem, 1)
                    if rec and m == 1:
                        act.wait_ge(ss_ready.sem, ss_ready.at(r, 3))
                        act.activation(RN[:, 2, :], RN[:, 2, :], ACT.Sqrt, bias=eps[:, 0:1], scale=1.0 / DH)\
                            .then_inc(rstd_ready.sem, 1)
                asteps.reset()
            passes(act, body)
            input_std(NBLK - 1)
            act.wait_ge(blocks_done, 1)
            act.activation(MSQ[:, :, :], MSQ[:, :, :], ACT.Sqrt, bias=eps[:, 1:2]).then_inc(sstd_ready, 1)
            act.wait_ge(d_w_loaded, 16 * N_DW)
            act.wait_ge(d_const, 1)
            with act.Fori(0, NPAIR) as i:
                act.wait_ge(pturn_ready.sem, pturn_ready.at(i, 1))
                for h in range(KC):
                    for jh in range(2):
                        act.activation(HT[:, h, :, jh * C:jh * C + C].rearrange("p b (j t) -> p j b t", t=TB),
                                       PS[:, 2 * h + jh, :].rearrange("p (j b t) -> p j b t", j=4, b=2),
                                       ACT.Identity, scale=n1w[:, h:h + 1]).then_inc(hT_ready.sem, 1)
                for b2 in range(2):
                    act.wait_ge(vproj_ready.sem, vproj_ready.at(i, b2 + 1))
                    act.wait_ge(vo_stored.sem, vo_stored.at(i, b2))
                    act.activation(VO[:, :, :, 0:DH].rearrange("p k h d -> p (k h) d"),
                                   PS[:, 4:6, :].rearrange("p s (k d) -> p (s k) d", d=DH),
                                   ACT.Copy).then_inc(vo_ready.sem, 1)
                    act.wait_ge(st_free.sem, st_free.at(i, b2))
                    for m in range(2):
                        act.wait_ge(qk_ready.sem, qk_ready.at(i, 2 * b2 + m + 1))
                        for h in range(KC):
                            act.activation(SP3[:, m, 0, h, :], PS[:, 2 * m + h, :], ACT.Copy).then_inc(hi_ready.sem, 1)
                    for m in range(2):
                        for h in range(KC):
                            act.wait_ge(r1_ready.sem, r1_ready.at(i, 4 * b2 + 2 * m + h + 1))
                            act.activation(SP3[:, m, 1, h, :], R1[:, m, h, :], ACT.Copy).then_inc(mid_ready.sem, 1)

            def max_row_out(i, n):
                act.wait_ge(mt_ready.sem, mt_ready.at(i, n + 1))
                act.wait_ge(mrow_in.sem, mrow_in.at(i, n))
                act.activation(MROW[0:DH, :], PS[0:DH, 2, 0:P], ACT.Copy, scale=-1.0).then_inc(mrow_ready.sem, 1)

            def batch_out(i, b2):
                for h in range(KC):
                    act.wait_ge(cx_ready.sem, cx_ready.at(i, 2 * b2 + h + 1))
                    act.activation(CTT[:, h, :, b2, :], PS[:, 2, :].rearrange("p (j t) -> p j t", t=TB),
                                   ACT.Copy).then_inc(cx_kept.sem, 1)

            def values_out(i, n):
                act.wait_ge(pv_ready.sem, pv_ready.at(i, KT * (n + 1)))
                act.wait_ge(vtt_ready.sem, vtt_ready.at(i, n))
                act.activation(VT, PS[:, 7, :], ACT.Copy).then_inc(vt_ready.sem, 1)

            def groups(i, last):
                for n in range(NG):
                    for kt in range(KT):
                        act.wait_ge(pv_ready.sem, pv_ready.at(i, KT * n + kt - 1))
                        for hp in range(2):
                            act.wait_ge(sc_ready.sem, sc_ready.at(i, 8 * n + 2 * kt + hp + 1))
                            act.activation(PT[kt % 2][:, 2 * hp:2 * hp + 2, :], PS[:, 3 + 2 * hp:5 + 2 * hp, :],
                                           ACT.Exp, scale=DH ** -0.5).then_inc(exp_ready.sem, 1)
                            if kt == KT - 1 and hp == 0:
                                if n + 1 < NG:
                                    max_row_out(i, n + 1)
                                elif not last:
                                    max_row_out(i + 1, 0)
                        if kt == 0 and n:
                            values_out(i, n - 1)
                        if kt == 1 and n == 4:
                            batch_out(i, 0)
                values_out(i, NG - 1)
                batch_out(i, 1)
            act.wait_ge(vo_stored.sem, vo_stored.at(NPAIR, 0))
            max_row_out(0, 0)
            with act.Fori(0, NPAIR - 1) as i:
                groups(i, False)
            groups(NPAIR - 1, True)
            act.wait_ge(op_added.sem, op_added.at(NPAIR, 0))
            for g in range(NTOK):
                asteps.link(act.activation(SQ2, X[:, g // NT, g % NT, :], ACT.Square, accum_out=SS2[:, g:g + 1]))
            act.activation(SD2, SS2, ACT.Sqrt, bias=eps[:, 1:2], scale=1.0 / C).then_inc(rstd2_ready, 1)
            asteps.reset()
            with act.Fori(0, NBLK) as j:
                act.wait_ge(h2_ready.sem, h2_ready.at(j, 1))
                apart(act)
                act.activation(H2[:, bass.ds(j * NT, NT), :], XN2, ACT.Copy).then_inc(h2_kept.sem, 1)
                act.wait_ge(h2_turned.sem, h2_turned.at(j, 1))
                for h in range(KC):
                    act.activation(HB2[:, h, :], PS[:, h, :], ACT.Copy).then_inc(ht2_ready.sem, 1)
                act.wait_ge(ht2_ready.sem, ht2_ready.at(j, 2))
                apart(act)
                for h in range(KC):
                    last = act.activation(HT2[:, h, bass.ds(j * NT, NT), :],
                                          HB2[:, h, :].rearrange("p (i n) -> p i n", i=NT), ACT.Copy)
                asteps.link(last)
                act.wait_ge(lg_ready.sem, lg_ready.at(j, 1))
                apart(act)
                act.activation(LGT[:, bass.ds(j * NT, NT), :], PS[:, 2, 0:NT * E1].rearrange("p (i e) -> p i e", i=NT),
                               ACT.Copy).then_inc(lg_kept.sem, 1)
                asteps.reset()
            act.wait_ge(route_in, 1)
            act.activation(EX2, EX2, ACT.Exp)
            act.activation(WW[:, 1, :], WW[:, 1, :], ACT.Exp).then_inc(route_exp, 1)
            act.wait_ge(route_in, 2)
            act.activation(WW[:, 1, :], WW[:, 1, :], ACT.Exp).then_inc(route_exp, 1)
            with act.Fori(0, NBLK) as j:
                for n in range(FT):
                    act.wait_ge(su_ready.sem, su_ready.at(j, n + 1))
                    act.wait_ge(sh_ready.sem, sh_ready.at(j, n - 1))
                    act.activation(SG2[:, n % 2, :], PS[:, 2 * (n % 2), :], ACT.Silu).then_inc(ss_silu.sem, 1)
            act.wait_ge(sz_added.sem, sz_added.at(NBLK, 0))

            def rows_kept(q, u):
                b = u % 2
                act.wait_ge(xs_turned.sem, xs_turned.at(q, u + 1))
                act.activation(XST[b], PS[:, b, 0:C].rearrange("p (h n) -> p h n", h=KC), ACT.Copy)\
                    .then_inc(xst_ready.sem, 1)

            def before_out(q, u):
                act.wait_ge(hk_turned.sem, hk_turned.at(q, u))
                act.activation(HTT[1 - u], PS[:, 6, :].rearrange("p (r n) -> p r n", r=FT), ACT.Copy)\
                    .then_inc(htt_ready.sem, 1)
                act.wait_ge(y_out.sem, y_out.at(q, u))
                stored_to = ys_stored[1 - u]
                act.wait_ge(stored_to.sem, stored_to.at(q, u - 1))
                act.activation(YS[1 - u], PS[:, 7, 0:C], ACT.Copy).then_inc(ys_ready.sem, 1)

            def tile(q, u, first=False, final=False):
                if not final:
                    rows_kept(q, u + 1)
                act.wait_ge(gate_ready.sem, gate_ready.at(q, u + 1))
                act.wait_ge(hk_ready.sem, hk_ready.at(q, u - 1))
                act.activation(SGT[u], PS[:, 2 + 2 * u, :], ACT.Silu).then_inc(gsilu_ready.sem, 1)
                if not first:
                    before_out(q, u)
            rows_kept(0, 0)
            tile(0, 0, first=True)
            tile(0, 1)
            with act.Fori(1, NTILE // 2 - 1) as q:
                tile(q, 0)
                tile(q, 1)
            tile(NTILE // 2 - 1, 0)
            tile(NTILE // 2 - 1, 1, final=True)
            before_out(NTILE // 2, 0)

        @block.vector
        def _(dve):
            steps = Steps(dve, vec_step)
            dve.wait_ge(wt_ready, 2)
            dve.tensor_copy(wT[:, 2:4, :, :], PS[:, 2:4, :].rearrange("p m (h n) -> p m h n", h=KC))\
                .then_inc(wt_kept, 1)
            dve.tensor_copy(wgT[:, :, :], PS[:, 4, 0:KC * E0].rearrange("p (h n) -> p h n", h=KC))\
                .then_inc(wt_kept, 1)
            dve.wait_ge(wt_kept, 5)
            dve.wait_ge(loaded, 16 * N_SMALL)
            steps.mark(dve.tensor_scalar(gpar[0:HEADS, 1:2], gpar[0:HEADS, 1:2], -1.0, None, ALU.mult))
            steps.mark(dve.tensor_scalar(gpar[32:48, 0:1], gpar[32:48, 0:1], 0.5, None, ALU.mult))
            steps.after(steps.n)
            steps.reset()
            dve.wait_ge(x_loaded, 16 * 2 * B)
            dve.sem_inc(setup_done, 1)

            def ln(j, n):
                apart(dve)
                for i in range(NT):
                    steps.mark(dve.bn_stats(stats[:, i, :], X[:, j, i, :]))
                steps.after(steps.n)
                for i in range(NT):
                    last = dve.bn_aggr(mv[:, i, :], stats[:, i, :])
                    if i < NT - 1:
                        steps.mark(last)
                last.then_inc(stats_ready.sem, 1)
                dve.wait_ge(std_ready.sem, std_ready.at(j, n + 1))
                steps.link(dve.reciprocal(rs[:, :], sd[:, :]))
                dve.wait_ge(gb_stored.sem, gb_stored.at(j, 0))
                for i in range(NT):
                    last = dve.tensor_scalar(xn[:, i, :], X[:, j, i, :], mv[:, i, 0:1], rs[:, i:i + 1],
                                             ALU.subtract, ALU.mult)
                    if i < NT - 1:
                        steps.mark(last)
                last.then_inc(norm_ready.sem, 1)

            turn = [0, 0]

            def recur(j, t0, n):
                for t in range(t0, t0 + n):
                    if t % 8 == 0 and t >= 16:
                        dve.wait_ge(hist_used.sem, hist_used.at(j - 1, t // 8 - 1))
                    k = RK[:, :, t].unsqueeze(1).to_broadcast([P, DH // 2, DH])
                    for stage in range(5):
                        for half in range(2):
                            v = slice(half * (DH // 2), (half + 1) * (DH // 2))
                            before, now = HIST[:, (t - 1) % 16, v, :], HIST[:, t % 16, v, :]
                            if stage == 0 and half == 1 and t % 8 == 0 and t:
                                dve.wait_ge(hist_ready.sem, hist_ready.at(j - 1, t // 8))
                            elif stage or t:
                                steps.after(turn[half])
                            if stage == 0:
                                op = dve.tensor_tensor(PR[:, v, :], before, k, ALU.mult)
                            elif stage == 1:
                                op = dve.tensor_reduce(PD[:, v], PR[:, v, :], AX.X, ALU.add)
                            elif stage == 2:
                                op = dve.scalar_tensor_tensor(DL[:, v], in0=PD[:, v], scalar=NBE[:, t:t + 1],
                                                              in1=RV[:, v, t], op0=ALU.mult, op1=ALU.add)
                            elif stage == 3:
                                op = dve.tensor_tensor(UP[:, v, :], DL[:, v].unsqueeze(2)
                                                       .to_broadcast([P, DH // 2, DH]), k, ALU.mult)
                            else:
                                op = dve.scalar_tensor_tensor(now, in0=before, scalar=EG[:, t:t + 1],
                                                              in1=UP[:, v, :], op0=ALU.mult, op1=ALU.add)
                            if stage == 4 and half == 1 and t % 8 == 7:
                                op.then_inc(hist_ready.sem, 1)
                            else:
                                turn[half] = steps.mark(op)

            def output_gated(j):
                dve.wait_ge(og_loaded.sem, og_loaded.at(j, 3))
                for h in range(KC):
                    dve.scalar_tensor_tensor(XM[:, 0, h, :], in0=KV[:, h, :], scalar=gnorm[:, :], in1=XM[:, 1, h, :],
                                             op0=ALU.mult, op1=ALU.mult).then_inc(og_ready.sem, 1)

            def output_added(j):
                dve.wait_ge(attn1_ready.sem, attn1_ready.at(j, 1))
                for s in range(2):
                    last = dve.tensor_tensor(X[:, j, 2 * s:2 * s + 2, :], X[:, j, 2 * s:2 * s + 2, :],
                                             PS[:, 2 + s, :].rearrange("p (i n) -> p i n", i=2), ALU.add)
                last.then_inc(attn1_added.sem, 1)
                dve.wait_ge(attn1_added.sem, attn1_added.at(j, 1))
                for i in range(NT):
                    last = dve.bn_stats(stats[:, i, :], X[:, j, i, :])
                steps.link(last)
                for i in range(NT):
                    last = dve.bn_aggr(mv[:, i, :], stats[:, i, :])
                last.then_inc(xstats_ready.sem, 1)

            def input_normal(j):
                dve.wait_ge(xstd_ready.sem, xstd_ready.at(j, 1))
                steps.link(dve.reciprocal(rs[:, :], sd[:, :]))
                steps.mark(dve.tensor_tensor(MSQ[:, j, :], mv[:, :, 1], rs[:, :], ALU.mult))
                dve.wait_ge(xi_saved.sem, xi_saved.at(j, 1))
                for i in range(NT):
                    last = dve.tensor_scalar(X[:, j, i, :], X[:, j, i, :], mv[:, i, 0:1], rs[:, i:i + 1],
                                             ALU.subtract, ALU.mult)
                steps.link(last)
                steps.link(dve.tensor_tensor(MSQ[:, j, :], MSQ[:, j, :], rs[:, :], ALU.mult))

            def body(j, rec, blk):
                def early():
                    dve.wait_ge(rec_ready.sem, rec_ready.at(j - 1, 1))
                    recur(j, 0, 4)
                if blk:
                    ln(j, 0)
                    dve.wait_ge(xT_ready.sem, xT_ready.at(j, 2))
                    steps.link(dve.tensor_tensor(DF, XN[:, :, :, 1:TB + 1], XN[:, :, :, 0:TB], ALU.subtract))
                    dve.wait_ge(stored.sem, stored.at(j, 0))
                    for m in range(3):
                        for h in range(KC):
                            last = dve.scalar_tensor_tensor(
                                XM[:, m, h, :].rearrange("p (b t) -> p b t", b=B), in0=DF[:, h, :, :],
                                scalar=vec0[:, m, h:h + 1], in1=XN[:, h, :, 0:TB], op0=ALU.mult, op1=ALU.add)
                            if h == 0:
                                steps.mark(last)
                        if m < 2:
                            last.then_inc(mixed.sem, 1)
                        else:
                            steps.link(last)
                    dve.tensor_copy(XN[:, :, :, 0:1], XN[:, :, :, TB:TB + 1]).then_inc(mixed.sem, 1)
                    dve.wait_ge(k_kept.sem, k_kept.at(j, 2))
                    dve.wait_ge(proj_ready.sem, proj_ready.at(j, 2))
                    for h in range(KC):
                        steps.mark(dve.tensor_tensor(KV[:, h, :], DFf[:, h, :], PS[:, 4 + h, :], ALU.mult))
                    steps.after(steps.n)
                    for h in range(KC):
                        for b in range(B):
                            steps.mark(dve.tensor_tensor_scan(
                                ST[:, h, b * TB:(b + 1) * TB], data0=vec0[:, 3, h:h + 1].to_broadcast([P, TB]),
                                data1=KV[:, h, b * TB:(b + 1) * TB], initial=ST[:, h, (b + 1) * TB - 1:(b + 1) * TB],
                                op0=ALU.mult, op1=ALU.add))
                    steps.after(steps.n)
                    for h in range(KC):
                        steps.mark(dve.scalar_tensor_tensor(KV[:, h, :], in0=KV[:, h, :], scalar=vec0[:, 4, h:h + 1],
                                                            in1=ST[:, h, :], op0=ALU.mult, op1=ALU.add))
                    steps.after(steps.n)
                if rec:
                    for m in range(2):
                        dve.wait_ge(rstd_ready.sem, rstd_ready.at(j - 1, m + 1))
                        dve.reciprocal(RN[:, m, :], RN[:, m, :]).then_inc(rnorm_ready.sem, 1)
                if blk:
                    dve.wait_ge(proj_ready.sem, proj_ready.at(j, 3))
                    steps.mark(dve.tensor_tensor(KV[:, 0, :], KV[:, 0, :], PS[:, 6, :], ALU.mult))
                    dve.tensor_tensor(KV[:, 1, :], KV[:, 1, :], PS[:, 7, :], ALU.mult).then_inc(o_ready.sem, 1)
                    dve.wait_ge(mu_ready.sem, mu_ready.at(j, 1))
                    for h in range(KC):
                        dve.tensor_tensor(XM[:, 1, h, :], KV[:, h, :], PS[:, 0, :], ALU.subtract)\
                            .then_inc(centred.sem, 1)
                    dve.wait_ge(ostd_ready.sem, ostd_ready.at(j, 1))
                    steps.link(dve.reciprocal(DFf[:, 1, :], DFf[:, 0, :]))
                    for h in range(KC):
                        dve.scalar_tensor_tensor(XM[:, 0, h, :], in0=XM[:, 1, h, :], scalar=vec0[:, 5, h:h + 1],
                                                 in1=DFf[:, 1, :], op0=ALU.mult, op1=ALU.mult)\
                            .then_inc(y_scaled.sem, 1)
                    if rec:
                        early()
                    dve.wait_ge(attn0_ready.sem, attn0_ready.at(j, 1))
                    steps.mark(dve.tensor_tensor(X[:, j, 0:2, :], X[:, j, 0:2, :],
                                                 PS[:, 2, :].rearrange("p (i n) -> p i n", i=2), ALU.add))
                    dve.tensor_tensor(X[:, j, 2:4, :], X[:, j, 2:4, :],
                                      PS[:, 3, :].rearrange("p (i n) -> p i n", i=2), ALU.add)\
                        .then_inc(attn0_added.sem, 1)
                    dve.wait_ge(attn0_added.sem, attn0_added.at(j, 1))
                    ln(j, 1)
                    if rec:
                        recur(j, 4, 4)
                    dve.wait_ge(logits_kept.sem, logits_kept.at(j, 1))
                    apart(dve)
                    for i in range(NT):
                        steps.mark(dve.max(MX[:, i, :], LG[:, i, :]))
                    steps.after(steps.n)
                    for i in range(NT):
                        steps.mark(dve.max_index(MI[:, i, :], MX[:, i, :], LG[:, i, :]))
                    steps.mark(dve.tensor_scalar(NM[:, :], MX[:, :, 0], -1.0, None, ALU.mult))
                    dve.tensor_tensor(E2[:, :], MX[:, :, 1], MX[:, :, 0], ALU.subtract).then_inc(max_ready.sem, 1)
                    steps.after(steps.n)
                    steps.mark(dve.tensor_copy(MF[:, :, :], MI[:, :, :]))
                    dve.wait_ge(exps_ready.sem, exps_ready.at(j, 1))
                    steps.link(dve.reciprocal(W12[:, :, 0], ZS[:, :]))
                    steps.link(dve.tensor_tensor(W12[:, :, 1], E2[:, :], W12[:, :, 0], ALU.mult))
                    for i in range(NT):
                        steps.mark(dve.tensor_scalar(CW[:, i, :], iota[:, :], MF[:, i, 0:1], W12[:, i, 0:1],
                                                     ALU.is_equal, ALU.mult))
                        steps.mark(dve.tensor_scalar(CT[:, i, :], iota[:, :], MF[:, i, 1:2], W12[:, i, 1:2],
                                                     ALU.is_equal, ALU.mult))
                    steps.after(steps.n)
                    dve.tensor_tensor(CW[:, :, :], CW[:, :, :], CT[:, :, :], ALU.add).then_inc(cw_ready.sem, 1)
                if rec and not blk:
                    early()
                    recur(j, 4, 4)
                for n in range(NU):
                    if blk:
                        dve.wait_ge(silu_ready.sem, silu_ready.at(j, n + 1))
                        if n >= 4:
                            dve.wait_ge(z_ready.sem, z_ready.at(j, n - 3))
                        elif n == 3:
                            dve.wait_ge(z_ready.sem, z_ready.at(j, 1))
                        dve.tensor_tensor(Hh[:, n % 3, :], SG[:, n % 2, :], PS[:, 2 * (n % 2), :], ALU.mult)\
                            .then_inc(h_ready.sem, 1)
                    other = n // 2 if not blk and n // 2 < NBLK - 1 else None
                    if other is not None and n % 2 == 0:
                        output_gated(other)
                    if rec and 1 <= n <= 15:
                        recur(j, 3 * n + 5, 3 if n < 15 else 2)
                    if other is not None:
                        (output_added, input_normal)[n % 2](other)
                if rec:
                    recur(j, TB - 12, 4)
                if blk:
                    dve.wait_ge(z_added.sem, z_added.at(j, NJ))
                    ln(j, 2)
                if rec:
                    recur(j, TB - 8, 8)
                if blk:
                    dve.wait_ge(gates_kept.sem, gates_kept.at(j, 1))
                    steps.mark(dve.tensor_scalar(GB[32:48, :], GT1[32:48, :], 0.5, 0.5, ALU.mult, ALU.add))
                    steps.link(dve.tensor_scalar(GB[0:HEADS, :], PS[0:HEADS, 6, :], gpar[0:HEADS, 0:1], 0.0,
                                                 ALU.add, ALU.max))
                    dve.sem_inc(gates_kept.sem, 1)
                    dve.sem_inc(beta_ready.sem, 1)
                    dve.wait_ge(softplus_ready.sem, softplus_ready.at(j, 1))
                    dve.tensor_tensor(GT1[0:HEADS, :], GT1[0:HEADS, :], GB[0:HEADS, :], ALU.add)\
                        .then_inc(relu_ready.sem, 1)
                for m in range(3):
                    if rec and m == 2:
                        dve.wait_ge(rstd_ready.sem, rstd_ready.at(j - 1, 3))
                        dve.reciprocal(RN[:, 2, :], RN[:, 2, :]).then_inc(rnorm_ready.sem, 1)
                    if blk:
                        dve.wait_ge(pre_kept.sem, pre_kept.at(j, 2 * m + 2))
                        done = [0, 0]
                        for tap in range(TAPS):
                            for h in range(KC):
                                y = CV[:, m, h, :].rearrange("p (b t) -> p b t", b=B)
                                x, w = PRE[:, m, h, :, tap:tap + TB], taps[:, m, h, tap:tap + 1]
                                if tap == 0:
                                    done[h] = steps.mark(dve.tensor_scalar(y, x, w, None, ALU.mult))
                                    continue
                                steps.after(done[h])
                                last = dve.scalar_tensor_tensor(y, in0=x, scalar=w, in1=y, op0=ALU.mult, op1=ALU.add)
                                if tap < TAPS - 1:
                                    done[h] = steps.mark(last)
                                elif m < 2 or h == 0:
                                    last.then_inc(conv_ready.sem, 1)
                                else:
                                    steps.link(last)
                        if m == 2:
                            dve.tensor_copy(
                                PRE[:, :, :, :, 0:TAPS - 1].rearrange("p m h b t -> p (m h b) t"),
                                PRE[:, :, :, :, TB:PADT].rearrange("p m h b t -> p (m h b) t"))\
                                .then_inc(conv_ready.sem, 1)
                steps.reset()
            passes(dve, body)
            output_gated(NBLK - 1)
            output_added(NBLK - 1)
            input_normal(NBLK - 1)
            steps.reset()
            dve.sem_inc(blocks_done, 1)
            dve.wait_ge(sstd_ready, 1)
            steps.link(dve.reciprocal(MSQ[:, :, :], MSQ[:, :, :]))
            steps.reset()

            def tokens(i):
                dve.wait_ge(pturn_ready.sem, pturn_ready.at(i, 0))
                apart(dve)
                for j in range(NBLK):
                    last = dve.tensor_scalar(xnp[:, j, :], X[:, j, bass.ds(i, 1), :].rearrange("p i n -> p (i n)"),
                                             MSQ[:, j, bass.ds(i, 1)], None, ALU.mult)
                last.then_inc(pn_ready.sem, 1)

            def remainders(i, n0, n1):
                for n in range(n0, n1):
                    m, h = (n // 2) % 2, n % 2
                    dve.wait_ge(hi_ready.sem, hi_ready.at(i, n + 1))
                    dve.wait_ge(lo_ready.sem, lo_ready.at(i, n - 3))
                    dve.tensor_tensor(R1[:, m, h, :], PS[:, 2 * m + h, :], SP3[:, m, 0, h, :], ALU.subtract)\
                        .then_inc(r1_ready.sem, 1)
            tokens(0)
            with dve.Fori(0, NPAIR - 1) as i:
                remainders(i, 0, 4)
                tokens(i + 1)
                remainders(i, 4, 8)
            remainders(NPAIR - 1, 0, 8)

            def maxima(i, n, s0=0, s1=16):
                dve.wait_ge(mt_ready.sem, mt_ready.at(i, n - 1))
                for s in range(s0, s1):
                    dve.wait_ge(ms_ready.sem, ms_ready.at(i, 16 * n + s + 1))
                    dve.tensor_reduce(MXS[n % 2][:, s:s + 1], PS[:, s % 2, :], AX.X, ALU.max)\
                        .then_inc(ms_used.sem, 1)

            def context(i, n):
                dve.wait_ge(vtt_ready.sem, vtt_ready.at(i, n + 1))
                v = PS[:, 2, :].rearrange("p (q n) -> p q n", n=32)
                steps.link(dve.reciprocal(RC.unsqueeze(2), v[:, :, DH:DH + 1]))
                g = 64 * (n % 4)
                for qt in range(KT):
                    last = dve.tensor_tensor(CTX[:, qt, g:g + 64].rearrange("p (h d) -> p h d", h=4),
                                             v[:, 4 * qt:4 * qt + 4, 0:DH],
                                             RC[:, 4 * qt:4 * qt + 4].unsqueeze(2).to_broadcast([P, 4, DH]), ALU.mult)
                last.then_inc(ctx_ready.sem, 1)

            def groups(i, last):
                for n in range(NG):
                    nxt = (i, n + 1) if n + 1 < NG else None if last else (i + 1, 0)
                    if nxt:
                        maxima(*nxt, 0, 11)
                    if n:
                        dve.wait_ge(ctx_ready.sem, ctx_ready.at(i, n - 1))
                        context(i, n - 1)
                    if nxt:
                        maxima(*nxt, 11, 16)
                dve.wait_ge(ctx_ready.sem, ctx_ready.at(i, NG - 1))
                context(i, NG - 1)
                for jj in range(NBLK // 2):
                    dve.wait_ge(op_ready.sem, op_ready.at(i, jj + 1))
                    x = X[:, 2 * jj:2 * jj + 2, bass.ds(i, 1), :].rearrange("p j i n -> p (j i) n") \
                        if not last else X[:, 2 * jj:2 * jj + 2, i, :]
                    dve.tensor_tensor(x, x, PS[:, 3 + jj, :].rearrange("p (j n) -> p j n", j=2), ALU.add)\
                        .then_inc(op_added.sem, 1)
                steps.reset()
            maxima(0, 0)
            with dve.Fori(0, NPAIR - 1) as i:
                groups(i, False)
            groups(NPAIR - 1, True)
            dve.wait_ge(op_added.sem, op_added.at(NPAIR, 0))
            dve.wait_ge(rstd2_ready, 1)
            steps.link(dve.reciprocal(SD2, SD2))
            steps.reset()
            with dve.Fori(0, NBLK) as j:
                dve.wait_ge(h2_turned.sem, h2_turned.at(j, 0))
                dve.wait_ge(h2_kept.sem, h2_kept.at(j, 0))
                apart(dve)
                for i in range(NT):
                    last = dve.scalar_tensor_tensor(XN2[:, i, :], in0=X[:, j, i, :],
                                                    scalar=SD2[:, bass.ds(j * NT + i, 1)], in1=n2b,
                                                    op0=ALU.mult, op1=ALU.mult)
                last.then_inc(h2_ready.sem, 1)
                steps.reset()
            dve.wait_ge(lg_kept.sem, lg_kept.at(NBLK, 0))
            for g in range(NTOK):
                last = dve.max(MX2[:, g, :], LGT[:, g, :])
            steps.link(last)
            for g in range(NTOK):
                last = dve.max_index(MI2[:, g, :], MX2[:, g, :], LGT[:, g, :])
            steps.mark(last)
            dve.tensor_tensor(EX2, LGT, MX2[:, :, 0:1].to_broadcast([P, NTOK, E1]), ALU.subtract)
            dve.tensor_tensor(WW[:, 1, :], MX2[:, :, 1], MX2[:, :, 0], ALU.subtract).then_inc(route_in, 1)
            steps.after(steps.n)
            steps.link(dve.tensor_copy(MF2, MI2))
            for m in range(2):
                last = dve.tensor_tensor(OH[:, m, :, :], MF2[:, :, m:m + 1].to_broadcast([P, NTOK, E1]),
                                         iota[:, 0:E1].unsqueeze(1).to_broadcast([P, NTOK, E1]), ALU.is_equal)
            steps.link(last)
            dve.tensor_tensor(MM, OH[:, 0, :, :], OH[:, 1, :, :], ALU.add).then_inc(masks_ready, 1)
            dve.wait_ge(route_exp, 1)
            steps.link(dve.tensor_reduce(ZZ, EX2, AX.X, ALU.add))
            steps.link(dve.reciprocal(ZZ, ZZ))
            steps.link(dve.tensor_tensor(WW[:, 1, :], WW[:, 1, :], ZZ, ALU.mult))
            dve.tensor_tensor(WW[:, 1, :], WW[:, 1, :], ZZ, ALU.subtract).then_inc(route_in, 1)
            dve.wait_ge(route_exp, 2)
            steps.link(dve.tensor_scalar(WW[:, 0, :], WW[:, 1, :], 1.0, None, ALU.add))
            steps.link(dve.reciprocal(WW[:, 0, :], WW[:, 0, :]))
            steps.link(dve.tensor_tensor(WW[:, 1, :], WW[:, 1, :], WW[:, 0, :], ALU.mult))
            dve.wait_ge(ranks_ready, 1)
            dve.wait_ge(d_iota, 3)
            for e in range(E1):
                last = dve.tensor_tensor_scan(CNT[:, :, e], data0=ONE[:, 0:NTOK],
                                              data1=PS[:, 1, 0:NTOK * E1].rearrange("p (g e) -> p g e", e=E1)[:, :, e],
                                              initial=0.0, op0=ALU.mult, op1=ALU.add)
            steps.link(last)
            steps.mark(dve.tensor_tensor(PO, CNT, PS[:, 1, 0:NTOK * E1].rearrange("p (g e) -> p g e", e=E1),
                                          ALU.subtract))
            steps.link(dve.tensor_tensor(CM2, CNT[:, NTOK - 1, :].unsqueeze(2).to_broadcast([P, E1, NTOK]),
                                          IOG.unsqueeze(1).to_broadcast([P, E1, NTOK]), ALU.is_gt))
            steps.link(dve.tensor_reduce(TE, CM2, AX.X, ALU.add))
            steps.link(dve.tensor_tensor_scan(ENDS, data0=ONE[:, 0:E1], data1=TE, initial=0.0,
                                               op0=ALU.mult, op1=ALU.add))
            steps.mark(dve.tensor_tensor(OFF, ENDS, TE, ALU.subtract))
            steps.link(dve.tensor_tensor(CMP, ENDS.unsqueeze(1).to_broadcast([P, NTILE, E1]),
                                          IOT.unsqueeze(2).to_broadcast([P, NTILE, E1]), ALU.is_le))
            steps.mark(dve.tensor_reduce(TEF, CMP, AX.X, ALU.add))
            steps.link(dve.tensor_scalar(OFF, OFF, float(P), None, ALU.mult))
            steps.mark(dve.tensor_scalar(TEF, TEF, float(E1 - 1), None, ALU.min))
            steps.link(dve.tensor_tensor(PO, PO, OFF.unsqueeze(1).to_broadcast([P, NTOK, E1]), ALU.add))
            steps.mark(dve.tensor_copy(TEI, TEF))
            steps.link(dve.tensor_tensor(PO, PO, PS[:, 0, 0:NTOK * E1].rearrange("p (g e) -> p g e", e=E1), ALU.add))
            for m in range(2):
                last = dve.tensor_tensor(SEL[:, m, :, :], OH[:, m, :, :], PO, ALU.mult)
            steps.link(last)
            for m in range(2):
                last = dve.tensor_reduce(PF[:, m, :], SEL[:, m, :, :], AX.X, ALU.add)
            steps.link(last)
            steps.link(dve.tensor_copy(PI, PF))
            dve.sem_inc(pos_ready, 1)
            steps.reset()
            with dve.Fori(0, NBLK) as j:
                for n in range(FT):
                    dve.wait_ge(ss_silu.sem, ss_silu.at(j, n + 1))
                    dve.wait_ge(sz_ready.sem, sz_ready.at(j, 0))
                    dve.tensor_tensor(HS[:, n, :], SG2[:, n % 2, :], PS[:, 2 * (n % 2) + 1, :], ALU.mult)\
                        .then_inc(sh_ready.sem, 1)
                dve.wait_ge(sz_ready.sem, sz_ready.at(j, 1))
                for s in range(2):
                    x = X[:, bass.ds(j, 1), 2 * s:2 * s + 2, :].rearrange("p j i n -> p (j i) n")
                    last = dve.tensor_tensor(x, x, PS[:, 4 + s, :].rearrange("p (i n) -> p i n", i=2), ALU.add)
                last.then_inc(sz_added.sem, 1)
            dve.wait_ge(sz_added.sem, sz_added.at(NBLK, 0))
            def hidden(q):
                for u in range(2):
                    dve.wait_ge(gsilu_ready.sem, gsilu_ready.at(q, u + 1))
                    dve.wait_ge(up_ready.sem, up_ready.at(q, u + 1))
                    dve.wait_ge(hk_turned.sem, hk_turned.at(q, u - 1))
                    dve.tensor_tensor(HTK[u], SGT[u], PS[:, 3 + 2 * u, :], ALU.mult).then_inc(hk_ready.sem, 1)
            first = NTILE // 2 - NBLK
            with dve.Fori(0, first) as q:
                hidden(q)
            dve.wait_ge(xi_loaded, 16)
            with dve.Fori(0, NBLK) as j:
                hidden(j + first)
                x = X[:, bass.ds(j, 1), :, :].rearrange("p j i n -> p (j i) n")
                steps.link(dve.tensor_tensor(x, x, XI[:, bass.ds(j, 1), :, :].rearrange("p j i n -> p (j i) n"),
                                             ALU.add))
                steps.reset()
            for g in range(NTOK):
                x = X[:, g // NT, g % NT, :]
                for m in range(2):
                    n = 2 * g + m
                    dve.wait_ge(yg_loaded[n % 4], 16 * (n // 4 + 1))
                    if m:
                        dve.wait_ge(yg_used, n)
                    dve.scalar_tensor_tensor(x, in0=YG[n % 4], scalar=WW[:, m, g:g + 1], in1=x,
                                             op0=ALU.mult, op1=ALU.add).then_inc(yg_used, 1)
                if g % NT == NT - 1:
                    dve.wait_ge(yg_used, 2 * g + 2)
                    dve.sem_inc(x_final, 1)
            steps.reset()


def kernel(**inputs):
    import numpy as _np
    import concourse.bacc as _bacc
    from concourse import mybir as _mybir
    from concourse.bass_utils import run_bass_kernel_spmd as _run

    nc = _bacc.Bacc("TRN2", target_bir_lowering=False, num_devices=1)
    arrays, aps = {}, {}
    for name, value in inputs.items():
        v = _np.ascontiguousarray(value)
        arrays[name] = v
        aps[name] = nc.dram_tensor(name, v.shape, _mybir.dt.from_np(v.dtype), kind="ExternalInput").ap()
    arrays["rope"] = rope_table()
    aps["rope"] = nc.dram_tensor("rope", arrays["rope"].shape, F32, kind="ExternalInput").ap()
    scratch = {
        "qkv": nc.dram_tensor("qkv", (NBLK, 3, B, C, TB), F32, kind="Internal").ap(),
        "gb": nc.dram_tensor("gb", (NBLK, 2, B, HEADS, TB), F32, kind="Internal").ap(),
        "gate": nc.dram_tensor("gate", (NBLK, P, KC * COLS), F32, kind="Internal").ap(),
        "stack": nc.dram_tensor("stack", (2, B // 2, 2, HEADS // 4, 3, 4 * DH, T), BF16, kind="Internal").ap(),
        "xi": nc.dram_tensor("xi", (NBLK, P, NT * C), F32, kind="Internal").ap(),
        "xs": nc.dram_tensor("xs", (2 * B * T // P + E1, P, C), F32, kind="Internal").ap(),
        "ys": nc.dram_tensor("ys", (2 * B * T // P + E1, P, C), F32, kind="Internal").ap(),
        "v": nc.dram_tensor("v", (B // 2, 2, P, T // P * HEADS * 2 * DH), F32, kind="Internal").ap(),
        "o": nc.dram_tensor("o", (NBLK, B, HEADS, DH, TB), F32, kind="Internal").ap(),
    }
    res = nc.dram_tensor("result", (B, T, C), F32, kind="ExternalOutput").ap()
    two_layers(nc, aps, res, scratch)
    r = _run(nc, [arrays], core_ids=[0])
    return r.results[0]["result"]
```
